# Optimizing a Trainium2 kernel written in Bass

```python
import numpy as np
import jax
import jax.numpy as jnp

def _softmax(x, axis=-1):
    return jax.nn.softmax(x, axis=axis)

def _gelu(x):
    return jax.nn.gelu(x, approximate=True)

def _silu(x):
    return jax.nn.silu(x)

def _sigmoid(x):
    return jax.nn.sigmoid(x)

def _layernorm(x, axis=-1, eps=1e-05):
    m = jnp.mean(x, axis=axis, keepdims=True)
    v = jnp.var(x, axis=axis, keepdims=True)
    return (x - m) / jnp.sqrt(v + eps)

def _scatter_add(tgt, idx, src, axis=0):
    return tgt.at[idx].add(src)

def _segment_sum(src, seg, n):
    return jax.ops.segment_sum(src, seg, n)
kernel_name = 'mk_seq_postln_d1_jaxref_r8_4d5402'

def setup_inputs(seed: int=0):
    np.random.seed(seed)
    _w = jnp.asarray

    def _L0_attn_setup():
        import jax, jax.numpy as jnp
        import numpy as np
        import math
        D_MODEL = 128
        D_STATE = 128
        D_CONV = 4
        EXPAND = 2
        HEADDIM = 64
        NGROUPS = 1
        D_INNER = EXPAND * D_MODEL
        NHEADS = D_INNER // HEADDIM
        CONV_DIM = D_INNER + 2 * NGROUPS * D_STATE
        D_IN_PROJ = 2 * D_INNER + 2 * NGROUPS * D_STATE + NHEADS
        EPS = 1e-05
        BATCH, SEQLEN = (2, 128)
        DT_MIN, DT_MAX, DT_FLOOR = (0.001, 0.1, 0.0001)
        key = jax.random.key(seed)
        ks = jax.random.split(key, 8)
        x = jax.random.normal(ks[0], (BATCH, SEQLEN, D_MODEL), jnp.float32)
        Win = jax.random.normal(ks[1], (D_IN_PROJ, D_MODEL), jnp.float32) / math.sqrt(D_MODEL)
        conv_w = jax.random.normal(ks[2], (CONV_DIM, D_CONV), jnp.float32) / math.sqrt(D_CONV)
        conv_b = jnp.zeros((CONV_DIM,), jnp.float32)
        dt = jnp.exp(jax.random.uniform(ks[3], (NHEADS,)) * (math.log(DT_MAX) - math.log(DT_MIN)) + math.log(DT_MIN))
        dt = jnp.clip(dt, DT_FLOOR)
        dt_bias = dt + jnp.log(-jnp.expm1(-dt))
        A_log = jnp.log(jax.random.uniform(ks[4], (NHEADS,), minval=1.0, maxval=16.0))
        D = jnp.ones((NHEADS,), jnp.float32)
        norm_w = jnp.ones((D_INNER,), jnp.float32)
        Wout = jax.random.normal(ks[5], (D_MODEL, D_INNER), jnp.float32) / math.sqrt(D_INNER)
        return dict(x=x, Win=Win, conv_w=conv_w, conv_b=conv_b, dt_bias=dt_bias, A_log=A_log, D=D, norm_w=norm_w, Wout=Wout)
    _L0_attn_in = _L0_attn_setup()

    def _L0_ffn_setup():
        import jax, jax.numpy as jnp
        import numpy as np
        E = 8
        TOP_K = 2
        D = 128
        DFF = 4 * D
        key = jax.random.key(seed)
        ks = jax.random.split(key, 6)
        b, s = (4, 128)
        x = jax.random.normal(ks[0], (b, s, D), dtype=jnp.float32)
        centroids = jax.random.normal(ks[1], (E, D), dtype=jnp.float32)
        W1 = jax.random.normal(ks[2], (E, D, DFF), dtype=jnp.float32) * (1.0 / np.sqrt(D))
        b1 = jax.random.normal(ks[3], (E, DFF), dtype=jnp.float32) * 0.01
        W2 = jax.random.normal(ks[4], (E, DFF, D), dtype=jnp.float32) * (1.0 / np.sqrt(DFF))
        b2 = jax.random.normal(ks[5], (E, D), dtype=jnp.float32) * 0.01
        return {'x': x, 'centroids': centroids, 'W1': W1, 'b1': b1, 'W2': W2, 'b2': b2}
    _L0_ffn_in = _L0_ffn_setup()
    _d = {'L0_attn_x': _L0_attn_in['x'], 'L0_attn_Win': _L0_attn_in['Win'], 'L0_attn_conv_w': _L0_attn_in['conv_w'], 'L0_attn_conv_b': _L0_attn_in['conv_b'], 'L0_attn_dt_bias': _L0_attn_in['dt_bias'], 'L0_attn_A_log': _L0_attn_in['A_log'], 'L0_attn_D': _L0_attn_in['D'], 'L0_attn_norm_w': _L0_attn_in['norm_w'], 'L0_attn_Wout': _L0_attn_in['Wout'], 'L0_ffn_centroids': _L0_ffn_in['centroids'], 'L0_ffn_W1': _L0_ffn_in['W1'], 'L0_ffn_b1': _L0_ffn_in['b1'], 'L0_ffn_W2': _L0_ffn_in['W2'], 'L0_ffn_b2': _L0_ffn_in['b2']}
    _x0 = _d['L0_attn_x']
    _d['L0_attn_x'] = jax.random.normal(jax.random.fold_in(jax.random.key(seed), 1), (16, 512, 128), dtype=_x0.dtype)
    del _x0
    return _d

def reference(L0_attn_x, L0_attn_Win, L0_attn_conv_w, L0_attn_conv_b, L0_attn_dt_bias, L0_attn_A_log, L0_attn_D, L0_attn_norm_w, L0_attn_Wout, L0_ffn_centroids, L0_ffn_W1, L0_ffn_b1, L0_ffn_W2, L0_ffn_b2):

    def _L0_attn_ref(x, Win, conv_w, conv_b, dt_bias, A_log, D, norm_w, Wout):
        import jax, jax.numpy as jnp
        import numpy as np
        import math
        D_MODEL = 128
        D_STATE = 128
        D_CONV = 4
        EXPAND = 2
        HEADDIM = 64
        NGROUPS = 1
        D_INNER = EXPAND * D_MODEL
        NHEADS = D_INNER // HEADDIM
        CONV_DIM = D_INNER + 2 * NGROUPS * D_STATE
        D_IN_PROJ = 2 * D_INNER + 2 * NGROUPS * D_STATE + NHEADS
        EPS = 1e-05
        BATCH, SEQLEN = (2, 128)
        DT_MIN, DT_MAX, DT_FLOOR = (0.001, 0.1, 0.0001)
        b, l, _ = x.shape
        zxbcdt = x @ Win.T
        z = zxbcdt[..., :D_INNER]
        xBC = zxbcdt[..., D_INNER:D_INNER + CONV_DIM]
        dt = zxbcdt[..., D_INNER + CONV_DIM:]
        xBC = jnp.transpose(xBC, (0, 2, 1))
        xBC = jax.lax.conv_general_dilated(xBC, conv_w[:, None, :], window_strides=(1,), padding=[(D_CONV - 1, 0)], feature_group_count=CONV_DIM, dimension_numbers=('NCH', 'OIH', 'NCH'))
        xBC = xBC + conv_b[None, :, None]
        xBC = jnp.transpose(xBC, (0, 2, 1))
        xBC = jax.nn.silu(xBC)
        x_ssm = xBC[..., :D_INNER].reshape(b, l, NHEADS, HEADDIM)
        Bm = xBC[..., D_INNER:D_INNER + D_STATE]
        Cm = xBC[..., D_INNER + D_STATE:]
        A = -jnp.exp(A_log)
        dtp = jax.nn.softplus(dt + dt_bias)
        dA = jnp.exp(dtp * A)

        def step(h, inp):
            dA_t, dt_t, x_t, B_t, C_t = inp
            dBx = (dt_t[:, :, None] * x_t)[..., None] * B_t[:, None, None, :]
            h = dA_t[:, :, None, None] * h + dBx
            y = jnp.einsum('bn,bhpn->bhp', C_t, h) + D[None, :, None] * x_t
            return (h, y)
        h0 = jnp.zeros((b, NHEADS, HEADDIM, D_STATE), x.dtype)
        xs = (jnp.moveaxis(dA, 1, 0), jnp.moveaxis(dtp, 1, 0), jnp.moveaxis(x_ssm, 1, 0), jnp.moveaxis(Bm, 1, 0), jnp.moveaxis(Cm, 1, 0))
        _, ys = jax.lax.scan(step, h0, xs)
        y = jnp.moveaxis(ys, 0, 1).reshape(b, l, D_INNER)
        yn = y * jax.lax.rsqrt(jnp.mean(y * y, axis=-1, keepdims=True) + EPS) * norm_w
        y = yn * jax.nn.silu(z)
        return y @ Wout.T

    def _L0_ffn_ref(x, centroids, W1, b1, W2, b2):
        import jax, jax.numpy as jnp
        import numpy as np
        E = 8
        TOP_K = 2
        D = 128
        DFF = 4 * D
        b, s, d = x.shape
        u = x.reshape(b * s, d)
        n = u.shape[0]
        gates = jax.nn.sigmoid(u @ centroids.T)
        if TOP_K < E:
            topk_vals, topk_idx = jax.lax.top_k(gates, TOP_K)
            mask = jnp.zeros_like(gates).at[jnp.arange(n)[:, None], topk_idx].set(topk_vals)
            gates = mask / jnp.sum(mask, axis=-1, keepdims=True)
        h = jax.nn.gelu(jnp.einsum('nd,edf->enf', u, W1) + b1[:, None, :], approximate=False)
        outs = jnp.einsum('enf,efd->end', h, W2) + b2[:, None, :]
        out = jnp.einsum('ne,end->nd', gates, outs)
        return out.reshape(b, s, d)
    x = L0_attn_x
    x = _layernorm(x + _L0_attn_ref(x, L0_attn_Win, L0_attn_conv_w, L0_attn_conv_b, L0_attn_dt_bias, L0_attn_A_log, L0_attn_D, L0_attn_norm_w, L0_attn_Wout), axis=-1)
    x = _layernorm(x + _L0_ffn_ref(x, L0_ffn_centroids, L0_ffn_W1, L0_ffn_b1, L0_ffn_W2, L0_ffn_b2), axis=-1)
    return x

_drawn_inputs = setup_inputs


def setup_inputs(seed=0):
    import zlib

    import numpy as np

    out = dict(_drawn_inputs(seed))
    spreads = {'L0_attn_conv_b': (0.0, 0.1), 'L0_attn_D': (1.0, 0.2), 'L0_attn_norm_w': (1.0, 0.2)}
    factors = {'L0_ffn_b1': 8.0, 'L0_ffn_b2': 8.0}
    for name, (base, spread) in spreads.items():
        noise = np.random.default_rng([zlib.crc32(name.encode()), seed]).standard_normal(out[name].shape)
        drawn = base * np.exp(spread * noise) if base else spread * noise
        out[name] = jnp.asarray(drawn.astype(out[name].dtype))
    for name, factor in factors.items():
        out[name] = (out[name] * factor).astype(out[name].dtype)
    return out
```

```python
from contextlib import ExitStack

import concourse.bass as bass
from concourse import mybir
from concourse.alu_op_type import AluOpType as ALU

F32 = mybir.dt.float32
BF16 = mybir.dt.bfloat16
I32 = mybir.dt.int32
U32 = mybir.dt.uint32
ACT = mybir.ActivationFunctionType
AX_X = mybir.AxisListType.X

P = 128
SEQS, TOKS = 16, 512
NC = TOKS // P
H, HD = 4, 64
DI = H * HD
CC = DI // P
XC = CC + 2
TAPS = 4
E, FF = 8, 512
FB = FF // P
EPS = 1e-5
PADN = 96
TOKENS = SEQS * TOKS
ROW = P + 2
REGION = TOKENS + P
TILES = 2 * TOKENS // P + E
SPARE = E * REGION
LOG_TERMS = (13, 11, 9, 7, 5, 3)
SP_STEPS = 13
LN_STEPS = 2
GATE_STEPS = 6
POS_STEPS = 4
FIN_STEPS = 4


class Seq:

    def __init__(self, half, off):
        self.half, self.off = half, off
        self.n = 2 * half + off
        self.par = off % 2
        self.use = half + off // 2

    def plus(self, d):
        return Seq(self.half, self.off + d)


def wait(eng, sem, value):
    if not isinstance(value, int) or value > 0:
        eng.wait_ge(sem, value)


def build(nc, t, out):
    ctx = ExitStack()
    with ctx:
        def sb(name, shape, dt=F32):
            return ctx.enter_context(nc.sbuf_tensor(name, shape, dt))

        def bank(name):
            return ctx.enter_context(nc.psum_tensor(name, [P, 512], F32))

        def sem(name):
            return ctx.enter_context(nc.semaphore(name))

        sorted_rows = nc.dram_tensor("sorted_rows", [SPARE + E * P, ROW], F32, kind="Internal").ap()
        moe_rows = nc.dram_tensor("moe_rows", [2 * TOKENS, P], F32, kind="Internal").ap()

        w_z = sb("w_z", [P, DI])
        w_xbc = sb("w_xbc", [P, XC * P])
        w_dt = sb("w_dt", [P, PADN])
        w_gate = sb("w_gate", [P, PADN])
        w_out = sb("w_out", [P, CC, P])
        conv_w = sb("conv_w_sb", [P, XC, TAPS])
        conv_b = sb("conv_b_sb", [P, XC])
        skip = sb("skip", [P, CC])
        norm_w = sb("norm_w_sb", [P, CC])
        dt_bias = sb("dt_bias_sb", [P, H])
        neg_a = sb("neg_a", [P, H])
        w1 = sb("w1", [P, E, FF])
        w2 = sb("w2", [P, E, FB, P])
        b1 = sb("b1_sb", [P, E * FB])
        b2 = sb("b2_sb", [3, E * P], BF16)
        pick3 = sb("pick3", [3, 3])
        ones3 = sb("ones3", [3, P], BF16)
        ident = sb("ident", [P, P])
        upto = sb("upto", [P, P])
        after = sb("after", [P, P])
        before_b = sb("before_b", [P, P], BF16)
        ones = sb("ones", [P, P])
        ones_b = sb("ones_b", [P, P], BF16)
        neg_half = sb("neg_half", [P, NC])
        iota8 = sb("iota8", [P, E])
        iota_tile = sb("iota_tile", [P, TILES])
        token_id = sb("token_id", [P, NC])
        region = sb("region", [P, E])
        next_row = sb("next_row", [P, E])
        pad_tile = sb("pad_tile", [P, ROW])

        xa = [sb(f"xa{i}", [P, NC, P]) for i in range(2)]
        xres = [sb(f"xres{i}", [P, NC, P]) for i in range(2)]
        xT = [sb(f"xT{i}", [P, TOKS]) for i in range(2)]
        acc = sb("acc", [P, XC, TOKS])
        xc = [sb(f"xc{i}", [P, XC, TOKS]) for i in range(2)]
        sz = [sb(f"sz{i}", [P, CC, TOKS]) for i in range(2)]
        xD = [sb(f"xD{i}", [P, CC, TOKS]) for i in range(2)]
        v = sb("v", [P, NC, H])
        vabs = sb("vabs", [P, NC * H])
        ev = sb("ev", [P, NC * H])
        sp = [sb(f"sp{i}", [P, NC * H]) for i in range(5)]
        dtp = [sb(f"dtp{i}", [P, NC * H]) for i in range(2)]
        a = [sb(f"a{i}", [P, PADN]) for i in range(2)]
        decays = [sb(f"decays{i}", [P, 3, NC * H]) for i in range(2)]
        lhsA = [sb(f"lhsA{i}", [P, H, P]) for i in range(2)]
        L = [sb(f"L{i}", [P, H, P]) for i in range(2)]
        Gm = sb("Gm", [P, NC, P])
        M = [sb(f"M{i}", [P, H, P]) for i in range(2)]
        Xdt = [sb(f"Xdt{i}", [P, DI]) for i in range(2)]
        Xdd = [sb(f"Xdd{i}", [P, DI]) for i in range(2)]
        Btok = [sb(f"Btok{i}", [P, P]) for i in range(2)]
        state = [sb(f"state{i}", [P, DI]) for i in range(2)]
        decayed = sb("decayed", [P, DI])
        carried = sb("carried", [P, DI])
        yv = [sb(f"yv{i}", [P, CC, P]) for i in range(2)]
        ysq = sb("ysq", [P, CC, TOKS])
        gt = sb("gt", [P, CC, TOKS])
        ms = sb("ms", [P, NC])
        rms = sb("rms", [P, NC])
        st = sb("st", [P, NC, 6])
        mv = sb("mv", [P, NC, 2])
        ve = sb("ve", [P, NC])
        rstd = sb("rstd", [P, NC])
        rowA = [sb(f"rowA{i}", [P, NC, ROW]) for i in range(2)]
        rowB = [sb(f"rowB{i}", [P, NC, ROW]) for i in range(2)]
        u_all = sb("u_all", [P, SEQS * NC, P])
        b2f, b2r, b2s = (u_all[0:3, E * k:E * (k + 1), :].rearrange("p e d -> p (e d)") for k in range(3))
        b2p = u_all[0:3, 3 * E:5 * E, :].rearrange("p e d -> p (e d)").bitcast(BF16)
        b2p = b2p[:, 0:3 * E * P].rearrange("p (k n) -> p k n", k=3)
        uT = sb("uT", [P, TOKS])
        eg = sb("eg", [P, NC, E])
        gates = sb("gates", [P, NC, E])
        top = sb("top", [P, NC, 8])
        topi = sb("topi", [P, NC, 8], U32)
        topf = sb("topf", [P, NC, 2])
        picks = sb("picks", [P, NC, 2, E])
        chosen = sb("chosen", [P, NC, E], BF16)
        gsum = sb("gsum", [P, NC])
        rows = sb("rows", [P, NC, E])
        prow = sb("prow", [P, NC, 2, E])
        slotf = sb("slotf", [P, NC, 2])
        slot = [sb(f"slot{i}", [P, NC, 2], I32) for i in range(2)]

        tb = sb("tb", [P, 8, E])
        tbi = sb("tbi", [P, E], I32)
        tcmp = sb("tcmp", [1, TILES, E])
        tval = sb("tval", [1, 4, TILES])
        table = sb("table", [1, 2, TILES], I32)
        pad_at = sb("pad_at", [P, E], I32)

        RING = 8
        xs = [sb(f"xs{i}", [P, ROW]) for i in range(RING)]
        sT = Btok
        w1e = [M[i][:, :, :].rearrange("p h s -> p (h s)") for i in range(2)]
        hT = L
        ye = [yv[i // 2][:, i % 2, :] for i in range(4)]

        yy = [acc[:, 2 * i:2 * i + 2, :].rearrange("p k (c d) -> p k c d", c=NC) for i in range(2)]
        fin = [xc[i][:, 0, :].rearrange("p (c d) -> p c d", c=NC) for i in range(2)]
        fout = [xc[i][:, 1, :].rearrange("p (c d) -> p c d", c=NC) for i in range(2)]
        fst = [sb(f"fst{i}", [P, NC, 6]) for i in range(2)]
        fmv = [sb(f"fmv{i}", [P, NC, 2]) for i in range(2)]
        fve = [sb(f"fve{i}", [P, NC]) for i in range(2)]
        frs = [sb(f"frs{i}", [P, NC]) for i in range(2)]
        fnb = [sb(f"fnb{i}", [P, NC]) for i in range(2)]

        pj = [bank(f"pj{i}") for i in range(2)]
        pl = [bank(f"pl{i}") for i in range(2)]
        p4 = bank("p4")
        p5 = bank("p5")
        p6 = bank("p6")
        p7 = bank("p7")

        w_in = sem("w_in")
        moe_w_in = sem("moe_w_in")
        const_ready = sem("const_ready")
        const_step = sem("const_step")
        pool_const = sem("pool_const")
        xa_in = [sem(f"xa_in{i}") for i in range(2)]
        xres_in = [sem(f"xres_in{i}") for i in range(2)]
        names_pe = ("xT_psum", "dt_psum", "proj_psum", "z_psum", "sums_psum", "diff_psum", "G_psum",
                    "tr_psum", "off_psum", "y_psum", "state_psum", "ss_psum", "out_psum", "uT_psum",
                    "logit_psum", "rank_psum")
        (xT_psum, dt_psum, proj_psum, z_psum, sums_psum, diff_psum, G_psum, tr_psum, off_psum, y_psum,
         state_psum, ss_psum, out_psum, uT_psum, logit_psum, rank_psum) = [sem(n) for n in names_pe]
        names_act = ("xT_ready", "abs_done", "ev_ready", "L_ready", "tap0_done", "Btok_ready", "sq_done",
                     "uT_ready", "rowB_ready", "eg_ready", "decays_ready", "xc_ready", "sz_ready",
                     "xD_ready")
        (xT_ready, abs_done, ev_ready, L_ready, tap0_done, Btok_ready, sq_done, uT_ready, rowB_ready,
         eg_ready, decays_ready, xc_ready, sz_ready, xD_ready) = [sem(n) for n in names_act]
        names_dve = ("x1_ready", "Gm_ready", "M_ready", "Xdt_ready", "v_ready", "yv_ready", "state_ready",
                     "sp_step", "a_ready", "tap_done", "conv_done", "carried_ready", "ln_step", "ve_ready",
                     "u_ready", "gate_step", "chosen_ready", "ms_ready", "pos_step", "rank_read",
                     "slot_ready")
        (x1_ready, Gm_ready, M_ready, Xdt_ready, v_ready, yv_ready, state_ready, sp_step, a_ready,
         tap_done, conv_done, carried_ready, ln_step, ve_ready, u_ready, gate_step, chosen_ready,
         ms_ready, pos_step, rank_read, slot_ready) = [sem(n) for n in names_dve]
        names_pool = ("lhsA_ready", "Xdd_ready", "decayed_ready", "g_ready", "rms_ready", "rstd_ready")
        (lhsA_ready, Xdd_ready, decayed_ready, g_ready, rms_ready, rstd_ready) = [sem(n) for n in names_pool]
        scattered = [sem(f"scattered{i}") for i in range(2)]
        u_kept = [sem(f"u_kept{i}") for i in range(2)]
        table_step = sem("table_step")
        table_ready = sem("table_ready")
        spare_in = sem("spare_in")
        pads_in = sem("pads_in")
        xs_in = [sem(f"xs_in{i}") for i in range(RING)]
        rows_out = [sem(f"rows_out{i}") for i in range(RING)]
        names_b = ("sT_psum", "sT_ready", "w1e_ready", "h_psum", "hT_ready", "ye_psum", "ye_ready")
        (sT_psum, sT_ready, w1e_ready, h_psum, hT_ready, ye_psum, ye_ready) = [sem(n) for n in names_b]
        yy_in = [sem(f"yy_in{i}") for i in range(2)]
        fin_out = [sem(f"fin_out{i}") for i in range(2)]
        (fin_step, fve_ready, frs_ready, fnb_ready, fout_ready) = [
            sem(n) for n in ("fin_step", "fve_ready", "frs_ready", "fnb_ready", "fout_ready")]

        CONSTS = 9

        def wait_apart(eng, sem, value):
            if not isinstance(value, int):
                value = eng.to_reg(value)
            eng.wait_ge(const_ready, CONSTS)
            eng.wait_ge(sem, value)

        block = ctx.enter_context(nc.Block())

        x_seq = t["x"].rearrange("b (c p) d -> b p c d", p=P)
        out_seq = out.rearrange("b (c p) d -> b p c d", p=P)
        moe_seq = moe_rows.rearrange("(k b c p) d -> b p k c d", k=2, b=SEQS, p=P)

        def tokens(ap, n=H):
            return ap.rearrange("p (c h) -> p c h", h=n)

        def per_head(ap, c):
            return ap[:, c * H:(c + 1) * H].unsqueeze(2).broadcast_to([P, H, HD])

        def heads(ap):
            return ap.rearrange("p (h d) -> p h d", h=H)

        def slots(eng, slot_fn):
            slot_fn(Seq(0, -1), False, True, False)
            slot_fn(Seq(0, 0), True, True, False)
            slot_fn(Seq(0, 1), True, True, True)
            slot_fn(Seq(0, 2), True, True, True)
            with eng.Fori(1, (SEQS - 2) // 2) as i:
                slot_fn(Seq(i, 1), True, True, True)
                slot_fn(Seq(i, 2), True, True, True)
            slot_fn(Seq(0, SEQS - 1), True, False, True)
            slot_fn(Seq(0, SEQS), False, False, True)

        @block.sync
        def _(dq):
            dq.dma_start(xa[0][:, :, :], x_seq[0]).then_inc(xa_in[0], 16)
            for dst, name in ((w_xbc[:, :], "w_xbc"), (w_dt[:, 0:H], "w_dt"), (w_z[:, :], "w_z"),
                              (w_gate[:, 0:E], "w_gate"),
                              (w_out[:, :, :], "w_out"), (conv_w[:, :, :], "conv_w"),
                              (conv_b[:, :], "conv_b"), (skip[:, :], "skip"), (norm_w[:, :], "norm_w"),
                              (dt_bias[:, :], "dt_bias"), (neg_a[:, :], "A_log"), (b1[:, :], "b1"),
                              (b2f, "b2")):
                if name in ("w_dt", "w_gate"):
                    dq.wait_ge(const_ready, CONSTS)
                dq.dma_start(dst, t[name]).then_inc(w_in, 16)

            def slot_dma(s, scan, project, route):
                if project and not (isinstance(s.n, int) and s.n >= SEQS - 2):
                    q = s.plus(2)
                    wait(dq, xT_psum, q.n - 1)
                    dq.dma_start(xa[q.par][:, :, :], x_seq[q.n]).then_inc(xa_in[q.par], 16)
                if project:
                    q = s.plus(1)
                    wait(dq, x1_ready, NC * (q.n - 1))
                    dq.dma_start(xres[q.par][:, :, :], x_seq[q.n]).then_inc(xres_in[q.par], 16)
                if route:
                    r = s.plus(-1)
                    dq.wait_ge(u_ready, NC * (r.n + 1))
                    dq.dma_start(u_all[:, bass.ds(r.n * NC, NC), :],
                                 rowA[r.par][:, :, 0:P]).then_inc(u_kept[r.par], 16)

            slot_dma(Seq(0, -1), False, True, False)
            dq.dma_start(w1[:, :, :], t["w1"]).then_inc(moe_w_in, 16)
            slot_dma(Seq(0, 0), True, True, False)
            dq.dma_start(w2[:, :, :, :], t["w2"]).then_inc(moe_w_in, 16)
            for k in range(E):
                dq.dma_start(sorted_rows[SPARE + k * P:SPARE + (k + 1) * P, :],
                             pad_tile[:, :]).then_inc(spare_in, 16)
            slot_dma(Seq(0, 1), True, True, True)
            slot_dma(Seq(0, 2), True, True, True)
            with dq.Fori(1, (SEQS - 4) // 2) as i:
                slot_dma(Seq(i, 1), True, True, True)
                slot_dma(Seq(i, 2), True, True, True)
            slot_dma(Seq(0, SEQS - 3), True, True, True)
            slot_dma(Seq(0, SEQS - 2), True, True, True)
            slot_dma(Seq(0, SEQS - 1), True, False, True)
            slot_dma(Seq(0, SEQS), False, False, True)

            dq.wait_ge(table_ready, 1)
            for k in range(E):
                at = dq.value_load(pad_at[0:1, k:k + 1], min_val=k * REGION,
                                   max_val=k * REGION + TOKENS)
                dq.dma_start(sorted_rows[bass.ds(at, P), :], pad_tile[:, :]).then_inc(pads_in, 16)
            dq.wait_ge(pads_in, 16 * E)
            dq.wait_ge(spare_in, 16 * E)
            for i in range(2):
                dq.wait_ge(scattered[i], 16 * 2 * NC * SEQS // 2)

            def load_rows(tile, k, turn):
                wait(dq, rows_out[k], 16 * turn)
                at = dq.value_load(table[0:1, 0, bass.ds(tile, 1)], min_val=0, max_val=SPARE + (E - 1) * P)
                dq.dma_start(xs[k][:, :], sorted_rows[bass.ds(at, P), :]).then_inc(xs_in[k], 16)

            for k in range(RING):
                load_rows(k, k, 0)
            with dq.Fori(1, TILES // RING) as i:
                for k in range(RING):
                    load_rows(RING * i + k, k, i)

            for k in range(RING):
                dq.wait_ge(rows_out[k], 16 * TILES // RING)

            def load_moe(s):
                wait(dq, fin_step, FIN_STEPS * (s.n - 1))
                for k in range(2):
                    dq.dma_start(yy[s.par][:, k], moe_seq[s.n, :, k]).then_inc(yy_in[s.par], 16)

            load_moe(Seq(0, 0))
            load_moe(Seq(0, 1))
            with dq.Fori(0, SEQS // 2 - 1) as i:
                load_moe(Seq(i, 2))
                load_moe(Seq(i, 3))
            for i in range(2):
                dq.wait_ge(fin_out[i], 16 * SEQS // 2)

        @block.tensor
        def _(pe):
            pe.wait_ge(const_ready, CONSTS)

            def project_block(q, k):
                if k == 0:
                    pe.wait_ge(xT_ready, q.n + 1)
                elif k == 1:
                    pe.wait_ge(v_ready, q.n + 1)
                else:
                    pe.wait_ge(conv_done, XC * q.n + k - 1)
                pe.matmul(pj[k % 2][:, :], w_xbc[:, k * P:(k + 1) * P], xT[q.par][:, :],
                          start=True, stop=True).then_inc(proj_psum, 1)

            def z_block(q, k):
                pe.wait_ge(conv_done, XC * q.n + k + 3)
                pe.matmul(pj[k][:, :], w_z[:, k * P:(k + 1) * P], xT[q.par][:, :],
                          start=True, stop=True).then_inc(z_psum, 1)

            def exponents(n, c):
                pe.wait_ge(lhsA_ready, n + 1)
                wait(pe, L_ready, n - 1)
                for h in range(H):
                    mm = pe.matmul(pl[c % 2][:, h * P:(h + 1) * P], lhsA[c % 2][:, h, :], upto[:, :],
                                   start=True, stop=True)
                mm.then_inc(diff_psum, 1)

            def slot_pe(s, scan, project, route):
                q, r = s.plus(1), s.plus(-1)
                if project:
                    pe.wait_ge(xa_in[q.par], 16 * (q.use + 1))
                    wait(pe, sz_ready, CC * q.n - 1)
                    for c in range(NC):
                        mm = pe.transpose(pj[0][:, c * P:(c + 1) * P], xa[q.par][:, c, :], ident[:, :])
                    mm.then_inc(xT_psum, 1)
                    pe.wait_ge(xT_ready, q.n + 1)
                    wait(pe, sz_ready, CC * q.n)
                    if isinstance(s.n, int) and s.n < 0:
                        pe.wait_ge(w_in, 16 * 13)
                    for c in range(NC):
                        mm = pe.matmul(pj[1][:, c * PADN:(c + 1) * PADN], xT[q.par][:, c * P:(c + 1) * P],
                                       w_dt[:, :], start=True, stop=True)
                    mm.then_inc(dt_psum, 1)
                if scan:
                    pe.wait_ge(xc_ready, XC * (s.n + 1))
                    wait(pe, rank_read, s.n - 1)
                    pe.wait_ge(decays_ready, s.n + 1)
                    for c in range(NC):
                        tok = slice(c * P, (c + 1) * P)
                        mm = pe.matmul(p4[:, tok], xc[s.par][:, CC, tok], xc[s.par][:, CC + 1, tok],
                                       start=True, stop=True)
                    mm.then_inc(G_psum, 1)
                for c in range(NC):
                    tok = slice(c * P, (c + 1) * P)
                    n = NC * s.n + c
                    if scan and (c + 1 < NC or project):
                        exponents(n + 1, c + 1)
                    if scan:
                        pe.wait_ge(Xdt_ready, n) if not isinstance(n, int) or n > 0 else None
                        wait(pe, Btok_ready, (NC - 1) * s.n + c)
                        if c == 0:
                            wait(pe, x1_ready, NC * s.n)
                        for k in range(CC):
                            mm = pe.transpose(p5[:, k * P:(k + 1) * P], xc[s.par][:, k, tok], ident[:, :])
                        if c + 1 < NC:
                            mm = pe.transpose(p5[:, CC * P:(CC + 1) * P], xc[s.par][:, CC, tok], ident[:, :])
                        mm.then_inc(tr_psum, 1)
                    if project:
                        project_block(q, c)
                    if scan:
                        if c > 0:
                            pe.wait_ge(state_ready, (NC - 1) * s.n + c)
                            pe.matmul(p6[:, 0:DI], xc[s.par][:, CC + 1, tok], state[(c - 1) % 2][:, :],
                                      start=True, stop=True).then_inc(off_psum, 1)
                        pe.wait_ge(M_ready, n + 1)
                        pe.wait_ge(Xdt_ready, n + 1)
                        if c == 0:
                            wait(pe, ms_ready, s.n)
                        else:
                            pe.wait_ge(yv_ready, n)
                        for h in range(H):
                            half = slice((h % 2) * HD, (h % 2 + 1) * HD)
                            mm = pe.matmul(p7[half, (h // 2) * P:(h // 2 + 1) * P],
                                           Xdt[c % 2][:, h * HD:(h + 1) * HD], M[c % 2][:, h, :],
                                           start=(h < 2), stop=(c == 0), skip_group_check=True)
                        if c > 0:
                            pe.wait_ge(carried_ready, (NC - 1) * s.n + c)
                            for k in range(CC):
                                mm = pe.matmul(p7[:, k * P:(k + 1) * P], carried[:, k * P:(k + 1) * P],
                                               ident[:, :], start=False, stop=True, skip_group_check=True)
                        mm.then_inc(y_psum, 1)
                        if c + 1 < NC:
                            pe.wait_ge(Btok_ready, (NC - 1) * s.n + c + 1)
                            pe.wait_ge(Xdd_ready, (NC - 1) * s.n + c + 1)
                            if c == 0:
                                wait(pe, carried_ready, (NC - 1) * s.n)
                            pe.matmul(p6[:, DI:2 * DI], Btok[c % 2][:, :], Xdd[c % 2][:, :],
                                      start=True, stop=True).then_inc(state_psum, 1)
                    if route and c == 1:
                        pe.wait_ge(u_ready, NC * (r.n + 1))
                        if scan:
                            pe.wait_ge(Gm_ready, s.n + 1)
                        for k in range(NC):
                            mm = pe.transpose(p4[:, k * P:(k + 1) * P], rowA[r.par][:, k, 0:P], ident[:, :])
                        mm.then_inc(uT_psum, 1)
                    if route and c == 2:
                        pe.wait_ge(uT_ready, r.n + 1)
                        for k in range(NC):
                            mm = pe.matmul(p4[:, k * PADN:(k + 1) * PADN], uT[:, k * P:(k + 1) * P],
                                           w_gate[:, :], start=True, stop=True)
                        mm.then_inc(logit_psum, 1)
                if project:
                    pe.wait_ge(a_ready, q.n + 1)
                    if route:
                        pe.wait_ge(eg_ready, r.n + 1)
                    elif scan:
                        pe.wait_ge(Gm_ready, s.n + 1)
                    for k, mask in enumerate((upto, after, ones)):
                        mm = pe.matmul(p4[:, k * PADN:(k + 1) * PADN], mask[:, :], a[q.par][:, :],
                                       start=True, stop=True)
                    mm.then_inc(sums_psum, 1)
                if scan:
                    pe.wait_ge(sq_done, NC * (s.n + 1))
                    pe.wait_ge(yv_ready, NC * (s.n + 1))
                    for c in range(NC):
                        for k in range(CC):
                            mm = pe.matmul(p7[:, c * PADN:(c + 1) * PADN], ysq[:, k, c * P:(c + 1) * P],
                                           ones[:, 0:PADN], start=(k == 0), stop=(k == CC - 1))
                    mm.then_inc(ss_psum, 1)
                if project:
                    z_block(q, 0)
                if scan:
                    pe.wait_ge(g_ready, NC * (s.n + 1))
                    pe.wait_ge(Xdt_ready, NC * (s.n + 1))
                    for c in range(NC):
                        for k in range(CC):
                            mm = pe.matmul(p5[:, c * P:(c + 1) * P], gt[:, k, c * P:(c + 1) * P],
                                           w_out[:, k, :], start=(k == 0), stop=(k == CC - 1))
                    mm.then_inc(out_psum, 1)
                if route:
                    pe.wait_ge(chosen_ready, r.n + 1)
                    if project:
                        pe.wait_ge(decays_ready, q.n + 1)
                    else:
                        pe.wait_ge(eg_ready, r.n + 1)
                    for c in range(NC + 1):
                        for k in range(c):
                            mm = pe.matmul(p4[:, c * E:(c + 1) * E], ones_b[:, :], chosen[:, k, :],
                                           start=(k == 0), stop=(k == NC - 1))
                        if c < NC:
                            mm = pe.matmul(p4[:, c * E:(c + 1) * E], before_b[:, :], chosen[:, c, :],
                                           start=(c == 0), stop=True)
                    mm.then_inc(rank_psum, 1)
                if project:
                    z_block(q, 1)
                if project and not scan:
                    exponents(0, 0)

            slots(pe, slot_pe)

            pe.wait_ge(rank_read, SEQS)
            pe.wait_ge(table_ready, 1)
            pe.wait_ge(moe_w_in, 32)

            def transpose_rows(j, k, turn):
                pe.wait_ge(xs_in[k], 16 * (turn + 1))
                wait(pe, sT_ready, j - 1)
                pe.transpose(pj[k % 2][:, 0:P], xs[k][:, 0:P], ident[:, :]).then_inc(sT_psum, 1)

            def up(j, k):
                pe.wait_ge(sT_ready, j + 1)
                pe.wait_ge(w1e_ready, j + 1)
                wait(pe, hT_ready, FB * (j - 1))
                for f in range(FB):
                    mm = pe.matmul(pl[k % 2][:, f * P:(f + 1) * P], w1e[k % 2][:, f * P:(f + 1) * P],
                                   sT[k % 2][:, :], start=True, stop=True)
                mm.then_inc(h_psum, 1)

            def down(j, k):
                e = pe.value_load(table[0:1, 1, bass.ds(j, 1)], min_val=0, max_val=E - 1)
                pe.wait_ge(hT_ready, FB * (j + 1))
                wait(pe, ye_ready, j - 1)
                o = (p6, p7)[k % 2]
                pe.matmul(o[:, 0:P], ones3[:, :], b2[:, bass.ds(e * P, P)], start=True, stop=False)
                for f in range(FB):
                    mm = pe.matmul(o[:, 0:P], hT[k % 2][:, f, :], w2[:, bass.ds(e, 1), f, :].rearrange("p e d -> p (e d)"),
                                   start=False, stop=(f == FB - 1))
                mm.then_inc(ye_psum, 1)

            transpose_rows(0, 0, 0)
            transpose_rows(1, 1, 0)
            up(0, 0)
            def turn_pe(i):
                for k in range(RING):
                    j = RING * i + k
                    transpose_rows(j + 2, (k + 2) % RING, i + (k + 2) // RING)
                    up(j + 1, k + 1)
                    down(j, k)

            turn_pe(0)
            with pe.Fori(1, TILES // RING - 1) as i:
                turn_pe(i)
            for k in range(RING):
                j = TILES - RING + k
                if k + 2 < RING:
                    transpose_rows(j + 2, k + 2, TILES // RING - 1)
                if k + 1 < RING:
                    up(j + 1, k + 1)
                down(j, k)

        @block.scalar
        def _(act):
            act.wait_ge(w_in, 16 * 13)
            act.activation(neg_a[:, :], neg_a[:, :], ACT.Exp).then_inc(const_step, 1)

            def exp_exponents(n, c):
                act.wait_ge(diff_psum, n + 1)
                wait(act, M_ready, n - 1)
                act.activation(L[c % 2][:, :, :], pl[c % 2][:, :], ACT.Exp).then_inc(L_ready, 1)

            def slot_act(s, scan, project, route):
                q, r = s.plus(1), s.plus(-1)
                if project:
                    act.wait_ge(xT_psum, q.n + 1)
                    wait(act, z_psum, CC * (q.n - 1))
                    act.copy(xT[q.par][:, :], pj[0][:, :]).then_inc(xT_ready, 1)
                for c in range(NC):
                    n = NC * s.n + c
                    tok = slice(c * P, (c + 1) * P)
                    if scan and (c + 1 < NC or project):
                        exp_exponents(n + 1, c + 1)
                    if scan and c + 1 < NC:
                        act.wait_ge(tr_psum, n + 1)
                        wait(act, state_psum, (NC - 1) * s.n + c - 1)
                        act.copy(Btok[c % 2][:, :], p5[:, CC * P:(CC + 1) * P]).then_inc(Btok_ready, 1)
                    if project and c == 0:
                        act.wait_ge(v_ready, q.n + 1)
                        act.activation(vabs[:, :], v[:, :, :], ACT.Abs).then_inc(abs_done, 1)
                        act.wait_ge(abs_done, q.n + 1)
                        wait(act, a_ready, q.n)
                        act.activation(ev[:, :], vabs[:, :], ACT.Exp, scale=-1.0).then_inc(ev_ready, 1)
                    if project:
                        act.wait_ge(proj_psum, XC * q.n + c + 1)
                        wait(act, xc_ready, XC * (q.n - 1) + c + 1)
                        act.activation(acc[:, c, :], pj[c % 2][:, :], ACT.Identity,
                                       bias=conv_b[:, c:c + 1],
                                       scale=conv_w[:, c, TAPS - 1:TAPS]).then_inc(tap0_done, 1)
                    if scan:
                        act.wait_ge(yv_ready, n + 1)
                        wait(act, ss_psum, s.n)
                        act.activation(ysq[:, :, tok], yv[c % 2][:, :, :],
                                       ACT.Square).then_inc(sq_done, 1)
                    if route and c == 1:
                        act.wait_ge(uT_psum, r.n + 1)
                        act.copy(uT[:, :], p4[:, :]).then_inc(uT_ready, 1)
                        if not (isinstance(r.n, int) and r.n < 2):
                            act.wait_ge(scattered[r.par], 16 * 2 * NC * r.use)
                        act.copy(rowB[r.par][:, :, 0:P], rowA[r.par][:, :, 0:P]).then_inc(rowB_ready, 1)
                    if route and c == 2:
                        act.wait_ge(logit_psum, r.n + 1)
                        act.activation(eg[:, :, :],
                                       p4[:, 0:NC * PADN].rearrange("p (c e) -> p c e", e=PADN)[:, :, 0:E],
                                       ACT.Exp, scale=-1.0).then_inc(eg_ready, 1)
                if project:
                    act.wait_ge(sums_psum, q.n + 1)
                    act.activation(decays[q.par][:, :, :],
                                   p4[:, 0:3 * PADN].rearrange("p (k e) -> p k e", e=PADN)[:, :, 0:NC * H],
                                   ACT.Exp).then_inc(decays_ready, 1)
                    if not scan:
                        exp_exponents(0, 0)
                    for k in range(XC):
                        act.wait_ge(conv_done, XC * q.n + k + 1)
                        wait(act, y_psum, NC * (q.n - 1))
                        act.activation(xc[q.par][:, k, :], acc[:, k, :], ACT.Silu).then_inc(xc_ready, 1)
                    for k in range(CC):
                        act.wait_ge(z_psum, CC * q.n + k + 1)
                        wait(act, g_ready, NC * (q.n - 1))
                        act.activation(sz[q.par][:, k, :], pj[k][:, :], ACT.Silu).then_inc(sz_ready, 1)
                    for k in range(CC):
                        act.wait_ge(xc_ready, XC * q.n + k + 1)
                        wait(act, yv_ready, NC * (q.n - 1))
                        act.activation(xD[q.par][:, k, :], xc[q.par][:, k, :], ACT.Identity,
                                       scale=skip[:, k:k + 1]).then_inc(xD_ready, 1)

            slots(act, slot_act)

            def gelu(j, k):
                e = act.value_load(table[0:1, 1, bass.ds(j, 1)], min_val=0, max_val=E - 1)
                act.wait_ge(h_psum, j + 1)
                wait(act, ye_psum, j - 1)
                for f in range(FB):
                    act.activation(hT[k % 2][:, f, :], pl[k % 2][:, f * P:(f + 1) * P], ACT.Gelu,
                                   bias=b1[:, bass.ds(e * FB + f, 1)]).then_inc(hT_ready, 1)

            act.wait_ge(table_ready, 1)
            for k in range(RING):
                gelu(k, k)
            with act.Fori(1, TILES // RING) as i:
                for k in range(RING):
                    gelu(RING * i + k, k)

            def finish(s):
                act.wait_ge(frs_ready, s.n + 1)
                act.wait_ge(fnb_ready, s.n + 1)
                if not (isinstance(s.n, int) and s.n < 2):
                    act.wait_ge(fin_out[s.par], 16 * s.use)
                for c in range(NC):
                    act.activation(fout[s.par][:, c, :], fin[s.par][:, c, :], ACT.Identity,
                                   bias=fnb[s.par][:, c:c + 1],
                                   scale=frs[s.par][:, c:c + 1]).then_inc(fout_ready, 1)
                act.wait_ge(fout_ready, NC * (s.n + 1))
                act.dma_start(out_seq[s.n], fout[s.par]).then_inc(fin_out[s.par], 16)

            finish(Seq(0, 0))
            finish(Seq(0, 1))
            with act.Fori(0, SEQS // 2 - 1) as i:
                finish(Seq(i, 2))
                finish(Seq(i, 3))

        @block.vector
        def _(dve):
            def chain(s, base):
                count = [base]

                def link(ins, apart=False):
                    count[0] = count[0] + 1
                    ins.then_inc(s, 1)
                    if apart:
                        wait_apart(dve, s, count[0])
                    else:
                        dve.wait_ge(s, count[0])
                return link

            link = chain(const_step, 1)
            dve.memset(w_dt[:, :], 0.0).then_inc(const_ready, 1)
            dve.memset(w_gate[:, :], 0.0).then_inc(const_ready, 1)
            dve.memset(a[0][:, :], 0.0).then_inc(const_ready, 1)
            dve.memset(a[1][:, :], 0.0).then_inc(const_ready, 1)
            dve.memset(ones[:, :], 1.0).then_inc(const_ready, 1)
            dve.memset(ones_b[:, :], 1.0).then_inc(const_ready, 1)
            dve.memset(ones3[:, :], 1.0).then_inc(const_ready, 1)
            dve.memset(neg_half[:, :], -0.5).then_inc(const_ready, 1)
            dve.wait_ge(w_in, 16 * 13)
            dve.wait_ge(const_step, 1)
            link(dve.tensor_scalar(neg_a[:, :], neg_a[:, :], -1.0, None, ALU.mult))
            for k in range(CC):
                link(dve.tensor_scalar(w_out[:, k, :], w_out[:, k, :], norm_w[:, k:k + 1], None, ALU.mult))
            dve.wait_ge(const_ready, CONSTS)
            link(dve.tensor_copy(b2p[:, 0, :], b2f))
            link(dve.tensor_tensor(b2r, b2f, b2p[:, 0, :], ALU.subtract))
            link(dve.tensor_copy(b2p[:, 1, :], b2r))
            link(dve.tensor_tensor(b2r, b2r, b2p[:, 1, :], ALU.subtract))
            link(dve.tensor_copy(b2p[:, 2, :], b2r))
            link(dve.tensor_scalar(b2s, b2p[:, 0, :], pick3[:, 0:1], None, ALU.mult))
            link(dve.scalar_tensor_tensor(out=b2s, in0=b2p[:, 1, :], scalar=pick3[:, 1:2],
                                          in1=b2s, op0=ALU.mult, op1=ALU.add))
            link(dve.scalar_tensor_tensor(out=b2[:, :], in0=b2p[:, 2, :], scalar=pick3[:, 2:3],
                                          in1=b2s, op0=ALU.mult, op1=ALU.add))

            def tap(q, k, j):
                done = (TAPS - 2) * (XC * q.n + k)
                if j == 1:
                    dve.wait_ge(tap0_done, XC * q.n + k + 1)
                else:
                    dve.wait_ge(tap_done, done + j - 1)
                ins = dve.scalar_tensor_tensor(
                    out=acc[:, k, j:TOKS], in0=pj[k % 2][:, 0:TOKS - j],
                    scalar=conv_w[:, k, TAPS - 1 - j:TAPS - j], in1=acc[:, k, j:TOKS],
                    op0=ALU.mult, op1=ALU.add)
                if j < TAPS - 1:
                    ins.then_inc(tap_done, 1)
                else:
                    ins.then_inc(conv_done, 1)

            def softplus(q):
                link = chain(sp_step, SP_STEPS * q.n)
                w, w2_, pp, t1, mx = (b[:, :] for b in sp)
                dve.wait_ge(ev_ready, q.n + 1)
                link(dve.tensor_scalar(t1, ev[:, :], 2.0, None, ALU.add))
                link(dve.reciprocal(t1, t1))
                link(dve.tensor_tensor(w, t1, ev[:, :], ALU.mult))
                link(dve.tensor_tensor(w2_, w, w, ALU.mult))
                link(dve.tensor_scalar(pp, w2_, 1.0 / LOG_TERMS[0], None, ALU.mult))
                for term in LOG_TERMS[1:]:
                    link(dve.scalar_tensor_tensor(out=pp, in0=pp, scalar=1.0 / term, in1=w2_,
                                                  op0=ALU.add, op1=ALU.mult))
                link(dve.scalar_tensor_tensor(out=pp, in0=pp, scalar=1.0, in1=w, op0=ALU.add, op1=ALU.mult))
                link(dve.tensor_scalar(mx, v[:, :, :].rearrange("p c h -> p (c h)"), 0.0, None, ALU.max))
                if not (isinstance(q.n, int) and q.n < 2):
                    dve.wait_ge(Xdt_ready, NC * (q.n - 1))
                link(dve.scalar_tensor_tensor(out=dtp[q.par][:, :], in0=pp, scalar=2.0, in1=mx,
                                              op0=ALU.mult, op1=ALU.add))
                wait(dve, lhsA_ready, NC * (q.n - 1))
                dve.tensor_tensor(tokens(a[q.par][:, 0:NC * H]), tokens(dtp[q.par][:, :]),
                                  neg_a[:, :].unsqueeze(1).broadcast_to([P, NC, H]),
                                  ALU.mult).then_inc(a_ready, 1)

            def slot_dve(s, scan, project, route):
                q, r = s.plus(1), s.plus(-1)
                if route:
                    dve.wait_ge(out_psum, r.n + 1)
                    dve.wait_ge(rms_ready, r.n + 1)
                    dve.wait_ge(xres_in[r.par], 16 * (r.use + 1))
                    if not (isinstance(r.n, int) and r.n < 2):
                        dve.wait_ge(scattered[r.par], 16 * 2 * NC * r.use)
                        dve.wait_ge(u_kept[r.par], 16 * r.use)
                    for c in range(NC):
                        dve.scalar_tensor_tensor(
                            out=rowA[r.par][:, c, 0:P], in0=p5[:, c * P:(c + 1) * P],
                            scalar=rms[:, c:c + 1], in1=xres[r.par][:, c, :],
                            op0=ALU.mult, op1=ALU.add).then_inc(x1_ready, 1)
                if scan:
                    dve.wait_ge(G_psum, s.n + 1)
                    dve.tensor_tensor(Gm[:, :, :], p4[:, :].rearrange("p (c k) -> p c k", c=NC),
                                      upto[:, :].unsqueeze(1).broadcast_to([P, NC, P]),
                                      ALU.mult).then_inc(Gm_ready, 1)
                for c in range(NC):
                    n = NC * s.n + c
                    prev = c - 1
                    if scan:
                        dve.wait_ge(Gm_ready, s.n + 1)
                        dve.wait_ge(L_ready, n + 1)
                        wait(dve, y_psum, n - 1)
                        dve.tensor_tensor(M[c % 2][:, :, :], L[c % 2][:, :, :],
                                          Gm[:, c, :].unsqueeze(1).broadcast_to([P, H, P]),
                                          ALU.mult).then_inc(M_ready, 1)
                    if project and prev >= 0:
                        tap(q, prev, 1)
                    if scan:
                        dve.wait_ge(tr_psum, n + 1)
                        if c + 1 < NC:
                            dve.wait_ge(Btok_ready, (NC - 1) * s.n + c + 1)
                        wait(dve, Xdd_ready, (NC - 1) * s.n + max(c - 1, 0))
                        dve.tensor_tensor(heads(Xdt[c % 2][:, :]), heads(p5[:, 0:DI]),
                                          per_head(dtp[s.par], c), ALU.mult).then_inc(Xdt_ready, 1)
                    if project and prev >= 0:
                        tap(q, prev, 2)
                    if project and c == 0:
                        dve.wait_ge(dt_psum, q.n + 1)
                        wait(dve, a_ready, q.n)
                        wait(dve, abs_done, q.n)
                        dve.tensor_tensor(
                            v[:, :, :], pj[1][:, 0:NC * PADN].rearrange("p (c e) -> p c e", e=PADN)[:, :, 0:H],
                            dt_bias[:, :].unsqueeze(1).broadcast_to([P, NC, H]),
                            ALU.add).then_inc(v_ready, 1)
                    if route and c == 0:
                        ln = LN_STEPS * r.n
                        dve.wait_ge(x1_ready, NC * (r.n + 1))
                        for k in range(NC):
                            ins = dve.bn_stats(st[:, k, :], rowA[r.par][:, k, 0:P])
                        ins.then_inc(ln_step, 1)
                        wait_apart(dve, ln_step, ln + 1)
                        for k in range(NC):
                            ins = dve.bn_aggr(mv[:, k, :], st[:, k, :])
                        ins.then_inc(ln_step, 1)
                        dve.wait_ge(ln_step, ln + 2)
                        dve.tensor_scalar(ve[:, :], mv[:, :, 1], EPS, None, ALU.add).then_inc(ve_ready, 1)
                    if project and prev >= 0:
                        tap(q, prev, 3)
                    if route and c == 1:
                        dve.wait_ge(rstd_ready, r.n + 1)
                        for k in range(NC):
                            dve.tensor_scalar(rowA[r.par][:, k, 0:P], rowA[r.par][:, k, 0:P],
                                              mv[:, k, 0:1], rstd[:, k:k + 1], ALU.subtract,
                                              ALU.mult).then_inc(u_ready, 1)
                    if scan and c > 0:
                        dve.wait_ge(off_psum, (NC - 1) * s.n + c)
                        dve.tensor_tensor(heads(carried[:, :]), heads(p6[:, 0:DI]),
                                          per_head(decays[s.par][:, 0, :], c),
                                          ALU.mult).then_inc(carried_ready, 1)
                    if scan:
                        dve.wait_ge(y_psum, n + 1)
                        dve.wait_ge(xD_ready, CC * (s.n + 1))
                        wait(dve, sq_done, n - 1)
                        wait(dve, g_ready, n - 1)
                        dve.tensor_tensor(yv[c % 2][:, :, :], p7[:, 0:DI].rearrange("p (k d) -> p k d", k=CC),
                                          xD[s.par][:, :, c * P:(c + 1) * P], ALU.add).then_inc(yv_ready, 1)
                    if scan and c + 1 < NC:
                        dve.wait_ge(state_psum, (NC - 1) * s.n + c + 1)
                        if c == 0:
                            dve.tensor_copy(state[0][:, :], p6[:, DI:2 * DI]).then_inc(state_ready, 1)
                        else:
                            dve.wait_ge(decayed_ready, (NC - 2) * s.n + c)
                            dve.tensor_tensor(state[c % 2][:, :], p6[:, DI:2 * DI], decayed[:, :],
                                              ALU.add).then_inc(state_ready, 1)
                    if project and c == 0:
                        softplus(q)
                if route:
                    link = chain(gate_step, GATE_STEPS * r.n)
                    dve.wait_ge(eg_ready, r.n + 1)
                    link(dve.tensor_scalar(eg[:, :, :], eg[:, :, :], 1.0, None, ALU.add))
                    link(dve.reciprocal(gates[:, :, :], eg[:, :, :]), apart=True)
                    for k in range(NC):
                        ins = dve.max(top[:, k, :], gates[:, k, :])
                    link(ins, apart=True)
                    for k in range(NC):
                        ins = dve.max_index(topi[:, k, :], top[:, k, :], gates[:, k, :])
                    link(ins)
                    link(dve.tensor_copy(topf[:, :, :], topi[:, :, 0:2]))
                    if not (isinstance(r.n, int) and r.n < 1):
                        dve.wait_ge(slot_ready, r.n)
                    link(dve.tensor_tensor(
                        picks[:, :, :, :], iota8[:, :].unsqueeze(1).unsqueeze(1).broadcast_to([P, NC, 2, E]),
                        topf[:, :, :].unsqueeze(3).broadcast_to([P, NC, 2, E]), ALU.is_equal))
                    dve.tensor_tensor(chosen[:, :, :], picks[:, :, 0, :], picks[:, :, 1, :],
                                      ALU.add).then_inc(chosen_ready, 1)
                if project:
                    tap(q, NC - 1, 1)
                if scan:
                    dve.wait_ge(ss_psum, s.n + 1)
                    wait(dve, rms_ready, s.n)
                    dve.tensor_scalar(ms[:, :], p7[:, 0:NC * PADN].rearrange("p (c e) -> p c e", e=PADN)[:, :, 0],
                                      1.0 / DI, EPS, ALU.mult, ALU.add).then_inc(ms_ready, 1)
                if project:
                    tap(q, NC - 1, 2)
                    tap(q, NC - 1, 3)
                if route:
                    link = chain(pos_step, POS_STEPS * r.n)
                    dve.wait_ge(rank_psum, r.n + 1)
                    dve.tensor_tensor(rows[:, :, :], p4[:, 0:NC * E].rearrange("p (c e) -> p c e", e=E),
                                      next_row[:, :].unsqueeze(1).broadcast_to([P, NC, E]), ALU.add)
                    link(dve.tensor_tensor(gsum[:, :], top[:, :, 0], top[:, :, 1], ALU.add))
                    dve.tensor_tensor(next_row[:, :], p4[:, NC * E:(NC + 1) * E], next_row[:, :],
                                      ALU.add).then_inc(rank_read, 1)
                    dve.wait_ge(rowB_ready, r.n + 1)
                    dve.reciprocal(gsum[:, :], gsum[:, :])
                    link(dve.tensor_tensor(prow[:, :, :, :], picks[:, :, :, :],
                                           rows[:, :, :].unsqueeze(2).broadcast_to([P, NC, 2, E]), ALU.mult))
                    link(dve.tensor_reduce(slotf[:, :, :], prow[:, :, :, :], AX_X, ALU.add))
                    for row, k in ((rowA, 0), (rowB, 1)):
                        dve.tensor_tensor(row[r.par][:, :, P + 1], top[:, :, k], gsum[:, :], ALU.mult)
                        dve.tensor_scalar(row[r.par][:, :, P].bitcast(I32), token_id[:, :],
                                          float(TOKENS * k), None, ALU.add)
                    link(dve.tensor_copy(slot[r.par][:, :, :], slotf[:, :, :]))
                    dve.tensor_scalar(token_id[:, :], token_id[:, :], float(TOKS), None,
                                      ALU.add).then_inc(slot_ready, 1)

            slots(dve, slot_dve)

            link = chain(table_step, 0)
            dve.wait_ge(slot_ready, SEQS)
            cnt, f, tiles, ends = tb[:, 0, :], tb[:, 1, :], tb[:, 2, :], tb[:, 3, :]
            link(dve.tensor_copy(pad_at[:, :], next_row[:, :]))
            link(dve.tensor_tensor(cnt, next_row[:, :], region[:, :], ALU.subtract))
            link(dve.tensor_scalar(f, cnt, float(P - 1), None, ALU.add))
            link(dve.tensor_copy(tbi[:, :], f))
            link(dve.tensor_scalar(tbi[:, :], tbi[:, :], P.bit_length() - 1, None, ALU.logical_shift_right))
            link(dve.tensor_copy(tiles, tbi[:, :]))
            link(dve.tensor_copy(ends, tiles))
            for e in range(1, E):
                link(dve.tensor_tensor(ends[:, e:e + 1], ends[:, e - 1:e], ends[:, e:e + 1], ALU.add))
            one = slice(0, 1)
            expert, start, base, last = (tval[:, k, :] for k in range(4))
            tiles_of = iota_tile[one, :].unsqueeze(2).broadcast_to([1, TILES, E])
            link(dve.tensor_tensor(tcmp[:, :, :], tiles_of,
                                   ends[one, :].unsqueeze(1).broadcast_to([1, TILES, E]), ALU.is_ge))
            link(dve.tensor_reduce(expert, tcmp[:, :, :], AX_X, ALU.add))
            link(dve.tensor_tensor(tcmp[:, :, :], tcmp[:, :, :],
                                   tiles[one, :].unsqueeze(1).broadcast_to([1, TILES, E]), ALU.mult))
            link(dve.tensor_reduce(start, tcmp[:, :, :], AX_X, ALU.add))
            link(dve.tensor_tensor(start, iota_tile[one, :], start, ALU.subtract))
            link(dve.tensor_scalar(base, expert, float(REGION), None, ALU.mult))
            link(dve.scalar_tensor_tensor(out=base, in0=start, scalar=float(P), in1=base,
                                          op0=ALU.mult, op1=ALU.add))
            link(dve.tensor_copy(table[:, 0, :], base))
            link(dve.tensor_scalar(last, expert, float(E - 1), None, ALU.min))
            dve.tensor_copy(table[:, 1, :], last).then_inc(table_ready, 1)

            dve.wait_ge(table_ready, 1)
            dve.wait_ge(moe_w_in, 32)

            def fetch(j, k):
                e = dve.value_load(table[0:1, 1, bass.ds(j, 1)], min_val=0, max_val=E - 1)
                wait(dve, h_psum, j - 1)
                dve.tensor_copy(w1e[k % 2], w1[:, bass.ds(e, 1), :].rearrange("p e f -> p (e f)")).then_inc(w1e_ready, 1)
                dve.wait_ge(sT_psum, j + 1)
                dve.tensor_copy(sT[k % 2][:, :], pj[k % 2][:, 0:P]).then_inc(sT_ready, 1)

            def weigh(j, k, turn, first):
                dve.wait_ge(ye_psum, j + 1)
                if not first:
                    dve.wait_ge(rows_out[(k - 4) % RING], 16 * (turn + (1 if k >= 4 else 0)))
                dve.tensor_scalar(ye[k % 4], (p6, p7)[k % 2][:, 0:P], xs[k][:, P + 1:P + 2], None,
                                  ALU.mult).then_inc(ye_ready, 1)

            fetch(0, 0)
            fetch(1, 1)
            for k in range(RING):
                fetch(k + 2, k + 2)
                weigh(k, k, 0, k < 4)
            with dve.Fori(1, TILES // RING - 1) as i:
                for k in range(RING):
                    fetch(RING * i + k + 2, k + 2)
                    weigh(RING * i + k, k, i, False)
            for k in range(RING):
                j = TILES - RING + k
                if k + 2 < RING:
                    fetch(j + 2, k + 2)
                weigh(j, k, TILES // RING - 1, False)

            def finish(s):
                p = s.par
                link = chain(fin_step, FIN_STEPS * s.n)
                dve.wait_ge(yy_in[p], 32 * (s.use + 1))
                wait(dve, fout_ready, NC * (s.n - 1))
                link(dve.tensor_tensor(fin[p], yy[p][:, 0], yy[p][:, 1], ALU.add))
                link(dve.tensor_tensor(fin[p], u_all[:, bass.ds(s.n * NC, NC), :], fin[p], ALU.add))
                for c in range(NC):
                    ins = dve.bn_stats(fst[p][:, c, :], fin[p][:, c, :])
                link(ins, apart=True)
                for c in range(NC):
                    ins = dve.bn_aggr(fmv[p][:, c, :], fst[p][:, c, :])
                link(ins)
                dve.tensor_scalar(fve[p][:, :], fmv[p][:, :, 1], EPS, None, ALU.add).then_inc(fve_ready, 1)

            def minus_mean(s):
                dve.wait_ge(frs_ready, s.n + 1)
                dve.scalar_tensor_tensor(out=fnb[s.par][:, :], in0=fmv[s.par][:, :, 0], scalar=-1.0,
                                         in1=frs[s.par][:, :], op0=ALU.mult,
                                         op1=ALU.mult).then_inc(fnb_ready, 1)

            finish(Seq(0, 0))
            finish(Seq(0, 1))
            minus_mean(Seq(0, 0))
            with dve.Fori(0, SEQS // 2 - 1) as i:
                finish(Seq(i, 2))
                minus_mean(Seq(i, 1))
                finish(Seq(i, 3))
                minus_mean(Seq(i, 2))
            minus_mean(Seq(0, SEQS - 1))

        @block.gpsimd
        def _(pool):
            NCONST = [0]

            def step(ins):
                NCONST[0] += 1
                ins.then_inc(pool_const, 1)
                pool.wait_ge(pool_const, NCONST[0])

            step(pool.memset(ident[:, :], 0.0))
            step(pool.affine_select(out=ident[:, :], in_=ident[:, :], compare_op=ALU.not_equal, fill=1.0,
                                    base=0, pattern=[[-1, P]], channel_multiplier=1))
            step(pool.memset(upto[:, :], 0.0))
            step(pool.affine_select(out=upto[:, :], in_=upto[:, :], compare_op=ALU.is_gt, fill=1.0,
                                    base=0, pattern=[[-1, P]], channel_multiplier=1))
            step(pool.memset(after[:, :], 0.0))
            step(pool.affine_select(out=after[:, :], in_=after[:, :], compare_op=ALU.is_ge, fill=1.0,
                                    base=0, pattern=[[1, P]], channel_multiplier=-1))
            step(pool.memset(before_b[:, :], 0.0))
            step(pool.affine_select(out=before_b[:, :], in_=before_b[:, :], compare_op=ALU.is_ge, fill=1.0,
                                    base=0, pattern=[[-1, P]], channel_multiplier=1))
            step(pool.memset(pick3[:, :], 0.0))
            step(pool.affine_select(out=pick3[:, :], in_=pick3[:, :], compare_op=ALU.not_equal, fill=1.0,
                                    base=0, pattern=[[-1, 3]], channel_multiplier=1))
            step(pool.iota(iota8[:, :], pattern=[[1, E]], base=0, channel_multiplier=0,
                           allow_small_or_imprecise_dtypes=True))
            step(pool.iota(iota_tile[:, :], pattern=[[1, TILES]], base=0, channel_multiplier=0,
                           allow_small_or_imprecise_dtypes=True))
            step(pool.iota(token_id[:, :], pattern=[[P, NC]], base=0, channel_multiplier=1,
                           allow_small_or_imprecise_dtypes=True))
            step(pool.iota(region[:, :], pattern=[[REGION, E]], base=0, channel_multiplier=0,
                           allow_small_or_imprecise_dtypes=True))
            step(pool.iota(next_row[:, :], pattern=[[REGION, E]], base=0, channel_multiplier=0,
                           allow_small_or_imprecise_dtypes=True))
            step(pool.memset(pad_tile[:, :], 0.0))
            step(pool.iota(pad_tile[:, P:P + 1].bitcast(I32), pattern=[[0, 1]], base=2 * TOKENS,
                           channel_multiplier=1))
            pool.memset(decayed[:, :], 0.0).then_inc(const_ready, 1)

            def expand(n, c, par):
                wait(pool, diff_psum, n - 1)
                pool.tensor_tensor(lhsA[c % 2][:, :, :], after[:, :].unsqueeze(1).broadcast_to([P, H, P]),
                                   a[par][:, (c % NC) * H:(c % NC + 1) * H].unsqueeze(2).broadcast_to([P, H, P]),
                                   ALU.mult).then_inc(lhsA_ready, 1)

            def gate_y(s, c):
                n = NC * s.n + c
                pool.wait_ge(yv_ready, n + 1)
                pool.wait_ge(sz_ready, CC * (s.n + 1))
                wait(pool, out_psum, s.n)
                pool.tensor_tensor(gt[:, :, c * P:(c + 1) * P], yv[c % 2][:, :, :],
                                   sz[s.par][:, :, c * P:(c + 1) * P], ALU.mult).then_inc(g_ready, 1)

            def slot_pool(s, scan, project, route):
                q, r = s.plus(1), s.plus(-1)
                if route:
                    pool.wait_ge(ve_ready, r.n + 1)
                    pool.tensor_tensor(rstd[:, :], ve[:, :], neg_half[:, :], ALU.pow).then_inc(rstd_ready, 1)
                for c in range(NC):
                    n = NC * s.n + c
                    if scan and (c + 2 < NC or project):
                        if c + 2 >= NC:
                            pool.wait_ge(a_ready, q.n + 1)
                        expand(n + 2, c + 2, s.par if c + 2 < NC else q.par)
                    if scan and c + 1 < NC:
                        pool.wait_ge(Xdt_ready, n + 1)
                        wait(pool, state_psum, (NC - 1) * s.n + c - 1)
                        pool.tensor_tensor(heads(Xdd[c % 2][:, :]), heads(Xdt[c % 2][:, :]),
                                           per_head(decays[s.par][:, 1, :], c), ALU.mult).then_inc(Xdd_ready, 1)
                    if scan and 0 < c < NC - 1:
                        pool.wait_ge(state_ready, (NC - 1) * s.n + c)
                        pool.tensor_tensor(heads(decayed[:, :]), heads(state[(c - 1) % 2][:, :]),
                                           per_head(decays[s.par][:, 2, :], c), ALU.mult).then_inc(decayed_ready, 1)
                    if scan and c > 0:
                        gate_y(s, c - 1)
                if project and not scan:
                    pool.wait_ge(a_ready, 1)
                    expand(0, 0, 0)
                    expand(1, 1, 0)
                if scan:
                    gate_y(s, NC - 1)
                    pool.wait_ge(ms_ready, s.n + 1)
                    if not (isinstance(s.n, int) and s.n < 1):
                        pool.wait_ge(x1_ready, NC * s.n)
                    pool.tensor_tensor(rms[:, :], ms[:, :], neg_half[:, :], ALU.pow).then_inc(rms_ready, 1)
                if route:
                    wait_apart(pool, slot_ready, r.n + 1)
                    for k, row in enumerate((rowA, rowB)):
                        for c in range(NC):
                            pool.indirect_dma_start(
                                out=sorted_rows[:, :],
                                out_offset=bass.IndirectOffsetOnAxis(slot[r.par][:, c, k:k + 1], 0),
                                in_=row[r.par][:, c, :], in_offset=None).then_inc(scattered[r.par], 16)

            slots(pool, slot_pool)

            def store(j, k):
                wait_apart(pool, ye_ready, j + 1)
                pool.indirect_dma_start(
                    out=moe_rows[:, :], out_offset=bass.IndirectOffsetOnAxis(xs[k][:, P:P + 1].bitcast(I32), 0),
                    in_=ye[k % 4], in_offset=None, bounds_check=2 * TOKENS - 1,
                    oob_is_err=False).then_inc(rows_out[k], 16)

            with pool.Fori(0, TILES // RING) as i:
                for k in range(RING):
                    store(RING * i + k, k)

            def finish(s):
                pool.wait_ge(fve_ready, s.n + 1)
                if not (isinstance(s.n, int) and s.n < 2):
                    pool.wait_ge(fout_ready, NC * (s.n - 1))
                pool.tensor_tensor(frs[s.par][:, :], fve[s.par][:, :], neg_half[:, :],
                                   ALU.pow).then_inc(frs_ready, 1)

            finish(Seq(0, 0))
            finish(Seq(0, 1))
            with pool.Fori(0, SEQS // 2 - 1) as i:
                finish(Seq(i, 2))
                finish(Seq(i, 3))


def kernel(L0_attn_x, L0_attn_Win, L0_attn_conv_w, L0_attn_conv_b, L0_attn_dt_bias, L0_attn_A_log,
           L0_attn_D, L0_attn_norm_w, L0_attn_Wout, L0_ffn_centroids, L0_ffn_W1, L0_ffn_b1, L0_ffn_W2,
           L0_ffn_b2):
    import numpy as np
    import concourse.bacc as bacc
    from concourse.bass_utils import run_bass_kernel_spmd

    def arr(x):
        return np.ascontiguousarray(x)

    win = np.asarray(L0_attn_Win).T
    arrays = dict(
        x=arr(L0_attn_x),
        w_z=arr(win[:, 0:DI]),
        w_xbc=arr(win[:, DI:DI + XC * P]),
        w_dt=arr(win[:, DI + XC * P:]),
        w_gate=arr(np.asarray(L0_ffn_centroids).T),
        w_out=arr(np.asarray(L0_attn_Wout).T.reshape(CC, P, P).transpose(1, 0, 2)),
        conv_w=arr(np.asarray(L0_attn_conv_w).reshape(XC, P, TAPS).transpose(1, 0, 2)),
        conv_b=arr(np.asarray(L0_attn_conv_b).reshape(XC, P).T),
        skip=arr(np.repeat(np.asarray(L0_attn_D), HD).reshape(CC, P).T),
        norm_w=arr(np.asarray(L0_attn_norm_w).reshape(CC, P).T),
        dt_bias=arr(np.broadcast_to(np.asarray(L0_attn_dt_bias), (P, H))),
        A_log=arr(np.broadcast_to(np.asarray(L0_attn_A_log), (P, H))),
        w1=arr(np.asarray(L0_ffn_W1).transpose(1, 0, 2)),
        b1=arr(np.asarray(L0_ffn_b1).reshape(E * FB, P).T),
        w2=arr(np.asarray(L0_ffn_W2).reshape(E, FB, P, P).transpose(2, 0, 1, 3)),
        b2=arr(np.broadcast_to(np.asarray(L0_ffn_b2).reshape(1, E * P), (3, E * P))),
    )
    nc = bacc.Bacc("TRN2", target_bir_lowering=False, num_devices=1)
    t = {n: nc.dram_tensor(f"in_{n}", a.shape, mybir.dt.from_np(a.dtype), kind="ExternalInput").ap()
         for n, a in arrays.items()}
    out = nc.dram_tensor("out_0", [SEQS, TOKS, P], F32, kind="ExternalOutput").ap()
    build(nc, t, out)
    got = run_bass_kernel_spmd(nc, [{f"in_{n}": a for n, a in arrays.items()}], core_ids=[0])
    return got.results[0]["out_0"]
```

```python
from contextlib import ExitStack

import concourse.bass as bass
from concourse import mybir
from concourse.alu_op_type import AluOpType as ALU

F32 = mybir.dt.float32
BF16 = mybir.dt.bfloat16
I32 = mybir.dt.int32
U32 = mybir.dt.uint32
ACT = mybir.ActivationFunctionType
AX_X = mybir.AxisListType.X

P = 128
SEQS, TOKS = 16, 512
NC = TOKS // P
H, HD = 4, 64
DI = H * HD
CC = DI // P
XC = CC + 2
TAPS = 4
E, FF = 8, 512
FB = FF // P
EPS = 1e-5
PADN = 96
TOKENS = SEQS * TOKS
ROW = P + 2
REGION = TOKENS + P
TILES = 2 * TOKENS // P + E
SPARE = E * REGION
LOG_TERMS = (13, 11, 9, 7, 5, 3)
SP_STEPS = 13
LN_STEPS = 2
GATE_STEPS = 6
POS_STEPS = 4
FIN_STEPS = 4


class Seq:

    def __init__(self, half, off):
        self.half, self.off = half, off
        self.n = 2 * half + off
        self.par = off % 2
        self.use = half + off // 2

    def plus(self, d):
        return Seq(self.half, self.off + d)


def wait(eng, sem, value):
    if not isinstance(value, int) or value > 0:
        eng.wait_ge(sem, value)


def build(nc, t, out):
    ctx = ExitStack()
    with ctx:
        def sb(name, shape, dt=F32):
            return ctx.enter_context(nc.sbuf_tensor(name, shape, dt))

        def bank(name):
            return ctx.enter_context(nc.psum_tensor(name, [P, 512], F32))

        def sem(name):
            return ctx.enter_context(nc.semaphore(name))

        sorted_rows = nc.dram_tensor("sorted_rows", [SPARE + E * P, ROW], F32, kind="Internal").ap()
        moe_rows = nc.dram_tensor("moe_rows", [2 * TOKENS, P], F32, kind="Internal").ap()

        w_z = sb("w_z", [P, DI])
        w_xbc = sb("w_xbc", [P, XC * P])
        w_dt = sb("w_dt", [P, PADN])
        w_gate = sb("w_gate", [P, PADN])
        w_out = sb("w_out", [P, CC, P])
        conv_w = sb("conv_w_sb", [P, XC, TAPS])
        conv_b = sb("conv_b_sb", [P, XC])
        skip = sb("skip", [P, CC])
        norm_w = sb("norm_w_sb", [P, CC])
        dt_bias = sb("dt_bias_sb", [P, H])
        neg_a = sb("neg_a", [P, H])
        w1 = sb("w1", [P, E, FF])
        w2 = sb("w2", [P, E, FB, P])
        b1 = sb("b1_sb", [P, E * FB])
        b2 = sb("b2_sb", [3, E * P], BF16)
        pick3 = sb("pick3", [3, 3])
        ones3 = sb("ones3", [3, P], BF16)
        ident = sb("ident", [P, P])
        upto = sb("upto", [P, P])
        after = sb("after", [P, P])
        before_b = sb("before_b", [P, P], BF16)
        ones = sb("ones", [P, P])
        ones_b = sb("ones_b", [P, P], BF16)
        neg_half = sb("neg_half", [P, NC])
        iota8 = sb("iota8", [P, E])
        iota_tile = sb("iota_tile", [P, TILES])
        token_id = sb("token_id", [P, NC])
        region = sb("region", [P, E])
        next_row = sb("next_row", [P, E])
        pad_tile = sb("pad_tile", [P, ROW])

        xa = [sb(f"xa{i}", [P, NC, P]) for i in range(2)]
        xres = [sb(f"xres{i}", [P, NC, P]) for i in range(2)]
        xT = [sb(f"xT{i}", [P, TOKS]) for i in range(2)]
        acc = sb("acc", [P, XC, TOKS])
        xc = [sb(f"xc{i}", [P, XC, TOKS]) for i in range(2)]
        sz = [sb(f"sz{i}", [P, CC, TOKS]) for i in range(2)]
        xD = [sb(f"xD{i}", [P, CC, TOKS]) for i in range(2)]
        v = sb("v", [P, NC, H])
        vabs = sb("vabs", [P, NC * H])
        ev = sb("ev", [P, NC * H])
        sp = [sb(f"sp{i}", [P, NC * H]) for i in range(5)]
        dtp = [sb(f"dtp{i}", [P, NC * H]) for i in range(2)]
        a = [sb(f"a{i}", [P, PADN]) for i in range(2)]
        decays = [sb(f"decays{i}", [P, 3, NC * H]) for i in range(2)]
        lhsA = [sb(f"lhsA{i}", [P, H, P]) for i in range(2)]
        L = [sb(f"L{i}", [P, H, P]) for i in range(2)]
        Gm = sb("Gm", [P, NC, P])
        M = [sb(f"M{i}", [P, H, P]) for i in range(2)]
        Xdt = [sb(f"Xdt{i}", [P, DI]) for i in range(2)]
        Xdd = [sb(f"Xdd{i}", [P, DI]) for i in range(2)]
        Btok = [sb(f"Btok{i}", [P, P]) for i in range(2)]
        state = [sb(f"state{i}", [P, DI]) for i in range(2)]
        decayed = sb("decayed", [P, DI])
        carried = sb("carried", [P, DI])
        yv = [sb(f"yv{i}", [P, CC, P]) for i in range(2)]
        ysq = sb("ysq", [P, CC, TOKS])
        gt = sb("gt", [P, CC, TOKS])
        ms = sb("ms", [P, NC])
        rms = sb("rms", [P, NC])
        st = sb("st", [P, NC, 6])
        mv = sb("mv", [P, NC, 2])
        ve = sb("ve", [P, NC])
        rstd = sb("rstd", [P, NC])
        shift = sb("shift", [P, NC])
        rowA = [sb(f"rowA{i}", [P, NC, ROW]) for i in range(2)]
        rowB = [sb(f"rowB{i}", [P, NC, ROW]) for i in range(2)]
        u_all = sb("u_all", [P, SEQS * NC, P])
        b2f, b2r, b2s = (u_all[0:3, E * k:E * (k + 1), :].rearrange("p e d -> p (e d)") for k in range(3))
        b2p = u_all[0:3, 3 * E:5 * E, :].rearrange("p e d -> p (e d)").bitcast(BF16)
        b2p = b2p[:, 0:3 * E * P].rearrange("p (k n) -> p k n", k=3)
        uT = sb("uT", [P, TOKS])
        eg = sb("eg", [P, NC, E])
        gates = sb("gates", [P, NC, E])
        top = sb("top", [P, NC, 8])
        topi = sb("topi", [P, NC, 8], U32)
        topf = sb("topf", [P, NC, 2])
        picks = sb("picks", [P, NC, 2, E])
        chosen = sb("chosen", [P, NC, E], BF16)
        gsum = sb("gsum", [P, NC])
        rows = sb("rows", [P, NC, E])
        prow = sb("prow", [P, NC, 2, E])
        slotf = sb("slotf", [P, NC, 2])
        slot = [sb(f"slot{i}", [P, NC, 2], I32) for i in range(2)]

        tb = sb("tb", [P, 8, E])
        tbi = sb("tbi", [P, E], I32)
        tcmp = sb("tcmp", [1, TILES, E])
        tval = sb("tval", [1, 4, TILES])
        table = sb("table", [1, 2, TILES], I32)
        pad_at = sb("pad_at", [P, E], I32)

        RING = 8
        xs = [sb(f"xs{i}", [P, ROW]) for i in range(RING)]
        sT = Btok
        w1e = [M[i][:, :, :].rearrange("p h s -> p (h s)") for i in range(2)]
        hT = L
        ye = [yv[i // 2][:, i % 2, :] for i in range(4)]

        yy = [acc[:, 2 * i:2 * i + 2, :].rearrange("p k (c d) -> p k c d", c=NC) for i in range(2)]
        fin = [xc[i][:, 0, :].rearrange("p (c d) -> p c d", c=NC) for i in range(2)]
        fout = [xc[i][:, 1, :].rearrange("p (c d) -> p c d", c=NC) for i in range(2)]
        fst = [sb(f"fst{i}", [P, NC, 6]) for i in range(2)]
        fmv = [sb(f"fmv{i}", [P, NC, 2]) for i in range(2)]
        fve = [sb(f"fve{i}", [P, NC]) for i in range(2)]
        frs = [sb(f"frs{i}", [P, NC]) for i in range(2)]
        fnb = [sb(f"fnb{i}", [P, NC]) for i in range(2)]

        pj = [bank(f"pj{i}") for i in range(2)]
        pl = [bank(f"pl{i}") for i in range(2)]
        p4 = bank("p4")
        p5 = bank("p5")
        p6 = bank("p6")
        p7 = bank("p7")

        w_in = sem("w_in")
        moe_w_in = sem("moe_w_in")
        const_ready = sem("const_ready")
        const_step = sem("const_step")
        pool_const = sem("pool_const")
        xa_in = [sem(f"xa_in{i}") for i in range(2)]
        xres_in = [sem(f"xres_in{i}") for i in range(2)]
        names_pe = ("xT_psum", "dt_psum", "proj_psum", "z_psum", "sums_psum", "diff_psum", "G_psum",
                    "tr_psum", "off_psum", "y_psum", "state_psum", "ss_psum", "out_psum", "uT_psum",
                    "logit_psum", "rank_psum")
        (xT_psum, dt_psum, proj_psum, z_psum, sums_psum, diff_psum, G_psum, tr_psum, off_psum, y_psum,
         state_psum, ss_psum, out_psum, uT_psum, logit_psum, rank_psum) = [sem(n) for n in names_pe]
        names_act = ("xT_ready", "abs_done", "ev_ready", "L_ready", "tap0_done", "Btok_ready", "sq_done",
                     "uT_ready", "rowB_ready", "eg_ready", "decays_ready", "xc_ready", "sz_ready",
                     "xD_ready")
        (xT_ready, abs_done, ev_ready, L_ready, tap0_done, Btok_ready, sq_done, uT_ready, rowB_ready,
         eg_ready, decays_ready, xc_ready, sz_ready, xD_ready) = [sem(n) for n in names_act]
        names_dve = ("x1_ready", "Gm_ready", "M_ready", "Xdt_ready", "v_ready", "yv_ready", "state_ready",
                     "sp_step", "a_ready", "tap_done", "conv_done", "carried_ready", "ln_step", "ve_ready", "shift_ready",
                     "u_ready", "gate_step", "chosen_ready", "ms_ready", "pos_step", "rank_read",
                     "slot_ready")
        (x1_ready, Gm_ready, M_ready, Xdt_ready, v_ready, yv_ready, state_ready, sp_step, a_ready,
         tap_done, conv_done, carried_ready, ln_step, ve_ready, shift_ready, u_ready, gate_step, chosen_ready,
         ms_ready, pos_step, rank_read, slot_ready) = [sem(n) for n in names_dve]
        names_pool = ("lhsA_ready", "Xdd_ready", "decayed_ready", "g_ready", "rms_ready", "rstd_ready")
        (lhsA_ready, Xdd_ready, decayed_ready, g_ready, rms_ready, rstd_ready) = [sem(n) for n in names_pool]
        scattered = [[sem(f"scattered_{'AB'[k]}{i}") for k in range(2)] for i in range(2)]
        u_kept = [sem(f"u_kept{i}") for i in range(2)]
        table_step = sem("table_step")
        table_ready = sem("table_ready")
        spare_in = sem("spare_in")
        pads_in = sem("pads_in")
        xs_in = [sem(f"xs_in{i}") for i in range(RING)]
        rows_out = [sem(f"rows_out{i}") for i in range(RING)]
        names_b = ("sT_psum", "sT_ready", "w1e_ready", "h_psum", "hT_ready", "ye_psum", "ye_ready")
        (sT_psum, sT_ready, w1e_ready, h_psum, hT_ready, ye_psum, ye_ready) = [sem(n) for n in names_b]
        yy_in = [sem(f"yy_in{i}") for i in range(2)]
        fin_out = [sem(f"fin_out{i}") for i in range(2)]
        (fin_step, fve_ready, frs_ready, fnb_ready, fout_ready) = [
            sem(n) for n in ("fin_step", "fve_ready", "frs_ready", "fnb_ready", "fout_ready")]

        CONSTS = 9

        def wait_apart(eng, sem, value):
            if not isinstance(value, int):
                value = eng.to_reg(value)
            eng.wait_ge(const_ready, CONSTS)
            eng.wait_ge(sem, value)

        block = ctx.enter_context(nc.Block())

        x_seq = t["x"].rearrange("b (c p) d -> b p c d", p=P)
        out_seq = out.rearrange("b (c p) d -> b p c d", p=P)
        moe_seq = moe_rows.rearrange("(k b c p) d -> b p k c d", k=2, b=SEQS, p=P)

        def tokens(ap, n=H):
            return ap.rearrange("p (c h) -> p c h", h=n)

        def per_head(ap, c):
            return ap[:, c * H:(c + 1) * H].unsqueeze(2).broadcast_to([P, H, HD])

        def heads(ap):
            return ap.rearrange("p (h d) -> p h d", h=H)

        def is_last(s, k):
            return isinstance(s.n, int) and s.n > SEQS - 1 - k

        def slots(eng, slot_fn):
            slot_fn(Seq(0, -1), False, True, False)
            slot_fn(Seq(0, 0), True, True, False)
            slot_fn(Seq(0, 1), True, True, True)
            slot_fn(Seq(0, 2), True, True, True)
            with eng.Fori(1, (SEQS - 4) // 2) as i:
                slot_fn(Seq(i, 1), True, True, True)
                slot_fn(Seq(i, 2), True, True, True)
            slot_fn(Seq(0, SEQS - 3), True, True, True)
            slot_fn(Seq(0, SEQS - 2), True, True, True)
            slot_fn(Seq(0, SEQS - 1), True, False, True)
            slot_fn(Seq(0, SEQS), False, False, True)

        @block.sync
        def _(dq):
            dq.dma_start(xa[0][:, :, :], x_seq[0]).then_inc(xa_in[0], 16)
            for dst, name in ((w_xbc[:, :], "w_xbc"), (w_dt[:, 0:H], "w_dt"), (w_z[:, :], "w_z"),
                              (w_gate[:, 0:E], "w_gate"),
                              (w_out[:, :, :], "w_out"), (conv_w[:, :, :], "conv_w"),
                              (conv_b[:, :], "conv_b"), (skip[:, :], "skip"), (norm_w[:, :], "norm_w"),
                              (dt_bias[:, :], "dt_bias"), (neg_a[:, :], "A_log"), (b1[:, :], "b1"),
                              (b2f, "b2")):
                if name in ("w_dt", "w_gate"):
                    dq.wait_ge(const_ready, CONSTS)
                dq.dma_start(dst, t[name]).then_inc(w_in, 16)

            def slot_dma(s, scan, project, route):
                if project and not (isinstance(s.n, int) and s.n >= SEQS - 2):
                    q = s.plus(2)
                    wait(dq, xT_psum, q.n - 1)
                    dq.dma_start(xa[q.par][:, :, :], x_seq[q.n]).then_inc(xa_in[q.par], 16)
                if project:
                    q = s.plus(1)
                    wait(dq, x1_ready, NC * (q.n - 1))
                    dq.dma_start(xres[q.par][:, :, :], x_seq[q.n]).then_inc(xres_in[q.par], 16)
                if route:
                    r = s.plus(-1)
                    dq.wait_ge(u_ready, NC * (r.n + 1))
                    dq.dma_start(u_all[:, bass.ds(r.n * NC, NC), :],
                                 rowA[r.par][:, :, 0:P]).then_inc(u_kept[r.par], 16)

            slot_dma(Seq(0, -1), False, True, False)
            dq.dma_start(w1[:, :, :], t["w1"]).then_inc(moe_w_in, 16)
            slot_dma(Seq(0, 0), True, True, False)
            dq.dma_start(w2[:, :, :, :], t["w2"]).then_inc(moe_w_in, 16)
            for k in range(E):
                dq.dma_start(sorted_rows[SPARE + k * P:SPARE + (k + 1) * P, :],
                             pad_tile[:, :]).then_inc(spare_in, 16)
            slot_dma(Seq(0, 1), True, True, True)
            slot_dma(Seq(0, 2), True, True, True)
            with dq.Fori(1, (SEQS - 4) // 2) as i:
                slot_dma(Seq(i, 1), True, True, True)
                slot_dma(Seq(i, 2), True, True, True)
            slot_dma(Seq(0, SEQS - 3), True, True, True)
            slot_dma(Seq(0, SEQS - 2), True, True, True)
            slot_dma(Seq(0, SEQS - 1), True, False, True)
            slot_dma(Seq(0, SEQS), False, False, True)

            dq.wait_ge(table_ready, 1)
            for k in range(E):
                at = dq.value_load(pad_at[0:1, k:k + 1], min_val=k * REGION,
                                   max_val=k * REGION + TOKENS)
                dq.dma_start(sorted_rows[bass.ds(at, P), :], pad_tile[:, :]).then_inc(pads_in, 16)
            dq.wait_ge(pads_in, 16 * E)
            dq.wait_ge(spare_in, 16 * E)
            for i in range(2):
                for k in range(2):
                    dq.wait_ge(scattered[i][k], 16 * NC * SEQS // 2)

            def load_rows(tile, k, turn):
                wait(dq, rows_out[k], 16 * turn)
                at = dq.value_load(table[0:1, 0, bass.ds(tile, 1)], min_val=0, max_val=SPARE + (E - 1) * P)
                dq.dma_start(xs[k][:, :], sorted_rows[bass.ds(at, P), :]).then_inc(xs_in[k], 16)

            for k in range(RING):
                load_rows(k, k, 0)
            with dq.Fori(1, TILES // RING) as i:
                for k in range(RING):
                    load_rows(RING * i + k, k, i)

            for k in range(RING):
                dq.wait_ge(rows_out[k], 16 * TILES // RING)

            def load_moe(s):
                wait(dq, fin_step, FIN_STEPS * (s.n - 1))
                for k in range(2):
                    dq.dma_start(yy[s.par][:, k], moe_seq[s.n, :, k]).then_inc(yy_in[s.par], 16)

            load_moe(Seq(0, 0))
            load_moe(Seq(0, 1))
            with dq.Fori(0, SEQS // 2 - 1) as i:
                load_moe(Seq(i, 2))
                load_moe(Seq(i, 3))
            for i in range(2):
                dq.wait_ge(fin_out[i], 16 * SEQS // 2)

        @block.tensor
        def _(pe):
            pe.wait_ge(const_ready, CONSTS)

            def project_block(q, k):
                if k == 0:
                    pe.wait_ge(xT_ready, q.n + 1)
                    wait(pe, sz_ready, CC * (q.n - 1) + 1)
                elif k == 1:
                    pe.wait_ge(v_ready, q.n + 1)
                else:
                    pe.wait_ge(conv_done, XC * q.n + k - 1)
                pe.matmul(pj[k % 2][:, :], w_xbc[:, k * P:(k + 1) * P], xT[q.par][:, :],
                          start=True, stop=True).then_inc(proj_psum, 1)

            def z_block(q, k):
                pe.wait_ge(xT_ready, q.n + 1)
                if k > 0:
                    wait(pe, carried_ready, (NC - 1) * q.n)
                elif is_last(q, 1):
                    pe.wait_ge(conv_done, XC * q.n + 3)
                else:
                    pe.wait_ge(xT_ready, q.n + 2)
                pe.matmul((pj[0], p6)[k][:, :], w_z[:, k * P:(k + 1) * P], xT[q.par][:, :],
                          start=True, stop=True).then_inc(z_psum, 1)

            def exponents(n, c):
                pe.wait_ge(lhsA_ready, n + 1)
                wait(pe, L_ready, n - 1)
                for h in range(H):
                    mm = pe.matmul(pl[c % 2][:, h * P:(h + 1) * P], lhsA[c % 2][:, h, :], upto[:, :],
                                   start=True, stop=True)
                mm.then_inc(diff_psum, 1)

            def enter_x(q, convolved):
                pe.wait_ge(xa_in[q.par], 16 * (q.use + 1))
                wait(pe, conv_done, convolved)
                for c in range(NC):
                    mm = pe.transpose(pj[0][:, c * P:(c + 1) * P], xa[q.par][:, c, :], ident[:, :])
                mm.then_inc(xT_psum, 1)

            def enter_dt(q, convolved):
                pe.wait_ge(xT_ready, q.n + 1)
                wait(pe, conv_done, convolved)
                for c in range(NC):
                    mm = pe.matmul(pj[1][:, c * PADN:(c + 1) * PADN], xT[q.par][:, c * P:(c + 1) * P],
                                   w_dt[:, :], start=True, stop=True)
                mm.then_inc(dt_psum, 1)

            def slot_pe(s, scan, project, route):
                q, r, nxt = s.plus(1), s.plus(-1), s.plus(2)
                if not scan and project:
                    enter_x(q, 0)
                    pe.wait_ge(w_in, 16 * 13)
                    enter_dt(q, 0)
                if scan:
                    pe.wait_ge(xc_ready, XC * (s.n + 1))
                    wait(pe, ms_ready, s.n)
                    for c in range(NC):
                        tok = slice(c * P, (c + 1) * P)
                        mm = pe.matmul(p7[:, tok], xc[s.par][:, CC, tok], xc[s.par][:, CC + 1, tok],
                                       start=True, stop=True)
                    mm.then_inc(G_psum, 1)
                for c in range(NC):
                    tok = slice(c * P, (c + 1) * P)
                    n = NC * s.n + c
                    if scan and (c + 1 < NC or project):
                        exponents(n + 1, c + 1)
                    if scan:
                        pe.wait_ge(Xdt_ready, n) if not isinstance(n, int) or n > 0 else None
                        wait(pe, Btok_ready, (NC - 1) * s.n + c)
                        if c == 0:
                            wait(pe, x1_ready, NC * s.n)
                        for k in range(CC):
                            mm = pe.transpose(p5[:, k * P:(k + 1) * P], xc[s.par][:, k, tok], ident[:, :])
                        if c + 1 < NC:
                            mm = pe.transpose(p5[:, CC * P:(CC + 1) * P], xc[s.par][:, CC, tok], ident[:, :])
                        mm.then_inc(tr_psum, 1)
                        if c > 0:
                            pe.wait_ge(state_ready, (NC - 1) * s.n + c)
                            pe.matmul(p6[:, 0:DI], xc[s.par][:, CC + 1, tok], state[(c - 1) % 2][:, :],
                                      start=True, stop=True).then_inc(off_psum, 1)
                    if project:
                        project_block(q, c)
                    if scan:
                        pe.wait_ge(M_ready, n + 1)
                        pe.wait_ge(Xdt_ready, n + 1)
                        if c > 0:
                            pe.wait_ge(yv_ready, n)
                        for h in range(H):
                            half = slice((h % 2) * HD, (h % 2 + 1) * HD)
                            mm = pe.matmul(p7[half, (h // 2) * P:(h // 2 + 1) * P],
                                           Xdt[c % 2][:, h * HD:(h + 1) * HD], M[c % 2][:, h, :],
                                           start=(h < 2), stop=(c == 0), skip_group_check=True)
                        if c > 0:
                            pe.wait_ge(carried_ready, (NC - 1) * s.n + c)
                            for k in range(CC):
                                mm = pe.matmul(p7[:, k * P:(k + 1) * P], carried[:, k * P:(k + 1) * P],
                                               ident[:, :], start=False, stop=True, skip_group_check=True)
                        mm.then_inc(y_psum, 1)
                        if c + 1 < NC:
                            pe.wait_ge(Btok_ready, (NC - 1) * s.n + c + 1)
                            pe.wait_ge(Xdd_ready, (NC - 1) * s.n + c + 1)
                            if c == 0:
                                pe.wait_ge(sz_ready, CC * (s.n + 1))
                            pe.matmul(p6[:, DI:2 * DI], Btok[c % 2][:, :], Xdd[c % 2][:, :],
                                      start=True, stop=True).then_inc(state_psum, 1)
                    if route and c == 1:
                        pe.wait_ge(u_ready, NC * (r.n + 1))
                        wait(pe, rank_read, r.n)
                        if scan:
                            pe.wait_ge(decays_ready, s.n + 1)
                        for k in range(NC):
                            mm = pe.transpose(p4[:, k * P:(k + 1) * P], rowA[r.par][:, k, 0:P], ident[:, :])
                        mm.then_inc(uT_psum, 1)
                    if route and c == 2:
                        pe.wait_ge(uT_ready, r.n + 1)
                        for k in range(NC):
                            mm = pe.matmul(p4[:, k * PADN:(k + 1) * PADN], uT[:, k * P:(k + 1) * P],
                                           w_gate[:, :], start=True, stop=True)
                        mm.then_inc(logit_psum, 1)
                if project and not is_last(s, 2):
                    enter_x(nxt, XC * q.n + 3)
                if project:
                    pe.wait_ge(a_ready, q.n + 1)
                    if route:
                        pe.wait_ge(eg_ready, r.n + 1)
                    for k, mask in enumerate((upto, after, ones)):
                        mm = pe.matmul(p4[:, k * PADN:(k + 1) * PADN], mask[:, :], a[q.par][:, :],
                                       start=True, stop=True)
                    mm.then_inc(sums_psum, 1)
                if scan:
                    pe.wait_ge(sq_done, NC * (s.n + 1))
                    pe.wait_ge(yv_ready, NC * (s.n + 1))
                    for c in range(NC):
                        for k in range(CC):
                            mm = pe.matmul(p7[:, c * PADN:(c + 1) * PADN], ysq[:, k, c * P:(c + 1) * P],
                                           ones[:, 0:PADN], start=(k == 0), stop=(k == CC - 1))
                    mm.then_inc(ss_psum, 1)
                if scan:
                    pe.wait_ge(g_ready, NC * (s.n + 1))
                    pe.wait_ge(Xdt_ready, NC * (s.n + 1))
                    for c in range(NC):
                        for k in range(CC):
                            mm = pe.matmul(p5[:, c * P:(c + 1) * P], gt[:, k, c * P:(c + 1) * P],
                                           w_out[:, k, :], start=(k == 0), stop=(k == CC - 1))
                    mm.then_inc(out_psum, 1)
                if project:
                    z_block(q, 0)
                    z_block(q, 1)
                if project and not is_last(s, 2):
                    enter_dt(nxt, XC * q.n + XC)
                if route:
                    pe.wait_ge(chosen_ready, r.n + 1)
                    if project:
                        pe.wait_ge(decays_ready, q.n + 1)
                    else:
                        pe.wait_ge(eg_ready, r.n + 1)
                    for c in range(NC + 1):
                        for k in range(c):
                            mm = pe.matmul(p4[:, c * E:(c + 1) * E], ones_b[:, :], chosen[:, k, :],
                                           start=(k == 0), stop=(k == NC - 1))
                        if c < NC:
                            mm = pe.matmul(p4[:, c * E:(c + 1) * E], before_b[:, :], chosen[:, c, :],
                                           start=(c == 0), stop=True)
                    mm.then_inc(rank_psum, 1)
                if project and not scan:
                    exponents(0, 0)

            slots(pe, slot_pe)

            pe.wait_ge(rank_read, SEQS)
            pe.wait_ge(table_ready, 1)
            pe.wait_ge(moe_w_in, 32)

            def transpose_rows(j, k, turn):
                pe.wait_ge(xs_in[k], 16 * (turn + 1))
                wait(pe, sT_ready, j - 1)
                pe.transpose(pj[k % 2][:, 0:P], xs[k][:, 0:P], ident[:, :]).then_inc(sT_psum, 1)

            def up(j, k):
                pe.wait_ge(sT_ready, j + 1)
                pe.wait_ge(w1e_ready, j + 1)
                wait(pe, hT_ready, FB * (j - 1))
                for f in range(FB):
                    mm = pe.matmul(pl[k % 2][:, f * P:(f + 1) * P], w1e[k % 2][:, f * P:(f + 1) * P],
                                   sT[k % 2][:, :], start=True, stop=True)
                mm.then_inc(h_psum, 1)

            def down(j, k):
                e = pe.value_load(table[0:1, 1, bass.ds(j, 1)], min_val=0, max_val=E - 1)
                pe.wait_ge(hT_ready, FB * (j + 1))
                wait(pe, ye_ready, j - 1)
                o = (p6, p7)[k % 2]
                pe.matmul(o[:, 0:P], ones3[:, :], b2[:, bass.ds(e * P, P)], start=True, stop=False)
                for f in range(FB):
                    mm = pe.matmul(o[:, 0:P], hT[k % 2][:, f, :], w2[:, bass.ds(e, 1), f, :].rearrange("p e d -> p (e d)"),
                                   start=False, stop=(f == FB - 1))
                mm.then_inc(ye_psum, 1)

            transpose_rows(0, 0, 0)
            transpose_rows(1, 1, 0)
            up(0, 0)
            def turn_pe(i):
                for k in range(RING):
                    j = RING * i + k
                    transpose_rows(j + 2, (k + 2) % RING, i + (k + 2) // RING)
                    up(j + 1, k + 1)
                    down(j, k)

            turn_pe(0)
            with pe.Fori(1, TILES // RING - 1) as i:
                turn_pe(i)
            for k in range(RING):
                j = TILES - RING + k
                if k + 2 < RING:
                    transpose_rows(j + 2, k + 2, TILES // RING - 1)
                if k + 1 < RING:
                    up(j + 1, k + 1)
                down(j, k)

        @block.scalar
        def _(act):
            act.wait_ge(w_in, 16 * 13)
            act.activation(neg_a[:, :], neg_a[:, :], ACT.Exp).then_inc(const_step, 1)

            def exp_exponents(n, c):
                act.wait_ge(diff_psum, n + 1)
                wait(act, M_ready, n - 1)
                act.activation(L[c % 2][:, :, :], pl[c % 2][:, :], ACT.Exp).then_inc(L_ready, 1)

            def enter(q):
                act.wait_ge(xT_psum, q.n + 1)
                wait(act, z_psum, CC * (q.n - 1))
                act.copy(xT[q.par][:, :], pj[0][:, :]).then_inc(xT_ready, 1)

            def square(s, c):
                act.wait_ge(yv_ready, NC * s.n + c + 1)
                wait(act, ss_psum, s.n)
                act.activation(ysq[:, :, c * P:(c + 1) * P], yv[c % 2][:, :, :],
                               ACT.Square).then_inc(sq_done, 1)

            def slot_act(s, scan, project, route):
                q, r = s.plus(1), s.plus(-1)
                if project and not scan:
                    enter(q)
                for c in range(NC):
                    n = NC * s.n + c
                    tok = slice(c * P, (c + 1) * P)
                    if scan and (c + 1 < NC or project):
                        exp_exponents(n + 1, c + 1)
                    if scan and c + 1 < NC:
                        act.wait_ge(tr_psum, n + 1)
                        wait(act, state_psum, (NC - 1) * s.n + c - 1)
                        act.copy(Btok[c % 2][:, :], p5[:, CC * P:(CC + 1) * P]).then_inc(Btok_ready, 1)
                    if project and c == 0:
                        act.wait_ge(v_ready, q.n + 1)
                        act.activation(vabs[:, :], v[:, :, :], ACT.Abs).then_inc(abs_done, 1)
                        act.wait_ge(abs_done, q.n + 1)
                        wait(act, a_ready, q.n)
                        act.activation(ev[:, :], vabs[:, :], ACT.Exp, scale=-1.0).then_inc(ev_ready, 1)
                    if project:
                        act.wait_ge(proj_psum, XC * q.n + c + 1)
                        wait(act, xc_ready, XC * (q.n - 1) + c + 1)
                        act.activation(acc[:, c, :], pj[c % 2][:, :], ACT.Identity,
                                       bias=conv_b[:, c:c + 1],
                                       scale=conv_w[:, c, TAPS - 1:TAPS]).then_inc(tap0_done, 1)
                    if route and c == 0:
                        act.wait_ge(shift_ready, r.n + 1)
                        act.wait_ge(rstd_ready, r.n + 1)
                        act.wait_ge(x1_ready, NC * (r.n + 1))
                        for k in range(NC):
                            act.activation(rowA[r.par][:, k, 0:P], rowA[r.par][:, k, 0:P], ACT.Identity,
                                           bias=shift[:, k:k + 1], scale=rstd[:, k:k + 1]).then_inc(u_ready, 1)
                    if scan and c > 0:
                        square(s, c - 1)
                    if route and c == 1:
                        act.wait_ge(u_ready, NC * (r.n + 1))
                        act.wait_ge(uT_psum, r.n + 1)
                        act.copy(uT[:, :], p4[:, :]).then_inc(uT_ready, 1)
                        if not (isinstance(r.n, int) and r.n < 2):
                            act.wait_ge(scattered[r.par][1], 16 * NC * r.use)
                        act.copy(rowB[r.par][:, :, 0:P], rowA[r.par][:, :, 0:P]).then_inc(rowB_ready, 1)
                    if route and c == 2:
                        act.wait_ge(logit_psum, r.n + 1)
                        act.activation(eg[:, :, :],
                                       p4[:, 0:NC * PADN].rearrange("p (c e) -> p c e", e=PADN)[:, :, 0:E],
                                       ACT.Exp, scale=-1.0).then_inc(eg_ready, 1)
                if scan:
                    square(s, NC - 1)
                if project and not is_last(s, 2):
                    enter(s.plus(2))
                if project:
                    act.wait_ge(sums_psum, q.n + 1)
                    act.activation(decays[q.par][:, :, :],
                                   p4[:, 0:3 * PADN].rearrange("p (k e) -> p k e", e=PADN)[:, :, 0:NC * H],
                                   ACT.Exp).then_inc(decays_ready, 1)
                    if not scan:
                        exp_exponents(0, 0)
                    for k in range(XC):
                        act.wait_ge(conv_done, XC * q.n + k + 1)
                        wait(act, y_psum, NC * (q.n - 1))
                        act.activation(xc[q.par][:, k, :], acc[:, k, :], ACT.Silu).then_inc(xc_ready, 1)
                    for k in range(CC):
                        act.wait_ge(z_psum, CC * q.n + k + 1)
                        wait(act, g_ready, NC * (q.n - 1))
                        act.activation(sz[q.par][:, k, :], (pj[0], p6)[k][:, :], ACT.Silu).then_inc(sz_ready, 1)
                    for k in range(CC):
                        act.wait_ge(xc_ready, XC * q.n + k + 1)
                        wait(act, yv_ready, NC * (q.n - 1))
                        act.activation(xD[q.par][:, k, :], xc[q.par][:, k, :], ACT.Identity,
                                       scale=skip[:, k:k + 1]).then_inc(xD_ready, 1)

            slots(act, slot_act)

            def gelu(j, k):
                e = act.value_load(table[0:1, 1, bass.ds(j, 1)], min_val=0, max_val=E - 1)
                act.wait_ge(h_psum, j + 1)
                wait(act, ye_psum, j - 1)
                for f in range(FB):
                    act.activation(hT[k % 2][:, f, :], pl[k % 2][:, f * P:(f + 1) * P], ACT.Gelu,
                                   bias=b1[:, bass.ds(e * FB + f, 1)]).then_inc(hT_ready, 1)

            act.wait_ge(table_ready, 1)
            for k in range(RING):
                gelu(k, k)
            with act.Fori(1, TILES // RING) as i:
                for k in range(RING):
                    gelu(RING * i + k, k)

            def finish(s):
                act.wait_ge(frs_ready, s.n + 1)
                act.wait_ge(fnb_ready, s.n + 1)
                if not (isinstance(s.n, int) and s.n < 2):
                    act.wait_ge(fin_out[s.par], 16 * s.use)
                for c in range(NC):
                    act.activation(fout[s.par][:, c, :], fin[s.par][:, c, :], ACT.Identity,
                                   bias=fnb[s.par][:, c:c + 1],
                                   scale=frs[s.par][:, c:c + 1]).then_inc(fout_ready, 1)
                act.wait_ge(fout_ready, NC * (s.n + 1))
                act.dma_start(out_seq[s.n], fout[s.par]).then_inc(fin_out[s.par], 16)

            finish(Seq(0, 0))
            finish(Seq(0, 1))
            with act.Fori(0, SEQS // 2 - 1) as i:
                finish(Seq(i, 2))
                finish(Seq(i, 3))

        @block.vector
        def _(dve):
            def chain(s, base):
                count = [base]

                def link(ins, apart=False):
                    count[0] = count[0] + 1
                    ins.then_inc(s, 1)
                    if apart:
                        wait_apart(dve, s, count[0])
                    else:
                        dve.wait_ge(s, count[0])
                return link

            link = chain(const_step, 1)
            dve.memset(w_dt[:, :], 0.0).then_inc(const_ready, 1)
            dve.memset(w_gate[:, :], 0.0).then_inc(const_ready, 1)
            dve.memset(a[0][:, :], 0.0).then_inc(const_ready, 1)
            dve.memset(a[1][:, :], 0.0).then_inc(const_ready, 1)
            dve.memset(ones[:, :], 1.0).then_inc(const_ready, 1)
            dve.memset(ones_b[:, :], 1.0).then_inc(const_ready, 1)
            dve.memset(ones3[:, :], 1.0).then_inc(const_ready, 1)
            dve.memset(neg_half[:, :], -0.5).then_inc(const_ready, 1)
            dve.wait_ge(w_in, 16 * 13)
            dve.wait_ge(const_step, 1)
            link(dve.tensor_scalar(neg_a[:, :], neg_a[:, :], -1.0, None, ALU.mult))
            for k in range(CC):
                link(dve.tensor_scalar(w_out[:, k, :], w_out[:, k, :], norm_w[:, k:k + 1], None, ALU.mult))
            dve.wait_ge(const_ready, CONSTS)
            link(dve.tensor_copy(b2p[:, 0, :], b2f))
            link(dve.tensor_tensor(b2r, b2f, b2p[:, 0, :], ALU.subtract))
            link(dve.tensor_copy(b2p[:, 1, :], b2r))
            link(dve.tensor_tensor(b2r, b2r, b2p[:, 1, :], ALU.subtract))
            link(dve.tensor_copy(b2p[:, 2, :], b2r))
            link(dve.tensor_scalar(b2s, b2p[:, 0, :], pick3[:, 0:1], None, ALU.mult))
            link(dve.scalar_tensor_tensor(out=b2s, in0=b2p[:, 1, :], scalar=pick3[:, 1:2],
                                          in1=b2s, op0=ALU.mult, op1=ALU.add))
            link(dve.scalar_tensor_tensor(out=b2[:, :], in0=b2p[:, 2, :], scalar=pick3[:, 2:3],
                                          in1=b2s, op0=ALU.mult, op1=ALU.add))

            def tap(q, k, j):
                done = (TAPS - 2) * (XC * q.n + k)
                if j == 1:
                    dve.wait_ge(tap0_done, XC * q.n + k + 1)
                else:
                    dve.wait_ge(tap_done, done + j - 1)
                ins = dve.scalar_tensor_tensor(
                    out=acc[:, k, j:TOKS], in0=pj[k % 2][:, 0:TOKS - j],
                    scalar=conv_w[:, k, TAPS - 1 - j:TAPS - j], in1=acc[:, k, j:TOKS],
                    op0=ALU.mult, op1=ALU.add)
                if j < TAPS - 1:
                    ins.then_inc(tap_done, 1)
                else:
                    ins.then_inc(conv_done, 1)

            def softplus_step(q, k):
                w, wsq, pp, t1, mx = (b[:, :] for b in sp)
                if k == 0:
                    dve.wait_ge(ev_ready, q.n + 1)
                else:
                    dve.wait_ge(sp_step, SP_STEPS * q.n + k)
                if k == 0:
                    ins = dve.tensor_scalar(t1, ev[:, :], 2.0, None, ALU.add)
                elif k == 1:
                    ins = dve.reciprocal(t1, t1)
                elif k == 2:
                    ins = dve.tensor_tensor(w, t1, ev[:, :], ALU.mult)
                elif k == 3:
                    ins = dve.tensor_tensor(wsq, w, w, ALU.mult)
                elif k == 4:
                    ins = dve.tensor_scalar(pp, wsq, 1.0 / LOG_TERMS[0], None, ALU.mult)
                elif k < 10:
                    ins = dve.scalar_tensor_tensor(out=pp, in0=pp, scalar=1.0 / LOG_TERMS[k - 4], in1=wsq,
                                                   op0=ALU.add, op1=ALU.mult)
                elif k == 10:
                    ins = dve.scalar_tensor_tensor(out=pp, in0=pp, scalar=1.0, in1=w, op0=ALU.add,
                                                   op1=ALU.mult)
                elif k == 11:
                    ins = dve.tensor_scalar(mx, v[:, :, :].rearrange("p c h -> p (c h)"), 0.0, None, ALU.max)
                elif k == 12:
                    if not (isinstance(q.n, int) and q.n < 2):
                        dve.wait_ge(Xdt_ready, NC * (q.n - 1))
                    ins = dve.scalar_tensor_tensor(out=dtp[q.par][:, :], in0=pp, scalar=2.0, in1=mx,
                                                   op0=ALU.mult, op1=ALU.add)
                else:
                    wait(dve, lhsA_ready, NC * (q.n - 1))
                    ins = dve.tensor_tensor(tokens(a[q.par][:, 0:NC * H]), tokens(dtp[q.par][:, :]),
                                            neg_a[:, :].unsqueeze(1).broadcast_to([P, NC, H]), ALU.mult)
                ins.then_inc(sp_step if k < SP_STEPS else a_ready, 1)

            def enter(q):
                dve.wait_ge(dt_psum, q.n + 1)
                wait(dve, a_ready, q.n)
                wait(dve, abs_done, q.n)
                dve.tensor_tensor(
                    v[:, :, :], pj[1][:, 0:NC * PADN].rearrange("p (c e) -> p c e", e=PADN)[:, :, 0:H],
                    dt_bias[:, :].unsqueeze(1).broadcast_to([P, NC, H]),
                    ALU.add).then_inc(v_ready, 1)

            def mask_chunk(s, c):
                n = NC * s.n + c
                dve.wait_ge(Gm_ready, s.n + 1)
                dve.wait_ge(L_ready, n + 1)
                wait(dve, y_psum, n - 1)
                dve.tensor_tensor(M[c % 2][:, :, :], L[c % 2][:, :, :],
                                  Gm[:, c, :].unsqueeze(1).broadcast_to([P, H, P]),
                                  ALU.mult).then_inc(M_ready, 1)

            def residual(s):
                dve.wait_ge(out_psum, s.n + 1)
                dve.wait_ge(rms_ready, s.n + 1)
                dve.wait_ge(xres_in[s.par], 16 * (s.use + 1))
                if not (isinstance(s.n, int) and s.n < 2):
                    dve.wait_ge(scattered[s.par][0], 16 * NC * s.use)
                    dve.wait_ge(u_kept[s.par], 16 * s.use)
                for c in range(NC):
                    dve.scalar_tensor_tensor(
                        out=rowA[s.par][:, c, 0:P], in0=p5[:, c * P:(c + 1) * P],
                        scalar=rms[:, c:c + 1], in1=xres[s.par][:, c, :],
                        op0=ALU.mult, op1=ALU.add).then_inc(x1_ready, 1)
                dve.wait_ge(x1_ready, NC * (s.n + 1))
                wait(dve, u_ready, NC * s.n)
                for k in range(NC):
                    ins = dve.bn_stats(st[:, k, :], rowA[s.par][:, k, 0:P])
                ins.then_inc(ln_step, 1)
                wait_apart(dve, ln_step, LN_STEPS * s.n + 1)
                for k in range(NC):
                    ins = dve.bn_aggr(mv[:, k, :], st[:, k, :])
                ins.then_inc(ln_step, 1)
                dve.wait_ge(ln_step, LN_STEPS * s.n + 2)
                dve.tensor_scalar(ve[:, :], mv[:, :, 1], EPS, None, ALU.add).then_inc(ve_ready, 1)

            def slot_dve(s, scan, project, route):
                q, r = s.plus(1), s.plus(-1)
                if project and not scan:
                    enter(q)
                if scan:
                    dve.wait_ge(G_psum, s.n + 1)
                    dve.tensor_tensor(Gm[:, :, :], p7[:, :].rearrange("p (c k) -> p c k", c=NC),
                                      upto[:, :].unsqueeze(1).broadcast_to([P, NC, P]),
                                      ALU.mult).then_inc(Gm_ready, 1)
                if scan:
                    mask_chunk(s, 0)
                if project and not scan:
                    for k in range(SP_STEPS + 1):
                        softplus_step(q, k)
                for c in range(NC):
                    n = NC * s.n + c

                    def spread(k):
                        if scan and project and 3 <= 7 * (c - 1) + k + 3 <= SP_STEPS:
                            softplus_step(q, 7 * (c - 1) + k + 3)

                    if project and c > 0:
                        tap(q, c - 1, 1)
                        spread(0)
                    if scan:
                        dve.wait_ge(tr_psum, n + 1)
                        if c + 1 < NC:
                            dve.wait_ge(Btok_ready, (NC - 1) * s.n + c + 1)
                        wait(dve, Xdd_ready, (NC - 1) * s.n + max(c - 1, 0))
                        dve.tensor_tensor(heads(Xdt[c % 2][:, :]), heads(p5[:, 0:DI]),
                                          per_head(dtp[s.par], c), ALU.mult).then_inc(Xdt_ready, 1)
                    if route and c == 0:
                        dve.wait_ge(rstd_ready, r.n + 1)
                        dve.scalar_tensor_tensor(out=shift[:, :], in0=mv[:, :, 0], scalar=-1.0,
                                                 in1=rstd[:, :], op0=ALU.mult,
                                                 op1=ALU.mult).then_inc(shift_ready, 1)
                    spread(1)
                    if scan and c > 0:
                        dve.wait_ge(off_psum, (NC - 1) * s.n + c)
                        dve.tensor_tensor(heads(carried[:, :]), heads(p6[:, 0:DI]),
                                          per_head(decays[s.par][:, 0, :], c),
                                          ALU.mult).then_inc(carried_ready, 1)
                    spread(2)
                    if scan and c + 1 < NC:
                        mask_chunk(s, c + 1)
                    spread(3)
                    if scan and project and c == 0:
                        softplus_step(q, 0)
                    if project and c > 0:
                        tap(q, c - 1, 2)
                    spread(4)
                    if project and c > 0:
                        tap(q, c - 1, 3)
                    if scan and project and c == 0:
                        softplus_step(q, 1)
                    spread(5)
                    if scan:
                        dve.wait_ge(y_psum, n + 1)
                        dve.wait_ge(xD_ready, CC * (s.n + 1))
                        wait(dve, sq_done, n - 1)
                        wait(dve, g_ready, n - 1)
                        dve.tensor_tensor(yv[c % 2][:, :, :], p7[:, 0:DI].rearrange("p (k d) -> p k d", k=CC),
                                          xD[s.par][:, :, c * P:(c + 1) * P], ALU.add).then_inc(yv_ready, 1)
                    if scan and c + 1 < NC:
                        dve.wait_ge(state_psum, (NC - 1) * s.n + c + 1)
                        if c == 0:
                            dve.tensor_copy(state[0][:, :], p6[:, DI:2 * DI]).then_inc(state_ready, 1)
                        else:
                            dve.wait_ge(decayed_ready, (NC - 2) * s.n + c)
                            dve.tensor_tensor(state[c % 2][:, :], p6[:, DI:2 * DI], decayed[:, :],
                                              ALU.add).then_inc(state_ready, 1)
                    if scan and project and c == 0:
                        softplus_step(q, 2)
                    spread(6)

                gate = GATE_STEPS * (r.n if route else 0)
                if project:
                    tap(q, NC - 1, 1)
                if route:
                    dve.wait_ge(eg_ready, r.n + 1)
                    dve.tensor_scalar(eg[:, :, :], eg[:, :, :], 1.0, None, ALU.add).then_inc(gate_step, 1)
                if project:
                    tap(q, NC - 1, 2)
                if route:
                    dve.wait_ge(gate_step, gate + 1)
                    dve.reciprocal(gates[:, :, :], eg[:, :, :]).then_inc(gate_step, 1)
                if route:
                    wait_apart(dve, gate_step, gate + 2)
                    for k in range(NC):
                        ins = dve.max(top[:, k, :], gates[:, k, :])
                    ins.then_inc(gate_step, 1)
                if project:
                    tap(q, NC - 1, 3)
                if route:
                    wait_apart(dve, gate_step, gate + 3)
                    for k in range(NC):
                        ins = dve.max_index(topi[:, k, :], top[:, k, :], gates[:, k, :])
                    ins.then_inc(gate_step, 1)
                if scan:
                    dve.wait_ge(ss_psum, s.n + 1)
                    wait(dve, rms_ready, s.n)
                    dve.tensor_scalar(ms[:, :], p7[:, 0:NC * PADN].rearrange("p (c e) -> p c e", e=PADN)[:, :, 0],
                                      1.0 / DI, EPS, ALU.mult, ALU.add).then_inc(ms_ready, 1)
                if route:
                    link = chain(gate_step, gate + 4)
                    dve.wait_ge(gate_step, gate + 4)
                    link(dve.tensor_copy(topf[:, :, :], topi[:, :, 0:2]))
                    wait(dve, slot_ready, r.n)
                    link(dve.tensor_tensor(
                        picks[:, :, :, :], iota8[:, :].unsqueeze(1).unsqueeze(1).broadcast_to([P, NC, 2, E]),
                        topf[:, :, :].unsqueeze(3).broadcast_to([P, NC, 2, E]), ALU.is_equal))
                    dve.tensor_tensor(chosen[:, :, :], picks[:, :, 0, :], picks[:, :, 1, :],
                                      ALU.add).then_inc(chosen_ready, 1)
                if scan:
                    residual(s)
                if project and not is_last(s, 2):
                    enter(s.plus(2))
                if route:
                    dve.wait_ge(rank_psum, r.n + 1)
                    dve.tensor_tensor(rows[:, :, :], p4[:, 0:NC * E].rearrange("p (c e) -> p c e", e=E),
                                      next_row[:, :].unsqueeze(1).broadcast_to([P, NC, E]), ALU.add)
                    dve.tensor_tensor(gsum[:, :], top[:, :, 0], top[:, :, 1], ALU.add).then_inc(pos_step, 1)
                    dve.wait_ge(pos_step, POS_STEPS * r.n + 1)
                    dve.tensor_tensor(next_row[:, :], p4[:, NC * E:(NC + 1) * E], next_row[:, :],
                                      ALU.add).then_inc(rank_read, 1)
                    link = chain(pos_step, POS_STEPS * r.n + 1)
                    dve.wait_ge(rowB_ready, r.n + 1)
                    dve.reciprocal(gsum[:, :], gsum[:, :])
                    link(dve.tensor_tensor(prow[:, :, :, :], picks[:, :, :, :],
                                           rows[:, :, :].unsqueeze(2).broadcast_to([P, NC, 2, E]), ALU.mult))
                    link(dve.tensor_reduce(slotf[:, :, :], prow[:, :, :, :], AX_X, ALU.add))
                    for row, k in ((rowA, 0), (rowB, 1)):
                        dve.tensor_tensor(row[r.par][:, :, P + 1], top[:, :, k], gsum[:, :], ALU.mult)
                        dve.tensor_scalar(row[r.par][:, :, P].bitcast(I32), token_id[:, :],
                                          float(TOKENS * k), None, ALU.add)
                    link(dve.tensor_copy(slot[r.par][:, :, :], slotf[:, :, :]))
                    dve.tensor_scalar(token_id[:, :], token_id[:, :], float(TOKS), None,
                                      ALU.add).then_inc(slot_ready, 1)

            slots(dve, slot_dve)

            link = chain(table_step, 0)
            dve.wait_ge(slot_ready, SEQS)
            cnt, f, tiles, ends = tb[:, 0, :], tb[:, 1, :], tb[:, 2, :], tb[:, 3, :]
            link(dve.tensor_copy(pad_at[:, :], next_row[:, :]))
            link(dve.tensor_tensor(cnt, next_row[:, :], region[:, :], ALU.subtract))
            link(dve.tensor_scalar(f, cnt, float(P - 1), None, ALU.add))
            link(dve.tensor_copy(tbi[:, :], f))
            link(dve.tensor_scalar(tbi[:, :], tbi[:, :], P.bit_length() - 1, None, ALU.logical_shift_right))
            link(dve.tensor_copy(tiles, tbi[:, :]))
            link(dve.tensor_copy(ends, tiles))
            for e in range(1, E):
                link(dve.tensor_tensor(ends[:, e:e + 1], ends[:, e - 1:e], ends[:, e:e + 1], ALU.add))
            one = slice(0, 1)
            expert, start, base, last = (tval[:, k, :] for k in range(4))
            tiles_of = iota_tile[one, :].unsqueeze(2).broadcast_to([1, TILES, E])
            link(dve.tensor_tensor(tcmp[:, :, :], tiles_of,
                                   ends[one, :].unsqueeze(1).broadcast_to([1, TILES, E]), ALU.is_ge))
            link(dve.tensor_reduce(expert, tcmp[:, :, :], AX_X, ALU.add))
            link(dve.tensor_tensor(tcmp[:, :, :], tcmp[:, :, :],
                                   tiles[one, :].unsqueeze(1).broadcast_to([1, TILES, E]), ALU.mult))
            link(dve.tensor_reduce(start, tcmp[:, :, :], AX_X, ALU.add))
            link(dve.tensor_tensor(start, iota_tile[one, :], start, ALU.subtract))
            link(dve.tensor_scalar(base, expert, float(REGION), None, ALU.mult))
            link(dve.scalar_tensor_tensor(out=base, in0=start, scalar=float(P), in1=base,
                                          op0=ALU.mult, op1=ALU.add))
            link(dve.tensor_copy(table[:, 0, :], base))
            link(dve.tensor_scalar(last, expert, float(E - 1), None, ALU.min))
            dve.tensor_copy(table[:, 1, :], last).then_inc(table_ready, 1)

            dve.wait_ge(table_ready, 1)
            dve.wait_ge(moe_w_in, 32)

            def fetch(j, k):
                e = dve.value_load(table[0:1, 1, bass.ds(j, 1)], min_val=0, max_val=E - 1)
                wait(dve, h_psum, j - 1)
                dve.tensor_copy(w1e[k % 2], w1[:, bass.ds(e, 1), :].rearrange("p e f -> p (e f)")).then_inc(w1e_ready, 1)
                dve.wait_ge(sT_psum, j + 1)
                dve.tensor_copy(sT[k % 2][:, :], pj[k % 2][:, 0:P]).then_inc(sT_ready, 1)

            def weigh(j, k, turn, first):
                dve.wait_ge(ye_psum, j + 1)
                if not first:
                    dve.wait_ge(rows_out[(k - 4) % RING], 16 * (turn + (1 if k >= 4 else 0)))
                dve.tensor_scalar(ye[k % 4], (p6, p7)[k % 2][:, 0:P], xs[k][:, P + 1:P + 2], None,
                                  ALU.mult).then_inc(ye_ready, 1)

            fetch(0, 0)
            fetch(1, 1)
            for k in range(RING):
                fetch(k + 2, k + 2)
                weigh(k, k, 0, k < 4)
            with dve.Fori(1, TILES // RING - 1) as i:
                for k in range(RING):
                    fetch(RING * i + k + 2, k + 2)
                    weigh(RING * i + k, k, i, False)
            for k in range(RING):
                j = TILES - RING + k
                if k + 2 < RING:
                    fetch(j + 2, k + 2)
                weigh(j, k, TILES // RING - 1, False)

            def finish(s):
                p = s.par
                link = chain(fin_step, FIN_STEPS * s.n)
                dve.wait_ge(yy_in[p], 32 * (s.use + 1))
                wait(dve, fout_ready, NC * (s.n - 1))
                link(dve.tensor_tensor(fin[p], yy[p][:, 0], yy[p][:, 1], ALU.add))
                link(dve.tensor_tensor(fin[p], u_all[:, bass.ds(s.n * NC, NC), :], fin[p], ALU.add))
                for c in range(NC):
                    ins = dve.bn_stats(fst[p][:, c, :], fin[p][:, c, :])
                link(ins, apart=True)
                for c in range(NC):
                    ins = dve.bn_aggr(fmv[p][:, c, :], fst[p][:, c, :])
                link(ins)
                dve.tensor_scalar(fve[p][:, :], fmv[p][:, :, 1], EPS, None, ALU.add).then_inc(fve_ready, 1)

            def minus_mean(s):
                dve.wait_ge(frs_ready, s.n + 1)
                dve.scalar_tensor_tensor(out=fnb[s.par][:, :], in0=fmv[s.par][:, :, 0], scalar=-1.0,
                                         in1=frs[s.par][:, :], op0=ALU.mult,
                                         op1=ALU.mult).then_inc(fnb_ready, 1)

            finish(Seq(0, 0))
            finish(Seq(0, 1))
            minus_mean(Seq(0, 0))
            with dve.Fori(0, SEQS // 2 - 1) as i:
                finish(Seq(i, 2))
                minus_mean(Seq(i, 1))
                finish(Seq(i, 3))
                minus_mean(Seq(i, 2))
            minus_mean(Seq(0, SEQS - 1))

        @block.gpsimd
        def _(pool):
            NCONST = [0]

            def step(ins):
                NCONST[0] += 1
                ins.then_inc(pool_const, 1)
                pool.wait_ge(pool_const, NCONST[0])

            step(pool.memset(ident[:, :], 0.0))
            step(pool.affine_select(out=ident[:, :], in_=ident[:, :], compare_op=ALU.not_equal, fill=1.0,
                                    base=0, pattern=[[-1, P]], channel_multiplier=1))
            step(pool.memset(upto[:, :], 0.0))
            step(pool.affine_select(out=upto[:, :], in_=upto[:, :], compare_op=ALU.is_gt, fill=1.0,
                                    base=0, pattern=[[-1, P]], channel_multiplier=1))
            step(pool.memset(after[:, :], 0.0))
            step(pool.affine_select(out=after[:, :], in_=after[:, :], compare_op=ALU.is_ge, fill=1.0,
                                    base=0, pattern=[[1, P]], channel_multiplier=-1))
            step(pool.memset(before_b[:, :], 0.0))
            step(pool.affine_select(out=before_b[:, :], in_=before_b[:, :], compare_op=ALU.is_ge, fill=1.0,
                                    base=0, pattern=[[-1, P]], channel_multiplier=1))
            step(pool.memset(pick3[:, :], 0.0))
            step(pool.affine_select(out=pick3[:, :], in_=pick3[:, :], compare_op=ALU.not_equal, fill=1.0,
                                    base=0, pattern=[[-1, 3]], channel_multiplier=1))
            step(pool.iota(iota8[:, :], pattern=[[1, E]], base=0, channel_multiplier=0,
                           allow_small_or_imprecise_dtypes=True))
            step(pool.iota(iota_tile[:, :], pattern=[[1, TILES]], base=0, channel_multiplier=0,
                           allow_small_or_imprecise_dtypes=True))
            step(pool.iota(token_id[:, :], pattern=[[P, NC]], base=0, channel_multiplier=1,
                           allow_small_or_imprecise_dtypes=True))
            step(pool.iota(region[:, :], pattern=[[REGION, E]], base=0, channel_multiplier=0,
                           allow_small_or_imprecise_dtypes=True))
            step(pool.iota(next_row[:, :], pattern=[[REGION, E]], base=0, channel_multiplier=0,
                           allow_small_or_imprecise_dtypes=True))
            step(pool.memset(pad_tile[:, :], 0.0))
            step(pool.iota(pad_tile[:, P:P + 1].bitcast(I32), pattern=[[0, 1]], base=2 * TOKENS,
                           channel_multiplier=1))
            pool.memset(decayed[:, :], 0.0).then_inc(const_ready, 1)

            def expand(n, c, par):
                wait(pool, diff_psum, n - 1)
                pool.tensor_tensor(lhsA[c % 2][:, :, :], after[:, :].unsqueeze(1).broadcast_to([P, H, P]),
                                   a[par][:, (c % NC) * H:(c % NC + 1) * H].unsqueeze(2).broadcast_to([P, H, P]),
                                   ALU.mult).then_inc(lhsA_ready, 1)

            def gate_y(s, c):
                n = NC * s.n + c
                pool.wait_ge(yv_ready, n + 1)
                pool.wait_ge(sz_ready, CC * (s.n + 1))
                wait(pool, out_psum, s.n)
                pool.tensor_tensor(gt[:, :, c * P:(c + 1) * P], yv[c % 2][:, :, :],
                                   sz[s.par][:, :, c * P:(c + 1) * P], ALU.mult).then_inc(g_ready, 1)

            def scatter(q, c, k):
                if (c, k) == (0, 0):
                    wait_apart(pool, slot_ready, q.n + 1)
                pool.indirect_dma_start(
                    out=sorted_rows[:, :],
                    out_offset=bass.IndirectOffsetOnAxis(slot[q.par][:, c, k:k + 1], 0),
                    in_=(rowA, rowB)[k][q.par][:, c, :], in_offset=None).then_inc(scattered[q.par][k], 16)

            def slot_pool(s, scan, project, route):
                q, r = s.plus(1), s.plus(-1)
                scatters = not (isinstance(s.n, int) and s.n < 2)
                for c in range(NC):
                    n = NC * s.n + c
                    if route and c == 0:
                        pool.wait_ge(ve_ready, r.n + 1)
                        pool.tensor_tensor(rstd[:, :], ve[:, :], neg_half[:, :], ALU.pow).then_inc(rstd_ready, 1)
                    if scan and 0 < c < NC - 1:
                        pool.wait_ge(state_ready, (NC - 1) * s.n + c)
                        pool.tensor_tensor(heads(decayed[:, :]), heads(state[(c - 1) % 2][:, :]),
                                           per_head(decays[s.par][:, 2, :], c), ALU.mult).then_inc(decayed_ready, 1)
                    if scan and c + 1 < NC:
                        pool.wait_ge(Xdt_ready, n + 1)
                        wait(pool, state_psum, (NC - 1) * s.n + c - 1)
                        pool.tensor_tensor(heads(Xdd[c % 2][:, :]), heads(Xdt[c % 2][:, :]),
                                           per_head(decays[s.par][:, 1, :], c), ALU.mult).then_inc(Xdd_ready, 1)
                    if scan and (c + 2 < NC or project):
                        if c + 2 >= NC:
                            pool.wait_ge(a_ready, q.n + 1)
                        expand(n + 2, c + 2, s.par if c + 2 < NC else q.par)
                    if scan and c > 0:
                        gate_y(s, c - 1)
                    if scatters:
                        scatter(s.plus(-2), c, 0)
                if project and not scan:
                    pool.wait_ge(a_ready, 1)
                    expand(0, 0, 0)
                    expand(1, 1, 0)
                if scan:
                    gate_y(s, NC - 1)
                    pool.wait_ge(ms_ready, s.n + 1)
                    if not (isinstance(s.n, int) and s.n < 1):
                        pool.wait_ge(x1_ready, NC * s.n)
                    pool.tensor_tensor(rms[:, :], ms[:, :], neg_half[:, :], ALU.pow).then_inc(rms_ready, 1)
                if scatters:
                    for c in range(NC):
                        scatter(s.plus(-2), c, 1)

            slots(pool, slot_pool)
            for k in range(2):
                for c in range(NC):
                    scatter(Seq(0, SEQS - 1), c, k)

            def store(j, k):
                wait_apart(pool, ye_ready, j + 1)
                pool.indirect_dma_start(
                    out=moe_rows[:, :], out_offset=bass.IndirectOffsetOnAxis(xs[k][:, P:P + 1].bitcast(I32), 0),
                    in_=ye[k % 4], in_offset=None, bounds_check=2 * TOKENS - 1,
                    oob_is_err=False).then_inc(rows_out[k], 16)

            with pool.Fori(0, TILES // RING) as i:
                for k in range(RING):
                    store(RING * i + k, k)

            def finish(s):
                pool.wait_ge(fve_ready, s.n + 1)
                if not (isinstance(s.n, int) and s.n < 2):
                    pool.wait_ge(fout_ready, NC * (s.n - 1))
                pool.tensor_tensor(frs[s.par][:, :], fve[s.par][:, :], neg_half[:, :],
                                   ALU.pow).then_inc(frs_ready, 1)

            finish(Seq(0, 0))
            finish(Seq(0, 1))
            with pool.Fori(0, SEQS // 2 - 1) as i:
                finish(Seq(i, 2))
                finish(Seq(i, 3))


def kernel(L0_attn_x, L0_attn_Win, L0_attn_conv_w, L0_attn_conv_b, L0_attn_dt_bias, L0_attn_A_log,
           L0_attn_D, L0_attn_norm_w, L0_attn_Wout, L0_ffn_centroids, L0_ffn_W1, L0_ffn_b1, L0_ffn_W2,
           L0_ffn_b2):
    import numpy as np
    import concourse.bacc as bacc
    from concourse.bass_utils import run_bass_kernel_spmd

    def arr(x):
        return np.ascontiguousarray(x)

    win = np.asarray(L0_attn_Win).T
    arrays = dict(
        x=arr(L0_attn_x),
        w_z=arr(win[:, 0:DI]),
        w_xbc=arr(win[:, DI:DI + XC * P]),
        w_dt=arr(win[:, DI + XC * P:]),
        w_gate=arr(np.asarray(L0_ffn_centroids).T),
        w_out=arr(np.asarray(L0_attn_Wout).T.reshape(CC, P, P).transpose(1, 0, 2)),
        conv_w=arr(np.asarray(L0_attn_conv_w).reshape(XC, P, TAPS).transpose(1, 0, 2)),
        conv_b=arr(np.asarray(L0_attn_conv_b).reshape(XC, P).T),
        skip=arr(np.repeat(np.asarray(L0_attn_D), HD).reshape(CC, P).T),
        norm_w=arr(np.asarray(L0_attn_norm_w).reshape(CC, P).T),
        dt_bias=arr(np.broadcast_to(np.asarray(L0_attn_dt_bias), (P, H))),
        A_log=arr(np.broadcast_to(np.asarray(L0_attn_A_log), (P, H))),
        w1=arr(np.asarray(L0_ffn_W1).transpose(1, 0, 2)),
        b1=arr(np.asarray(L0_ffn_b1).reshape(E * FB, P).T),
        w2=arr(np.asarray(L0_ffn_W2).reshape(E, FB, P, P).transpose(2, 0, 1, 3)),
        b2=arr(np.broadcast_to(np.asarray(L0_ffn_b2).reshape(1, E * P), (3, E * P))),
    )
    nc = bacc.Bacc("TRN2", target_bir_lowering=False, num_devices=1)
    t = {n: nc.dram_tensor(f"in_{n}", a.shape, mybir.dt.from_np(a.dtype), kind="ExternalInput").ap()
         for n, a in arrays.items()}
    out = nc.dram_tensor("out_0", [SEQS, TOKS, P], F32, kind="ExternalOutput").ap()
    build(nc, t, out)
    got = run_bass_kernel_spmd(nc, [{f"in_{n}": a for n, a in arrays.items()}], core_ids=[0])
    return got.results[0]["out_0"]
```

```python
from contextlib import ExitStack

import concourse.bass as bass
from concourse import mybir
from concourse.alu_op_type import AluOpType as ALU

F32 = mybir.dt.float32
BF16 = mybir.dt.bfloat16
I32 = mybir.dt.int32
U32 = mybir.dt.uint32
ACT = mybir.ActivationFunctionType
AX_X = mybir.AxisListType.X

P = 128
SEQS, TOKS = 16, 512
NC = TOKS // P
H, HD = 4, 64
DI = H * HD
CC = DI // P
XC = CC + 2
TAPS = 4
E, FF = 8, 512
FB = FF // P
EPS = 1e-5
PADN = 96
TOKENS = SEQS * TOKS
ROW = P + 2
REGION = TOKENS + P
TILES = 2 * TOKENS // P + E
SPARE = E * REGION
LOG_TERMS = (13, 11, 9, 7, 5, 3)
SP_STEPS = 13
LN_STEPS = 2
GATE_STEPS = 6
POS_STEPS = 4
FIN_STEPS = 3
ON_POOL = 1
FIN = 4


class Seq:

    def __init__(self, half, off):
        self.half, self.off = half, off
        self.n = 2 * half + off
        self.par = off % 2
        self.use = half + off // 2

    def plus(self, d):
        return Seq(self.half, self.off + d)


def wait(eng, sem, value):
    if not isinstance(value, int) or value > 0:
        eng.wait_ge(sem, value)


def build(nc, t, out):
    ctx = ExitStack()
    with ctx:
        def sb(name, shape, dt=F32):
            return ctx.enter_context(nc.sbuf_tensor(name, shape, dt))

        def bank(name):
            return ctx.enter_context(nc.psum_tensor(name, [P, 512], F32))

        def sem(name):
            return ctx.enter_context(nc.semaphore(name))

        sorted_rows = nc.dram_tensor("sorted_rows", [SPARE + E * P, ROW], F32, kind="Internal").ap()
        moe_rows = nc.dram_tensor("moe_rows", [2 * TOKENS, P], F32, kind="Internal").ap()

        w_z = sb("w_z", [P, DI])
        w_xbc = sb("w_xbc", [P, XC * P])
        w_dt = sb("w_dt", [P, PADN])
        w_gate = sb("w_gate", [P, PADN])
        w_out = sb("w_out", [P, CC, P])
        conv_w = sb("conv_w_sb", [P, XC, TAPS])
        conv_b = sb("conv_b_sb", [P, XC])
        skip = sb("skip", [P, CC])
        norm_w = sb("norm_w_sb", [P, CC])
        dt_bias = sb("dt_bias_sb", [P, H])
        neg_a = sb("neg_a", [P, H])
        w1 = sb("w1", [P, E, FF])
        w2 = sb("w2", [P, E, FB, P])
        b1 = sb("b1_sb", [P, E * FB])
        b2 = sb("b2_sb", [P, E, P])
        ident = sb("ident", [P, P])
        upto = sb("upto", [P, P])
        after = sb("after", [P, P])
        before_b = sb("before_b", [P, P], BF16)
        ones = sb("ones", [P, P])
        ones_b = sb("ones_b", [P, P], BF16)
        neg_half = sb("neg_half", [P, NC])
        iota8 = sb("iota8", [P, E])
        iota_tile = sb("iota_tile", [P, TILES])
        token_id = sb("token_id", [P, NC])
        region = sb("region", [P, E])
        next_row = sb("next_row", [P, E])
        pad_tile = sb("pad_tile", [P, ROW])

        xa = [sb(f"xa{i}", [P, NC, P]) for i in range(2)]
        xres = [sb(f"xres{i}", [P, NC, P]) for i in range(2)]
        xT = [sb(f"xT{i}", [P, TOKS]) for i in range(2)]
        acc = sb("acc", [P, XC, TOKS])
        xc = [sb(f"xc{i}", [P, XC, TOKS]) for i in range(2)]
        sz = [sb(f"sz{i}", [P, CC, TOKS]) for i in range(2)]
        xD = [sb(f"xD{i}", [P, CC, TOKS]) for i in range(2)]
        v = sb("v", [P, NC, H])
        vabs = sb("vabs", [P, NC * H])
        ev = sb("ev", [P, NC * H])
        sp = [sb(f"sp{i}", [P, NC * H]) for i in range(5)]
        dtp = [sb(f"dtp{i}", [P, NC * H]) for i in range(2)]
        a = [sb(f"a{i}", [P, PADN]) for i in range(2)]
        decays = [sb(f"decays{i}", [P, 3, NC * H]) for i in range(2)]
        lhsA = [sb(f"lhsA{i}", [P, H, P]) for i in range(2)]
        L = [sb(f"L{i}", [P, H, P]) for i in range(2)]
        Gm = sb("Gm", [P, NC, P])
        M = [sb(f"M{i}", [P, H, P]) for i in range(2)]
        Xdt = [sb(f"Xdt{i}", [P, DI]) for i in range(2)]
        Xdd = [sb(f"Xdd{i}", [P, DI]) for i in range(2)]
        Btok = [sb(f"Btok{i}", [P, P]) for i in range(2)]
        state = [sb(f"state{i}", [P, DI]) for i in range(2)]
        decayed = sb("decayed", [P, DI])
        carried = sb("carried", [P, DI])
        yv = [sb(f"yv{i}", [P, CC, P]) for i in range(2)]
        ysq = sb("ysq", [P, CC, TOKS])
        gt = sb("gt", [P, CC, TOKS])
        ms = sb("ms", [P, NC])
        rms = sb("rms", [P, NC])
        st = sb("st", [P, NC, 6])
        mv = sb("mv", [P, NC, 2])
        ve = sb("ve", [P, NC])
        rstd = sb("rstd", [P, NC])
        shift = sb("shift", [P, NC])
        rowA = [sb(f"rowA{i}", [P, NC, ROW]) for i in range(2)]
        rowB = [sb(f"rowB{i}", [P, NC, ROW]) for i in range(2)]
        uT = sb("uT", [P, TOKS])
        eg = sb("eg", [P, NC, E])
        gates = sb("gates", [P, NC, E])
        top = sb("top", [P, NC, 8])
        topi = sb("topi", [P, NC, 8], U32)
        topf = sb("topf", [P, NC, 2])
        picks = sb("picks", [P, NC, 2, E])
        chosen = sb("chosen", [P, NC, E], BF16)
        gsum = sb("gsum", [P, NC])
        rows = sb("rows", [P, NC, E])
        prow = sb("prow", [P, NC, 2, E])
        slotf = sb("slotf", [P, NC, 2])
        slot = [sb(f"slot{i}", [P, NC, 2], I32) for i in range(2)]

        tb = sb("tb", [P, 8, E])
        tbi = sb("tbi", [P, E], I32)
        tcmp = sb("tcmp", [1, TILES, E])
        tval = sb("tval", [1, 4, TILES])
        table = sb("table", [1, 2, TILES], I32)
        pad_at = sb("pad_at", [P, E], I32)

        RING = 8
        xs = [sb(f"xs{i}", [P, ROW]) for i in range(RING)]
        sT = Btok
        w1e = [M[i][:, :, :].rearrange("p h s -> p (h s)") for i in range(2)]
        hT = L
        b2e = [lhsA[i // 2][:, i % 2, :] for i in range(4)]
        ye = [yv[i // 2][:, i % 2, :] for i in range(4)]

        yy = [big[:, 2 * i:2 * i + 2, :].rearrange("p k (c d) -> p k c d", c=NC)
              for big in (acc, xc[0]) for i in range(2)]
        fin = [b.rearrange("p (c d) -> p c d", c=NC) for b in (xc[1][:, k, :] for k in range(4))]
        fout = [big[:, k, :].rearrange("p (c d) -> p c d", c=NC) for big in sz for k in range(2)]
        fst = [sb(f"fst{i}", [P, NC, 6]) for i in range(FIN)]
        fmv = [sb(f"fmv{i}", [P, NC, 2]) for i in range(FIN)]
        fve = [sb(f"fve{i}", [P, NC]) for i in range(FIN)]
        frs = [sb(f"frs{i}", [P, NC]) for i in range(FIN)]
        fnb = [sb(f"fnb{i}", [P, NC]) for i in range(FIN)]

        pj = [bank(f"pj{i}") for i in range(2)]
        pl = [bank(f"pl{i}") for i in range(2)]
        p4 = bank("p4")
        p5 = bank("p5")
        p6 = bank("p6")
        p7 = bank("p7")

        w_in = sem("w_in")
        moe_w_in = sem("moe_w_in")
        a_log_in = sem("a_log_in")
        padding_zero = sem("padding_zero")
        const_ready = sem("const_ready")
        const_step = sem("const_step")
        pool_const = sem("pool_const")
        xa_in = [sem(f"xa_in{i}") for i in range(2)]
        xres_in = [sem(f"xres_in{i}") for i in range(2)]
        names_pe = ("xT_psum", "dt_psum", "proj_psum", "z_psum", "sums_psum", "diff_psum", "G_psum",
                    "tr_psum", "off_psum", "y_psum", "state_psum", "ss_psum", "out_psum", "uT_psum",
                    "logit_psum", "rank_psum")
        (xT_psum, dt_psum, proj_psum, z_psum, sums_psum, diff_psum, G_psum, tr_psum, off_psum, y_psum,
         state_psum, ss_psum, out_psum, uT_psum, logit_psum, rank_psum) = [sem(n) for n in names_pe]
        names_act = ("xT_ready", "abs_done", "ev_ready", "L_ready", "tap0_done", "Btok_ready", "sq_done",
                     "uT_ready", "rowB_ready", "eg_ready", "decays_ready", "xc_ready", "sz_ready",
                     "xD_ready")
        (xT_ready, abs_done, ev_ready, L_ready, tap0_done, Btok_ready, sq_done, uT_ready, rowB_ready,
         eg_ready, decays_ready, xc_ready, sz_ready, xD_ready) = [sem(n) for n in names_act]
        names_dve = ("x1_ready", "Gm_ready", "M_ready", "Xdt_ready", "v_ready", "yv_ready", "state_ready",
                     "sp_step", "a_ready", "tap_done", "conv_done", "carried_ready", "ln_step", "ve_ready", "shift_ready",
                     "u_ready", "gate_step", "chosen_ready", "ms_ready", "pos_step", "rank_read",
                     "slot_ready")
        (x1_ready, Gm_ready, M_ready, Xdt_ready, v_ready, yv_ready, state_ready, sp_step, a_ready,
         tap_done, conv_done, carried_ready, ln_step, ve_ready, shift_ready, u_ready, gate_step, chosen_ready,
         ms_ready, pos_step, rank_read, slot_ready) = [sem(n) for n in names_dve]
        names_pool = ("lhsA_ready", "Xdd_ready", "decayed_ready", "g_ready", "rms_ready", "rstd_ready")
        (lhsA_ready, Xdd_ready, decayed_ready, g_ready, rms_ready, rstd_ready) = [sem(n) for n in names_pool]
        scattered = [[sem(f"scattered_{'AB'[k]}{i}") for k in range(2)] for i in range(2)]
        table_step = sem("table_step")
        table_ready = sem("table_ready")
        spare_in = sem("spare_in")
        pads_known = sem("pads_known")
        pads_in = sem("pads_in")
        xs_in = [sem(f"xs_in{i}") for i in range(RING)]
        rows_out = [sem(f"rows_out{i}") for i in range(RING)]
        names_b = ("sT_psum", "w1e_ready", "h_psum", "hT_ready", "ye_psum", "ye_ready")
        biased = sem("biased")
        b2e_ready = sem("b2e_ready")
        (sT_psum, w1e_ready, h_psum, hT_ready, ye_psum, ye_ready) = [sem(n) for n in names_b]
        yy_in = [sem(f"yy_in{i}") for i in range(FIN)]
        fin_out = [sem(f"fin_out{i}") for i in range(FIN)]
        (moe_sum, fin_step, fve_ready, frs_ready, fnb_ready, fout_ready) = [
            sem(n) for n in ("moe_sum", "fin_step", "fve_ready", "frs_ready", "fnb_ready", "fout_ready")]

        W_LOADS = 11
        MOE_W_LOADS = 3
        CONSTS = 6

        def wait_apart(eng, sem, value):
            if not isinstance(value, int):
                value = eng.to_reg(value)
            eng.wait_ge(const_ready, CONSTS)
            eng.wait_ge(sem, value)

        block = ctx.enter_context(nc.Block())

        x_seq = t["x"].rearrange("b (c p) d -> b p c d", p=P)
        out_seq = out.rearrange("b (c p) d -> b p c d", p=P)
        moe_seq = moe_rows.rearrange("(k b c p) d -> b p k c d", k=2, b=SEQS, p=P)

        def tokens(ap, n=H):
            return ap.rearrange("p (c h) -> p c h", h=n)

        def per_head(ap, c):
            return ap[:, c * H:(c + 1) * H].unsqueeze(2).broadcast_to([P, H, HD])

        def heads(ap):
            return ap.rearrange("p (h d) -> p h d", h=H)

        def is_last(s, k):
            return isinstance(s.n, int) and s.n > SEQS - 1 - k

        def slots(eng, slot_fn):
            slot_fn(Seq(0, -1), False, True, False)
            slot_fn(Seq(0, 0), True, True, False)
            slot_fn(Seq(0, 1), True, True, True)
            slot_fn(Seq(0, 2), True, True, True)
            with eng.Fori(1, (SEQS - 4) // 2) as i:
                slot_fn(Seq(i, 1), True, True, True)
                slot_fn(Seq(i, 2), True, True, True)
            slot_fn(Seq(0, SEQS - 3), True, True, True)
            slot_fn(Seq(0, SEQS - 2), True, True, True)
            slot_fn(Seq(0, SEQS - 1), True, False, True)
            slot_fn(Seq(0, SEQS), False, False, True)

        def write_pads(eng, experts):
            eng.wait_ge(pads_known, 1)
            for k in experts:
                at = eng.value_load(pad_at[0:1, k:k + 1], min_val=k * REGION, max_val=k * REGION + TOKENS)
                eng.dma_start(sorted_rows[bass.ds(at, P), :], pad_tile[:, :]).then_inc(pads_in, 16)

        @block.sync
        def _(dq):
            dq.dma_start(xa[0][:, :, :], x_seq[0]).then_inc(xa_in[0], 16)
            for dst, name in ((w_xbc[:, :], "w_xbc"), (dt_bias[:, :], "dt_bias"), (conv_w[:, :, :], "conv_w"),
                              (w_z[:, :], "w_z"), (skip[:, :], "skip"), (w_out[:, :, :], "w_out")):
                dq.dma_start(dst, t[name]).then_inc(w_in, 16)

            def slot_dma(s, scan, project, route):
                if project and not (isinstance(s.n, int) and s.n >= SEQS - 2):
                    q = s.plus(2)
                    wait(dq, xT_psum, q.n - 1)
                    dq.dma_start(xa[q.par][:, :, :], x_seq[q.n]).then_inc(xa_in[q.par], 16)
                if project:
                    q = s.plus(1)
                    wait(dq, x1_ready, NC * (q.n - 1))
                    dq.dma_start(xres[q.par][:, :, :], x_seq[q.n]).then_inc(xres_in[q.par], 16)

            slot_dma(Seq(0, -1), False, True, False)
            slot_dma(Seq(0, 0), True, True, False)
            dq.wait_ge(z_psum, CC)
            dq.dma_start(w1[:, :, :], t["w1"]).then_inc(moe_w_in, 16)
            dq.dma_start(w2[:, :, :, :], t["w2"]).then_inc(moe_w_in, 16)
            dq.dma_start(b2[:, :, :], t["b2"]).then_inc(moe_w_in, 16)
            for k in range(E):
                dq.dma_start(sorted_rows[SPARE + k * P:SPARE + (k + 1) * P, :],
                             pad_tile[:, :]).then_inc(spare_in, 16)
            slot_dma(Seq(0, 1), True, True, True)
            slot_dma(Seq(0, 2), True, True, True)
            with dq.Fori(1, (SEQS - 4) // 2) as i:
                slot_dma(Seq(i, 1), True, True, True)
                slot_dma(Seq(i, 2), True, True, True)
            slot_dma(Seq(0, SEQS - 3), True, True, True)
            slot_dma(Seq(0, SEQS - 2), True, True, True)
            slot_dma(Seq(0, SEQS - 1), True, False, True)
            slot_dma(Seq(0, SEQS), False, False, True)

            write_pads(dq, range(0, E // 2))
            dq.wait_ge(table_ready, 1)
            dq.wait_ge(pads_in, 16 * E)
            dq.wait_ge(spare_in, 16 * E)
            for i in range(2):
                for k in range(2):
                    dq.wait_ge(scattered[i][k], 16 * NC * SEQS // 2)

            def load_rows(tile, k, turn):
                wait(dq, rows_out[k], 16 * turn)
                at = dq.value_load(table[0:1, 0, bass.ds(tile, 1)], min_val=0, max_val=SPARE + (E - 1) * P)
                dq.dma_start(xs[k][:, :], sorted_rows[bass.ds(at, P), :]).then_inc(xs_in[k], 16)

            for k in range(RING):
                load_rows(k, k, 0)
            with dq.Fori(1, TILES // RING) as i:
                for k in range(RING):
                    load_rows(RING * i + k, k, i)

            for k in range(RING):
                dq.wait_ge(rows_out[k], 16 * TILES // RING)

            def load_moe(turn, i):
                n = FIN * turn + i
                wait(dq, moe_sum, n - FIN + 1)
                wait(dq, fve_ready, n - FIN + 1)
                for k in range(2):
                    dq.dma_start(yy[i][:, k], moe_seq[n, :, k]).then_inc(yy_in[i], 16)

            for i in range(FIN):
                load_moe(0, i)
            with dq.Fori(1, SEQS // FIN) as turn:
                for i in range(FIN):
                    load_moe(turn, i)
            for i in range(FIN):
                dq.wait_ge(fin_out[i], 16 * SEQS // FIN)

        @block.tensor
        def _(pe):
            pe.wait_ge(const_ready, CONSTS)

            def project_block(q, k):
                if k == 0:
                    pe.wait_ge(xT_ready, q.n + 1)
                    wait(pe, sz_ready, CC * (q.n - 1) + 1)
                elif k == 1:
                    pe.wait_ge(v_ready, q.n + 1)
                else:
                    pe.wait_ge(conv_done, XC * q.n + k - 1)
                pe.matmul(pj[k % 2][:, :], w_xbc[:, k * P:(k + 1) * P], xT[q.par][:, :],
                          start=True, stop=True).then_inc(proj_psum, 1)

            def z_block(q, k):
                pe.wait_ge(xT_ready, q.n + 1)
                if k > 0:
                    wait(pe, carried_ready, (NC - 1) * q.n)
                elif is_last(q, 1):
                    pe.wait_ge(conv_done, XC * q.n + 3)
                else:
                    pe.wait_ge(xT_ready, q.n + 2)
                pe.matmul((pj[0], p6)[k][:, :], w_z[:, k * P:(k + 1) * P], xT[q.par][:, :],
                          start=True, stop=True).then_inc(z_psum, 1)

            def exponents(n, c):
                pe.wait_ge(lhsA_ready, n + 1)
                wait(pe, L_ready, n - 1)
                for h in range(H):
                    mm = pe.matmul(pl[c % 2][:, h * P:(h + 1) * P], lhsA[c % 2][:, h, :], upto[:, :],
                                   start=True, stop=True)
                mm.then_inc(diff_psum, 1)

            def enter_x(q, convolved):
                pe.wait_ge(xa_in[q.par], 16 * (q.use + 1))
                wait(pe, conv_done, convolved)
                for c in range(NC):
                    mm = pe.transpose(pj[0][:, c * P:(c + 1) * P], xa[q.par][:, c, :], ident[:, :])
                mm.then_inc(xT_psum, 1)

            def enter_dt(q, convolved):
                pe.wait_ge(xT_ready, q.n + 1)
                wait(pe, conv_done, convolved)
                for c in range(NC):
                    mm = pe.matmul(pj[1][:, c * PADN:(c + 1) * PADN], xT[q.par][:, c * P:(c + 1) * P],
                                   w_dt[:, :], start=True, stop=True)
                mm.then_inc(dt_psum, 1)

            def slot_pe(s, scan, project, route):
                q, r, nxt = s.plus(1), s.plus(-1), s.plus(2)
                if not scan and project:
                    enter_x(q, 0)
                    pe.wait_ge(w_in, 16 * W_LOADS)
                    enter_dt(q, 0)
                if scan:
                    pe.wait_ge(xc_ready, XC * (s.n + 1))
                    wait(pe, ms_ready, s.n)
                    for c in range(NC):
                        tok = slice(c * P, (c + 1) * P)
                        mm = pe.matmul(p7[:, tok], xc[s.par][:, CC, tok], xc[s.par][:, CC + 1, tok],
                                       start=True, stop=True)
                    mm.then_inc(G_psum, 1)
                for c in range(NC):
                    tok = slice(c * P, (c + 1) * P)
                    n = NC * s.n + c
                    if scan and (c + 1 < NC or project):
                        exponents(n + 1, c + 1)
                    if scan:
                        pe.wait_ge(Xdt_ready, n) if not isinstance(n, int) or n > 0 else None
                        wait(pe, Btok_ready, (NC - 1) * s.n + c)
                        if c == 0:
                            wait(pe, x1_ready, NC * s.n)
                        for k in range(CC):
                            mm = pe.transpose(p5[:, k * P:(k + 1) * P], xc[s.par][:, k, tok], ident[:, :])
                        if c + 1 < NC:
                            mm = pe.transpose(p5[:, CC * P:(CC + 1) * P], xc[s.par][:, CC, tok], ident[:, :])
                        mm.then_inc(tr_psum, 1)
                        if c > 0:
                            pe.wait_ge(state_ready, (NC - 1) * s.n + c)
                            pe.matmul(p6[:, 0:DI], xc[s.par][:, CC + 1, tok], state[(c - 1) % 2][:, :],
                                      start=True, stop=True).then_inc(off_psum, 1)
                    if project:
                        project_block(q, c)
                    if scan:
                        pe.wait_ge(M_ready, n + 1)
                        pe.wait_ge(Xdt_ready, n + 1)
                        if c > 0:
                            pe.wait_ge(yv_ready, n)
                        for h in range(H):
                            half = slice((h % 2) * HD, (h % 2 + 1) * HD)
                            mm = pe.matmul(p7[half, (h // 2) * P:(h // 2 + 1) * P],
                                           Xdt[c % 2][:, h * HD:(h + 1) * HD], M[c % 2][:, h, :],
                                           start=(h < 2), stop=(c == 0), skip_group_check=True)
                        if c > 0:
                            pe.wait_ge(carried_ready, (NC - 1) * s.n + c)
                            for k in range(CC):
                                mm = pe.matmul(p7[:, k * P:(k + 1) * P], carried[:, k * P:(k + 1) * P],
                                               ident[:, :], start=False, stop=True, skip_group_check=True)
                        mm.then_inc(y_psum, 1)
                        if c + 1 < NC:
                            pe.wait_ge(Btok_ready, (NC - 1) * s.n + c + 1)
                            pe.wait_ge(Xdd_ready, (NC - 1) * s.n + c + 1)
                            if c == 0:
                                pe.wait_ge(sz_ready, CC * (s.n + 1))
                            pe.matmul(p6[:, DI:2 * DI], Btok[c % 2][:, :], Xdd[c % 2][:, :],
                                      start=True, stop=True).then_inc(state_psum, 1)
                    if route and c == 1:
                        pe.wait_ge(u_ready, NC * (r.n + 1))
                        wait(pe, rank_read, r.n)
                        if scan:
                            pe.wait_ge(decays_ready, s.n + 1)
                        for k in range(NC):
                            mm = pe.transpose(p4[:, k * P:(k + 1) * P], rowA[r.par][:, k, 0:P], ident[:, :])
                        mm.then_inc(uT_psum, 1)
                    if route and c == 2:
                        pe.wait_ge(uT_ready, r.n + 1)
                        for k in range(NC):
                            mm = pe.matmul(p4[:, k * PADN:(k + 1) * PADN], uT[:, k * P:(k + 1) * P],
                                           w_gate[:, :], start=True, stop=True)
                        mm.then_inc(logit_psum, 1)
                if project and not is_last(s, 2):
                    enter_x(nxt, XC * q.n + 3)
                if project:
                    pe.wait_ge(a_ready, q.n + 1)
                    if route:
                        pe.wait_ge(eg_ready, r.n + 1)
                    for k, mask in enumerate((upto, after, ones)):
                        mm = pe.matmul(p4[:, k * PADN:(k + 1) * PADN], mask[:, :], a[q.par][:, :],
                                       start=True, stop=True)
                    mm.then_inc(sums_psum, 1)
                if scan:
                    pe.wait_ge(sq_done, NC * (s.n + 1))
                    pe.wait_ge(yv_ready, NC * (s.n + 1))
                    for c in range(NC):
                        for k in range(CC):
                            mm = pe.matmul(p7[:, c * PADN:(c + 1) * PADN], ysq[:, k, c * P:(c + 1) * P],
                                           ones[:, 0:PADN], start=(k == 0), stop=(k == CC - 1))
                    mm.then_inc(ss_psum, 1)
                if scan:
                    pe.wait_ge(g_ready, NC * (s.n + 1))
                    pe.wait_ge(Xdt_ready, NC * (s.n + 1))
                    for c in range(NC):
                        for k in range(CC):
                            mm = pe.matmul(p5[:, c * P:(c + 1) * P], gt[:, k, c * P:(c + 1) * P],
                                           w_out[:, k, :], start=(k == 0), stop=(k == CC - 1))
                    mm.then_inc(out_psum, 1)
                if project:
                    z_block(q, 0)
                    z_block(q, 1)
                if project and not is_last(s, 2):
                    enter_dt(nxt, XC * q.n + XC)
                if route:
                    pe.wait_ge(chosen_ready, r.n + 1)
                    if project:
                        pe.wait_ge(decays_ready, q.n + 1)
                    else:
                        pe.wait_ge(eg_ready, r.n + 1)
                    for c in range(NC + 1):
                        for k in range(c):
                            mm = pe.matmul(p4[:, c * E:(c + 1) * E], ones_b[:, :], chosen[:, k, :],
                                           start=(k == 0), stop=(k == NC - 1))
                        if c < NC:
                            mm = pe.matmul(p4[:, c * E:(c + 1) * E], before_b[:, :], chosen[:, c, :],
                                           start=(c == 0), stop=True)
                    mm.then_inc(rank_psum, 1)
                if project and not scan:
                    exponents(0, 0)

            slots(pe, slot_pe)

            pe.wait_ge(rank_read, SEQS)
            pe.wait_ge(table_ready, 1)
            pe.wait_ge(moe_w_in, 16 * MOE_W_LOADS)

            def transpose_rows(j, k, turn):
                pe.wait_ge(xs_in[k], 16 * (turn + 1))
                pe.transpose(pj[k % 2][:, 0:P], xs[k][:, 0:P], ident[:, :]).then_inc(sT_psum, 1)

            def up(j, k):
                pe.wait_ge(w1e_ready, j + 1)
                for f in range(FB):
                    mm = pe.matmul(pl[k % 2][:, f * P:(f + 1) * P], w1e[k % 2][:, f * P:(f + 1) * P],
                                   sT[k % 2][:, :], start=True, stop=True)
                mm.then_inc(h_psum, 1)

            def expert_of(j):
                return pe.value_load(table[0:1, 1, bass.ds(j, 1)], min_val=0, max_val=E - 1)

            def down(j, k, e):
                pe.wait_ge(hT_ready, FB * (j + 1))
                wait(pe, biased, j - 1)
                o = (p6, p7)[k % 2]
                for f in range(FB):
                    mm = pe.matmul(o[:, 0:P], hT[k % 2][:, f, :], w2[:, bass.ds(e, 1), f, :].rearrange("p e d -> p (e d)"),
                                   start=(f == 0), stop=(f == FB - 1))
                mm.then_inc(ye_psum, 1)

            transpose_rows(0, 0, 0)
            transpose_rows(1, 1, 0)
            up(0, 0)
            def turn_pe(i):
                for k in range(RING):
                    j = RING * i + k
                    e = expert_of(j)
                    transpose_rows(j + 2, (k + 2) % RING, i + (k + 2) // RING)
                    up(j + 1, k + 1)
                    down(j, k, e)

            turn_pe(0)
            with pe.Fori(0, (TILES // RING - 3) // 2) as i:
                turn_pe(2 * i + 1)
                turn_pe(2 * i + 2)
            turn_pe(TILES // RING - 2)
            for k in range(RING):
                j = TILES - RING + k
                e = expert_of(j)
                if k + 2 < RING:
                    transpose_rows(j + 2, k + 2, TILES // RING - 1)
                if k + 1 < RING:
                    up(j + 1, k + 1)
                down(j, k, e)

        @block.scalar
        def _(act):
            act.dma_start(neg_a[:, :], t["A_log"]).then_inc(a_log_in, 16)
            act.wait_ge(padding_zero, 2)
            for dst, name in ((w_dt[:, 0:H], "w_dt"), (conv_b[:, :], "conv_b"), (w_gate[:, 0:E], "w_gate"),
                              (norm_w[:, :], "norm_w"), (b1[:, :], "b1")):
                act.dma_start(dst, t[name]).then_inc(w_in, 16)
            act.wait_ge(a_log_in, 16)
            act.activation(neg_a[:, :], neg_a[:, :], ACT.Exp).then_inc(const_step, 1)
            act.wait_ge(w_in, 16 * W_LOADS)

            def exp_exponents(n, c):
                act.wait_ge(diff_psum, n + 1)
                wait(act, M_ready, n - 1)
                act.activation(L[c % 2][:, :, :], pl[c % 2][:, :], ACT.Exp).then_inc(L_ready, 1)

            def enter(q):
                act.wait_ge(xT_psum, q.n + 1)
                wait(act, z_psum, CC * (q.n - 1))
                act.copy(xT[q.par][:, :], pj[0][:, :]).then_inc(xT_ready, 1)

            def square(s, c):
                act.wait_ge(yv_ready, NC * s.n + c + 1)
                wait(act, ss_psum, s.n)
                act.activation(ysq[:, :, c * P:(c + 1) * P], yv[c % 2][:, :, :],
                               ACT.Square).then_inc(sq_done, 1)

            def slot_act(s, scan, project, route):
                q, r = s.plus(1), s.plus(-1)
                if project and not scan:
                    enter(q)
                for c in range(NC):
                    n = NC * s.n + c
                    tok = slice(c * P, (c + 1) * P)
                    if scan and (c + 1 < NC or project):
                        exp_exponents(n + 1, c + 1)
                    if scan and c + 1 < NC:
                        act.wait_ge(tr_psum, n + 1)
                        wait(act, state_psum, (NC - 1) * s.n + c - 1)
                        act.copy(Btok[c % 2][:, :], p5[:, CC * P:(CC + 1) * P]).then_inc(Btok_ready, 1)
                    if project and c == 0:
                        act.wait_ge(v_ready, q.n + 1)
                        act.activation(vabs[:, :], v[:, :, :], ACT.Abs).then_inc(abs_done, 1)
                        act.wait_ge(abs_done, q.n + 1)
                        wait(act, a_ready, q.n)
                        act.activation(ev[:, :], vabs[:, :], ACT.Exp, scale=-1.0).then_inc(ev_ready, 1)
                    if project:
                        act.wait_ge(proj_psum, XC * q.n + c + 1)
                        wait(act, xc_ready, XC * (q.n - 1) + c + 1)
                        act.activation(acc[:, c, :], pj[c % 2][:, :], ACT.Identity,
                                       bias=conv_b[:, c:c + 1],
                                       scale=conv_w[:, c, TAPS - 1:TAPS]).then_inc(tap0_done, 1)
                    if route and c == 0:
                        act.wait_ge(shift_ready, r.n + 1)
                        act.wait_ge(rstd_ready, r.n + 1)
                        act.wait_ge(x1_ready, NC * (r.n + 1))
                        for k in range(NC):
                            act.activation(rowA[r.par][:, k, 0:P], rowA[r.par][:, k, 0:P], ACT.Identity,
                                           bias=shift[:, k:k + 1], scale=rstd[:, k:k + 1]).then_inc(u_ready, 1)
                    if scan and c > 0:
                        square(s, c - 1)
                    if route and c == 1:
                        act.wait_ge(u_ready, NC * (r.n + 1))
                        act.wait_ge(uT_psum, r.n + 1)
                        act.copy(uT[:, :], p4[:, :]).then_inc(uT_ready, 1)
                    if route and c == 2:
                        if not (isinstance(r.n, int) and r.n < 2):
                            act.wait_ge(scattered[r.par][1], 16 * NC * r.use)
                        act.copy(rowB[r.par][:, :, 0:P], rowA[r.par][:, :, 0:P]).then_inc(rowB_ready, 1)
                        act.wait_ge(logit_psum, r.n + 1)
                        act.activation(eg[:, :, :],
                                       p4[:, 0:NC * PADN].rearrange("p (c e) -> p c e", e=PADN)[:, :, 0:E],
                                       ACT.Exp, scale=-1.0).then_inc(eg_ready, 1)
                if scan:
                    square(s, NC - 1)
                if project and not is_last(s, 2):
                    enter(s.plus(2))
                if project:
                    act.wait_ge(sums_psum, q.n + 1)
                    act.activation(decays[q.par][:, :, :],
                                   p4[:, 0:3 * PADN].rearrange("p (k e) -> p k e", e=PADN)[:, :, 0:NC * H],
                                   ACT.Exp).then_inc(decays_ready, 1)
                    if not scan:
                        exp_exponents(0, 0)
                    for k in range(XC):
                        act.wait_ge(conv_done, XC * q.n + k + 1)
                        wait(act, y_psum, NC * (q.n - 1))
                        act.activation(xc[q.par][:, k, :], acc[:, k, :], ACT.Silu).then_inc(xc_ready, 1)
                    for k in range(CC):
                        act.wait_ge(xc_ready, XC * q.n + k + 1)
                        wait(act, yv_ready, NC * (q.n - 1))
                        act.activation(xD[q.par][:, k, :], xc[q.par][:, k, :], ACT.Identity,
                                       scale=skip[:, k:k + 1]).then_inc(xD_ready, 1)
                    for k in range(CC):
                        act.wait_ge(z_psum, CC * q.n + k + 1)
                        wait(act, g_ready, NC * (q.n - 1))
                        act.activation(sz[q.par][:, k, :], (pj[0], p6)[k][:, :], ACT.Silu).then_inc(sz_ready, 1)

            slots(act, slot_act)

            def gelu(j, k):
                e = act.value_load(table[0:1, 1, bass.ds(j, 1)], min_val=0, max_val=E - 1)
                act.wait_ge(h_psum, j + 1)
                wait(act, ye_psum, j - 1)
                for f in range(FB):
                    act.activation(hT[k % 2][:, f, :], pl[k % 2][:, f * P:(f + 1) * P], ACT.Gelu,
                                   bias=b1[:, bass.ds(e * FB + f, 1)]).then_inc(hT_ready, 1)

            write_pads(act, range(E // 2, E))
            act.wait_ge(table_ready, 1)
            def turn_act(i):
                for k in range(RING):
                    gelu(RING * i + k, k)

            turn_act(0)
            with act.Fori(0, (TILES // RING - 1) // 2) as i:
                turn_act(2 * i + 1)
                turn_act(2 * i + 2)

            def finish(turn, i):
                n = FIN * turn + i
                act.wait_ge(frs_ready, n + 1)
                act.wait_ge(fnb_ready, n + 1)
                wait(act, fin_out[i], 16 * turn)
                for c in range(NC):
                    act.activation(fout[i][:, c, :], fin[i][:, c, :], ACT.Identity,
                                   bias=fnb[i][:, c:c + 1],
                                   scale=frs[i][:, c:c + 1]).then_inc(fout_ready, 1)
                act.wait_ge(fout_ready, NC * (n + 1))
                act.dma_start(out_seq[n], fout[i]).then_inc(fin_out[i], 16)

            for i in range(FIN):
                finish(0, i)
            with act.Fori(1, SEQS // FIN) as turn:
                for i in range(FIN):
                    finish(turn, i)

        @block.vector
        def _(dve):
            def chain(s, base):
                count = [base]

                def link(ins, apart=False):
                    count[0] = count[0] + 1
                    ins.then_inc(s, 1)
                    if apart:
                        wait_apart(dve, s, count[0])
                    else:
                        dve.wait_ge(s, count[0])
                return link

            link = chain(const_step, 1)
            dve.memset(w_dt[:, :], 0.0).then_inc(padding_zero, 1)
            dve.memset(w_gate[:, :], 0.0).then_inc(padding_zero, 1)
            dve.memset(a[0][:, :], 0.0).then_inc(const_ready, 1)
            dve.memset(a[1][:, :], 0.0).then_inc(const_ready, 1)
            dve.memset(ones[:, :], 1.0).then_inc(const_ready, 1)
            dve.memset(ones_b[:, :], 1.0).then_inc(const_ready, 1)
            dve.memset(neg_half[:, :], -0.5).then_inc(const_ready, 1)
            dve.wait_ge(w_in, 16 * W_LOADS)
            dve.wait_ge(const_step, 1)
            link(dve.tensor_scalar(neg_a[:, :], neg_a[:, :], -1.0, None, ALU.mult))
            for k in range(CC):
                ins = dve.tensor_scalar(w_out[:, k, :], w_out[:, k, :], norm_w[:, k:k + 1], None, ALU.mult)
            link(ins)
            def tap(q, k, j):
                done = (TAPS - 2) * (XC * q.n + k)
                if j == 1:
                    dve.wait_ge(tap0_done, XC * q.n + k + 1)
                else:
                    dve.wait_ge(tap_done, done + j - 1)
                ins = dve.scalar_tensor_tensor(
                    out=acc[:, k, j:TOKS], in0=pj[k % 2][:, 0:TOKS - j],
                    scalar=conv_w[:, k, TAPS - 1 - j:TAPS - j], in1=acc[:, k, j:TOKS],
                    op0=ALU.mult, op1=ALU.add)
                if j < TAPS - 1:
                    ins.then_inc(tap_done, 1)
                else:
                    ins.then_inc(conv_done, 1)

            def softplus_step(q, k):
                w, wsq, pp, t1, mx = (b[:, :] for b in sp)
                if k == 0:
                    dve.wait_ge(ev_ready, q.n + 1)
                else:
                    dve.wait_ge(sp_step, SP_STEPS * q.n + k)
                if k == 0:
                    ins = dve.tensor_scalar(t1, ev[:, :], 2.0, None, ALU.add)
                elif k == 1:
                    ins = dve.reciprocal(t1, t1)
                elif k == 2:
                    ins = dve.tensor_tensor(w, t1, ev[:, :], ALU.mult)
                elif k == 3:
                    ins = dve.tensor_tensor(wsq, w, w, ALU.mult)
                elif k == 4:
                    ins = dve.tensor_scalar(pp, wsq, 1.0 / LOG_TERMS[0], None, ALU.mult)
                elif k < 10:
                    ins = dve.scalar_tensor_tensor(out=pp, in0=pp, scalar=1.0 / LOG_TERMS[k - 4], in1=wsq,
                                                   op0=ALU.add, op1=ALU.mult)
                elif k == 10:
                    ins = dve.scalar_tensor_tensor(out=pp, in0=pp, scalar=1.0, in1=w, op0=ALU.add,
                                                   op1=ALU.mult)
                elif k == 11:
                    ins = dve.tensor_scalar(mx, v[:, :, :].rearrange("p c h -> p (c h)"), 0.0, None, ALU.max)
                elif k == 12:
                    if not (isinstance(q.n, int) and q.n < 2):
                        dve.wait_ge(Xdt_ready, NC * (q.n - 1))
                    ins = dve.scalar_tensor_tensor(out=dtp[q.par][:, :], in0=pp, scalar=2.0, in1=mx,
                                                   op0=ALU.mult, op1=ALU.add)
                else:
                    wait(dve, lhsA_ready, NC * (q.n - 1))
                    ins = dve.tensor_tensor(tokens(a[q.par][:, 0:NC * H]), tokens(dtp[q.par][:, :]),
                                            neg_a[:, :].unsqueeze(1).broadcast_to([P, NC, H]), ALU.mult)
                ins.then_inc(sp_step if k < SP_STEPS else a_ready, 1)

            def enter(q):
                dve.wait_ge(dt_psum, q.n + 1)
                wait(dve, a_ready, q.n)
                wait(dve, abs_done, q.n)
                dve.tensor_tensor(
                    v[:, :, :], pj[1][:, 0:NC * PADN].rearrange("p (c e) -> p c e", e=PADN)[:, :, 0:H],
                    dt_bias[:, :].unsqueeze(1).broadcast_to([P, NC, H]),
                    ALU.add).then_inc(v_ready, 1)

            def mask_chunk(s, c):
                n = NC * s.n + c
                dve.wait_ge(Gm_ready, s.n + 1)
                dve.wait_ge(L_ready, n + 1)
                wait(dve, y_psum, n - 1)
                dve.tensor_tensor(M[c % 2][:, :, :], L[c % 2][:, :, :],
                                  Gm[:, c, :].unsqueeze(1).broadcast_to([P, H, P]),
                                  ALU.mult).then_inc(M_ready, 1)

            def place_rows(r):
                link = chain(pos_step, POS_STEPS * r.n + 1)
                dve.wait_ge(rank_read, r.n + 1)
                dve.wait_ge(rowB_ready, r.n + 1)
                dve.reciprocal(gsum[:, :], gsum[:, :])
                link(dve.tensor_tensor(prow[:, :, :, :], picks[:, :, :, :],
                                       rows[:, :, :].unsqueeze(2).broadcast_to([P, NC, 2, E]), ALU.mult))
                link(dve.tensor_reduce(slotf[:, :, :], prow[:, :, :, :], AX_X, ALU.add))
                for row, k in ((rowA, 0), (rowB, 1)):
                    dve.scalar_tensor_tensor(out=row[r.par][:, :, P + 1], in0=top[:, :, k], scalar=2.0,
                                             in1=gsum[:, :], op0=ALU.mult, op1=ALU.mult)
                    dve.tensor_scalar(row[r.par][:, :, P].bitcast(I32), token_id[:, :],
                                      float(TOKENS * k), None, ALU.add)
                link(dve.tensor_copy(slot[r.par][:, :, :], slotf[:, :, :]))
                dve.tensor_scalar(token_id[:, :], token_id[:, :], float(TOKS), None,
                                  ALU.add).then_inc(slot_ready, 1)

            def residual(s):
                dve.wait_ge(out_psum, s.n + 1)
                dve.wait_ge(rms_ready, s.n + 1)
                dve.wait_ge(xres_in[s.par], 16 * (s.use + 1))
                if not (isinstance(s.n, int) and s.n < 2):
                    dve.wait_ge(scattered[s.par][0], 16 * NC * s.use)
                for c in range(NC):
                    dve.scalar_tensor_tensor(
                        out=rowA[s.par][:, c, 0:P], in0=p5[:, c * P:(c + 1) * P],
                        scalar=rms[:, c:c + 1], in1=xres[s.par][:, c, :],
                        op0=ALU.mult, op1=ALU.add).then_inc(x1_ready, 1)
                dve.wait_ge(x1_ready, NC * (s.n + 1))
                wait(dve, u_ready, NC * s.n)
                for k in range(NC):
                    ins = dve.bn_stats(st[:, k, :], rowA[s.par][:, k, 0:P])
                ins.then_inc(ln_step, 1)
                wait_apart(dve, ln_step, LN_STEPS * s.n + 1)
                for k in range(NC):
                    ins = dve.bn_aggr(mv[:, k, :], st[:, k, :])
                ins.then_inc(ln_step, 1)
                dve.wait_ge(ln_step, LN_STEPS * s.n + 2)
                dve.tensor_scalar(ve[:, :], mv[:, :, 1], EPS, None, ALU.add).then_inc(ve_ready, 1)

            def slot_dve(s, scan, project, route):
                q, r = s.plus(1), s.plus(-1)
                if project and not scan:
                    enter(q)
                if scan:
                    dve.wait_ge(G_psum, s.n + 1)
                    dve.tensor_tensor(Gm[:, :, :], p7[:, :].rearrange("p (c k) -> p c k", c=NC),
                                      upto[:, :].unsqueeze(1).broadcast_to([P, NC, P]),
                                      ALU.mult).then_inc(Gm_ready, 1)
                if scan:
                    mask_chunk(s, 0)
                if project and not scan:
                    for k in range(SP_STEPS + 1):
                        softplus_step(q, k)
                for c in range(NC):
                    n = NC * s.n + c

                    def spread(k):
                        if scan and project and 3 <= 7 * (c - 1) + k + 3 <= SP_STEPS:
                            softplus_step(q, 7 * (c - 1) + k + 3)

                    if project and c > 0:
                        tap(q, c - 1, 1)
                        spread(0)
                    if scan:
                        dve.wait_ge(tr_psum, n + 1)
                        if c + 1 < NC:
                            dve.wait_ge(Btok_ready, (NC - 1) * s.n + c + 1)
                        wait(dve, Xdd_ready, (NC - 1) * s.n + max(c - 1, 0))
                        dve.tensor_tensor(heads(Xdt[c % 2][:, :]), heads(p5[:, 0:DI]),
                                          per_head(dtp[s.par], c), ALU.mult).then_inc(Xdt_ready, 1)
                    if route and c == 0:
                        dve.wait_ge(rstd_ready, r.n + 1)
                        dve.scalar_tensor_tensor(out=shift[:, :], in0=mv[:, :, 0], scalar=-1.0,
                                                 in1=rstd[:, :], op0=ALU.mult,
                                                 op1=ALU.mult).then_inc(shift_ready, 1)
                    spread(1)
                    if scan and c > 0:
                        dve.wait_ge(off_psum, (NC - 1) * s.n + c)
                        dve.tensor_tensor(heads(carried[:, :]), heads(p6[:, 0:DI]),
                                          per_head(decays[s.par][:, 0, :], c),
                                          ALU.mult).then_inc(carried_ready, 1)
                    spread(2)
                    if scan and c + 1 < NC:
                        mask_chunk(s, c + 1)
                    spread(3)
                    if scan and project and c == 0:
                        softplus_step(q, 0)
                    if project and c > 0:
                        tap(q, c - 1, 2)
                    spread(4)
                    if project and c > 0:
                        tap(q, c - 1, 3)
                    if scan and project and c == 0:
                        softplus_step(q, 1)
                    spread(5)
                    if scan:
                        dve.wait_ge(y_psum, n + 1)
                        dve.wait_ge(xD_ready, CC * (s.n + 1))
                        wait(dve, sq_done, n - 1)
                        wait(dve, g_ready, n - 1)
                        dve.tensor_tensor(yv[c % 2][:, :, :], p7[:, 0:DI].rearrange("p (k d) -> p k d", k=CC),
                                          xD[s.par][:, :, c * P:(c + 1) * P], ALU.add).then_inc(yv_ready, 1)
                    if c == 0 and not (isinstance(s.n, int) and s.n < 2):
                        place_rows(s.plus(-2))
                    if scan and c + 1 < NC:
                        dve.wait_ge(state_psum, (NC - 1) * s.n + c + 1)
                        if c == 0:
                            dve.tensor_copy(state[0][:, :], p6[:, DI:2 * DI]).then_inc(state_ready, 1)
                        else:
                            dve.wait_ge(decayed_ready, (NC - 2) * s.n + c)
                            dve.tensor_tensor(state[c % 2][:, :], p6[:, DI:2 * DI], decayed[:, :],
                                              ALU.add).then_inc(state_ready, 1)
                    if scan and project and c == 0:
                        softplus_step(q, 2)
                    spread(6)

                gate = GATE_STEPS * (r.n if route else 0)
                if project:
                    tap(q, NC - 1, 1)
                if route:
                    dve.wait_ge(eg_ready, r.n + 1)
                    dve.tensor_scalar(eg[:, :, :], eg[:, :, :], 1.0, None, ALU.add).then_inc(gate_step, 1)
                if project:
                    tap(q, NC - 1, 2)
                if route:
                    dve.wait_ge(gate_step, gate + 1)
                    dve.reciprocal(gates[:, :, :], eg[:, :, :]).then_inc(gate_step, 1)
                if route:
                    wait_apart(dve, gate_step, gate + 2)
                    for k in range(NC):
                        ins = dve.max(top[:, k, :], gates[:, k, :])
                    ins.then_inc(gate_step, 1)
                if project:
                    tap(q, NC - 1, 3)
                if route:
                    wait_apart(dve, gate_step, gate + 3)
                    for k in range(NC):
                        ins = dve.max_index(topi[:, k, :], top[:, k, :], gates[:, k, :])
                    ins.then_inc(gate_step, 1)
                if scan:
                    dve.wait_ge(ss_psum, s.n + 1)
                    wait(dve, rms_ready, s.n)
                    dve.tensor_scalar(ms[:, :], p7[:, 0:NC * PADN].rearrange("p (c e) -> p c e", e=PADN)[:, :, 0],
                                      1.0 / DI, EPS, ALU.mult, ALU.add).then_inc(ms_ready, 1)
                if route:
                    link = chain(gate_step, gate + 4)
                    dve.wait_ge(gate_step, gate + 4)
                    link(dve.tensor_copy(topf[:, :, :], topi[:, :, 0:2]))
                    wait(dve, slot_ready, r.n)
                    link(dve.tensor_tensor(
                        picks[:, :, :, :], iota8[:, :].unsqueeze(1).unsqueeze(1).broadcast_to([P, NC, 2, E]),
                        topf[:, :, :].unsqueeze(3).broadcast_to([P, NC, 2, E]), ALU.is_equal))
                    dve.tensor_tensor(chosen[:, :, :], picks[:, :, 0, :], picks[:, :, 1, :],
                                      ALU.add).then_inc(chosen_ready, 1)
                if scan:
                    residual(s)
                if project and not is_last(s, 2):
                    enter(s.plus(2))
                if route:
                    dve.wait_ge(rank_psum, r.n + 1)
                    dve.tensor_tensor(rows[:, :, :], p4[:, 0:NC * E].rearrange("p (c e) -> p c e", e=E),
                                      next_row[:, :].unsqueeze(1).broadcast_to([P, NC, E]), ALU.add)
                    dve.tensor_tensor(gsum[:, :], top[:, :, 0], top[:, :, 1], ALU.add).then_inc(pos_step, 1)
                    dve.wait_ge(pos_step, POS_STEPS * r.n + 1)
                    dve.tensor_tensor(next_row[:, :], p4[:, NC * E:(NC + 1) * E], next_row[:, :],
                                      ALU.add).then_inc(rank_read, 1)

            slots(dve, slot_dve)
            place_rows(Seq(0, SEQS - 1))

            link = chain(table_step, 0)
            dve.wait_ge(slot_ready, SEQS)
            cnt, f, tiles, ends = tb[:, 0, :], tb[:, 1, :], tb[:, 2, :], tb[:, 3, :]
            dve.wait_ge(rank_read, SEQS)
            dve.tensor_copy(pad_at[:, :], next_row[:, :]).then_inc(pads_known, 1)
            link(dve.tensor_tensor(cnt, next_row[:, :], region[:, :], ALU.subtract))
            link(dve.tensor_scalar(f, cnt, float(P - 1), None, ALU.add))
            link(dve.tensor_copy(tbi[:, :], f))
            link(dve.tensor_scalar(tbi[:, :], tbi[:, :], P.bit_length() - 1, None, ALU.logical_shift_right))
            link(dve.tensor_copy(tiles, tbi[:, :]))
            link(dve.tensor_copy(ends, tiles))
            for e in range(1, E):
                link(dve.tensor_tensor(ends[:, e:e + 1], ends[:, e - 1:e], ends[:, e:e + 1], ALU.add))
            one = slice(0, 1)
            expert, start, base, last = (tval[:, k, :] for k in range(4))
            tiles_of = iota_tile[one, :].unsqueeze(2).broadcast_to([1, TILES, E])
            link(dve.tensor_tensor(tcmp[:, :, :], tiles_of,
                                   ends[one, :].unsqueeze(1).broadcast_to([1, TILES, E]), ALU.is_ge))
            link(dve.tensor_reduce(expert, tcmp[:, :, :], AX_X, ALU.add))
            link(dve.tensor_tensor(tcmp[:, :, :], tcmp[:, :, :],
                                   tiles[one, :].unsqueeze(1).broadcast_to([1, TILES, E]), ALU.mult))
            link(dve.tensor_reduce(start, tcmp[:, :, :], AX_X, ALU.add))
            link(dve.tensor_tensor(start, iota_tile[one, :], start, ALU.subtract))
            link(dve.tensor_scalar(base, expert, float(REGION), None, ALU.mult))
            link(dve.scalar_tensor_tensor(out=base, in0=start, scalar=float(P), in1=base,
                                          op0=ALU.mult, op1=ALU.add))
            link(dve.tensor_copy(table[:, 0, :], base))
            link(dve.tensor_scalar(last, expert, float(E - 1), None, ALU.min))
            dve.tensor_copy(table[:, 1, :], last).then_inc(table_ready, 1)

            dve.wait_ge(table_ready, 1)
            dve.wait_ge(moe_w_in, 16 * MOE_W_LOADS)

            def expert_of(j):
                return dve.value_load(table[0:1, 1, bass.ds(j, 1)], min_val=0, max_val=E - 1)

            def fetch_rows(j, k):
                wait(dve, h_psum, j - 1)
                dve.wait_ge(sT_psum, j + 1)
                dve.tensor_copy(sT[k % 2][:, :], pj[k % 2][:, 0:P])

            def fetch_weights(j, k, e):
                dve.tensor_copy(w1e[k % 2], w1[:, bass.ds(e, 1), :].rearrange("p e f -> p (e f)")).then_inc(w1e_ready, 1)
                dve.tensor_copy(b2e[k % 4], b2[:, bass.ds(e, 1), :].rearrange("p e d -> p (e d)")).then_inc(b2e_ready, 1)

            def weigh(j, k, turn, first):
                dve.wait_ge(ye_psum, j + 1)
                dve.wait_ge(b2e_ready, j + 1)
                if not first:
                    dve.wait_ge(rows_out[(k - 4) % RING], 16 * (turn + (1 if k >= 4 else 0)))
                dve.tensor_tensor(ye[k % 4], (p6, p7)[k % 2][:, 0:P], b2e[k % 4],
                                  ALU.add).then_inc(biased, 1)
                dve.wait_ge(biased, j + 1)
                dve.scalar_tensor_tensor(out=ye[k % 4], in0=ye[k % 4], scalar=xs[k][:, P + 1:P + 2],
                                         in1=xs[k][:, 0:P], op0=ALU.mult, op1=ALU.add).then_inc(ye_ready, 1)

            for k in range(2):
                e = expert_of(k)
                fetch_rows(k, k)
                fetch_weights(k, k, e)

            def turn_dve(i, first, last):
                for k in range(RING):
                    if not (last and k + 2 >= RING):
                        e = expert_of(RING * i + k + 2)
                        fetch_rows(RING * i + k + 2, k + 2)
                        fetch_weights(RING * i + k + 2, k + 2, e)
                    weigh(RING * i + k, k, i, first and k < 4)

            turn_dve(0, True, False)
            with dve.Fori(0, (TILES // RING - 3) // 2) as i:
                turn_dve(2 * i + 1, False, False)
                turn_dve(2 * i + 2, False, False)
            turn_dve(TILES // RING - 2, False, False)
            turn_dve(TILES // RING - 1, False, True)

            def add_rows(turn, i):
                n = FIN * turn + i
                dve.wait_ge(yy_in[i], 32 * (turn + 1))
                wait(dve, fout_ready, NC * (n - FIN + 1))
                dve.tensor_tensor(fin[i][:, ON_POOL:NC], yy[i][:, 0, ON_POOL:NC], yy[i][:, 1, ON_POOL:NC],
                                  ALU.add).then_inc(fin_step, 1)

            def minus_mean(turn, i):
                dve.wait_ge(frs_ready, FIN * turn + i + 1)
                dve.scalar_tensor_tensor(out=fnb[i][:, :], in0=fmv[i][:, :, 0], scalar=-1.0,
                                         in1=frs[i][:, :], op0=ALU.mult,
                                         op1=ALU.mult).then_inc(fnb_ready, 1)

            def finish(turn, i, first=False, last=False):
                n = FIN * turn + i
                dve.wait_ge(fin_step, FIN_STEPS * n + 1)
                dve.wait_ge(moe_sum, n + 1)
                for c in range(NC):
                    ins = dve.bn_stats(fst[i][:, c, :], fin[i][:, c, :])
                ins.then_inc(fin_step, 1)
                if i > 0:
                    minus_mean(turn, i - 1)
                elif not first:
                    minus_mean(turn - 1, FIN - 1)
                wait_apart(dve, fin_step, FIN_STEPS * n + 2)
                for c in range(NC):
                    ins = dve.bn_aggr(fmv[i][:, c, :], fst[i][:, c, :])
                ins.then_inc(fin_step, 1)
                if not last:
                    add_rows(turn + (i + 1) // FIN, (i + 1) % FIN)
                dve.wait_ge(fin_step, FIN_STEPS * n + 3)
                dve.tensor_scalar(fve[i][:, :], fmv[i][:, :, 1], 4 * EPS, None, ALU.add).then_inc(fve_ready, 1)

            add_rows(0, 0)
            for i in range(FIN):
                finish(0, i, first=(i == 0))
            with dve.Fori(1, SEQS // FIN - 1) as turn:
                for i in range(FIN):
                    finish(turn, i)
            for i in range(FIN):
                finish(SEQS // FIN - 1, i, last=(i == FIN - 1))
            minus_mean(SEQS // FIN - 1, FIN - 1)

        @block.gpsimd
        def _(pool):
            NCONST = [0]

            def step(ins):
                NCONST[0] += 1
                ins.then_inc(pool_const, 1)
                pool.wait_ge(pool_const, NCONST[0])

            step(pool.memset(ident[:, :], 0.0))
            step(pool.affine_select(out=ident[:, :], in_=ident[:, :], compare_op=ALU.not_equal, fill=1.0,
                                    base=0, pattern=[[-1, P]], channel_multiplier=1))
            step(pool.memset(upto[:, :], 0.0))
            step(pool.affine_select(out=upto[:, :], in_=upto[:, :], compare_op=ALU.is_gt, fill=1.0,
                                    base=0, pattern=[[-1, P]], channel_multiplier=1))
            step(pool.memset(after[:, :], 0.0))
            step(pool.affine_select(out=after[:, :], in_=after[:, :], compare_op=ALU.is_ge, fill=1.0,
                                    base=0, pattern=[[1, P]], channel_multiplier=-1))
            step(pool.memset(before_b[:, :], 0.0))
            step(pool.affine_select(out=before_b[:, :], in_=before_b[:, :], compare_op=ALU.is_ge, fill=1.0,
                                    base=0, pattern=[[-1, P]], channel_multiplier=1))
            step(pool.iota(iota8[:, :], pattern=[[1, E]], base=0, channel_multiplier=0,
                           allow_small_or_imprecise_dtypes=True))
            step(pool.iota(iota_tile[:, :], pattern=[[1, TILES]], base=0, channel_multiplier=0,
                           allow_small_or_imprecise_dtypes=True))
            step(pool.iota(token_id[:, :], pattern=[[P, NC]], base=0, channel_multiplier=1,
                           allow_small_or_imprecise_dtypes=True))
            step(pool.iota(region[:, :], pattern=[[REGION, E]], base=0, channel_multiplier=0,
                           allow_small_or_imprecise_dtypes=True))
            step(pool.iota(next_row[:, :], pattern=[[REGION, E]], base=0, channel_multiplier=0,
                           allow_small_or_imprecise_dtypes=True))
            step(pool.memset(pad_tile[:, :], 0.0))
            pool.iota(pad_tile[:, P:P + 1].bitcast(I32), pattern=[[0, 1]], base=2 * TOKENS,
                      channel_multiplier=1).then_inc(const_ready, 1)

            def expand(n, c, par):
                wait(pool, diff_psum, n - 1)
                pool.tensor_tensor(lhsA[c % 2][:, :, :], after[:, :].unsqueeze(1).broadcast_to([P, H, P]),
                                   a[par][:, (c % NC) * H:(c % NC + 1) * H].unsqueeze(2).broadcast_to([P, H, P]),
                                   ALU.mult).then_inc(lhsA_ready, 1)

            def gate_y(s, c):
                n = NC * s.n + c
                pool.wait_ge(yv_ready, n + 1)
                pool.wait_ge(sz_ready, CC * (s.n + 1))
                wait(pool, out_psum, s.n)
                pool.tensor_tensor(gt[:, :, c * P:(c + 1) * P], yv[c % 2][:, :, :],
                                   sz[s.par][:, :, c * P:(c + 1) * P], ALU.mult).then_inc(g_ready, 1)

            def scatter(q, c, k):
                if (c, k) == (0, 0):
                    wait_apart(pool, slot_ready, q.n + 1)
                pool.indirect_dma_start(
                    out=sorted_rows[:, :],
                    out_offset=bass.IndirectOffsetOnAxis(slot[q.par][:, c, k:k + 1], 0),
                    in_=(rowA, rowB)[k][q.par][:, c, :], in_offset=None).then_inc(scattered[q.par][k], 16)

            def slot_pool(s, scan, project, route):
                q, r = s.plus(1), s.plus(-1)
                scatters = not (isinstance(s.n, int) and s.n < 2)
                if scan:
                    expand(NC * s.n + 2, 2, s.par)
                for c in range(NC):
                    n = NC * s.n + c
                    if route and c == 0:
                        pool.wait_ge(ve_ready, r.n + 1)
                        pool.tensor_tensor(rstd[:, :], ve[:, :], neg_half[:, :], ALU.pow).then_inc(rstd_ready, 1)
                    if scan and 0 < c < NC - 1:
                        pool.wait_ge(state_ready, (NC - 1) * s.n + c)
                        pool.tensor_tensor(heads(decayed[:, :]), heads(state[(c - 1) % 2][:, :]),
                                           per_head(decays[s.par][:, 2, :], c), ALU.mult).then_inc(decayed_ready, 1)
                    if scan and c + 1 < NC:
                        pool.wait_ge(Xdt_ready, n + 1)
                        wait(pool, state_psum, (NC - 1) * s.n + c - 1)
                        pool.tensor_tensor(heads(Xdd[c % 2][:, :]), heads(Xdt[c % 2][:, :]),
                                           per_head(decays[s.par][:, 1, :], c), ALU.mult).then_inc(Xdd_ready, 1)
                    if c > 0 and scan and (c + 2 < NC or project):
                        if c + 2 >= NC:
                            pool.wait_ge(a_ready, q.n + 1)
                        expand(n + 2, c + 2, s.par if c + 2 < NC else q.par)
                    if scan and c > 0:
                        gate_y(s, c - 1)
                    if scatters:
                        scatter(s.plus(-2), c, 0)
                if project and not scan:
                    pool.wait_ge(a_ready, 1)
                    expand(0, 0, 0)
                    expand(1, 1, 0)
                if scan:
                    gate_y(s, NC - 1)
                    pool.wait_ge(ms_ready, s.n + 1)
                    if not (isinstance(s.n, int) and s.n < 1):
                        pool.wait_ge(x1_ready, NC * s.n)
                    pool.tensor_tensor(rms[:, :], ms[:, :], neg_half[:, :], ALU.pow).then_inc(rms_ready, 1)
                if scatters:
                    for c in range(NC):
                        scatter(s.plus(-2), c, 1)

            slots(pool, slot_pool)
            for k in range(2):
                for c in range(NC):
                    scatter(Seq(0, SEQS - 1), c, k)

            def store(j, k):
                wait_apart(pool, ye_ready, j + 1)
                pool.indirect_dma_start(
                    out=moe_rows[:, :], out_offset=bass.IndirectOffsetOnAxis(xs[k][:, P:P + 1].bitcast(I32), 0),
                    in_=ye[k % 4], in_offset=None, bounds_check=2 * TOKENS - 1,
                    oob_is_err=False).then_inc(rows_out[k], 16)

            with pool.Fori(0, TILES // RING) as i:
                for k in range(RING):
                    store(RING * i + k, k)

            def add_experts(turn, i):
                n = FIN * turn + i
                pool.wait_ge(yy_in[i], 32 * (turn + 1))
                wait(pool, fout_ready, NC * (n - FIN + 1))
                pool.tensor_tensor(fin[i][:, 0:ON_POOL], yy[i][:, 0, 0:ON_POOL], yy[i][:, 1, 0:ON_POOL],
                                   ALU.add).then_inc(moe_sum, 1)

            def root(turn, i):
                n = FIN * turn + i
                pool.wait_ge(fve_ready, n + 1)
                pool.tensor_tensor(frs[i][:, :], fve[i][:, :], neg_half[:, :], ALU.pow).then_inc(frs_ready, 1)

            add_experts(0, 0)
            for i in range(1, FIN):
                add_experts(0, i)
                root(0, i - 1)
            with pool.Fori(1, SEQS // FIN) as turn:
                add_experts(turn, 0)
                root(turn - 1, FIN - 1)
                for i in range(1, FIN):
                    add_experts(turn, i)
                    root(turn, i - 1)
            root(SEQS // FIN - 1, FIN - 1)


def kernel(L0_attn_x, L0_attn_Win, L0_attn_conv_w, L0_attn_conv_b, L0_attn_dt_bias, L0_attn_A_log,
           L0_attn_D, L0_attn_norm_w, L0_attn_Wout, L0_ffn_centroids, L0_ffn_W1, L0_ffn_b1, L0_ffn_W2,
           L0_ffn_b2):
    import numpy as np
    import concourse.bacc as bacc
    from concourse.bass_utils import run_bass_kernel_spmd

    def arr(x):
        return np.ascontiguousarray(x)

    win = np.asarray(L0_attn_Win).T
    arrays = dict(
        x=arr(L0_attn_x),
        w_z=arr(win[:, 0:DI]),
        w_xbc=arr(win[:, DI:DI + XC * P]),
        w_dt=arr(win[:, DI + XC * P:]),
        w_gate=arr(np.asarray(L0_ffn_centroids).T),
        w_out=arr(np.asarray(L0_attn_Wout).T.reshape(CC, P, P).transpose(1, 0, 2)),
        conv_w=arr(np.asarray(L0_attn_conv_w).reshape(XC, P, TAPS).transpose(1, 0, 2)),
        conv_b=arr(np.asarray(L0_attn_conv_b).reshape(XC, P).T),
        skip=arr(np.repeat(np.asarray(L0_attn_D), HD).reshape(CC, P).T),
        norm_w=arr(np.asarray(L0_attn_norm_w).reshape(CC, P).T),
        dt_bias=arr(np.broadcast_to(np.asarray(L0_attn_dt_bias), (P, H))),
        A_log=arr(np.broadcast_to(np.asarray(L0_attn_A_log), (P, H))),
        w1=arr(np.asarray(L0_ffn_W1).transpose(1, 0, 2)),
        b1=arr(np.asarray(L0_ffn_b1).reshape(E * FB, P).T),
        w2=arr(np.asarray(L0_ffn_W2).reshape(E, FB, P, P).transpose(2, 0, 1, 3)),
        b2=arr(np.broadcast_to(np.asarray(L0_ffn_b2), (P, E, P))),
    )
    nc = bacc.Bacc("TRN2", target_bir_lowering=False, num_devices=1)
    t = {n: nc.dram_tensor(f"in_{n}", a.shape, mybir.dt.from_np(a.dtype), kind="ExternalInput").ap()
         for n, a in arrays.items()}
    out = nc.dram_tensor("out_0", [SEQS, TOKS, P], F32, kind="ExternalOutput").ap()
    build(nc, t, out)
    got = run_bass_kernel_spmd(nc, [{f"in_{n}": a for n, a in arrays.items()}], core_ids=[0])
    return got.results[0]["out_0"]
```
